# Optimizing a Trainium2 kernel written in Bass

```python
import numpy as np
import jax
import jax.numpy as jnp

def _softmax(x, axis=-1):
    return jax.nn.softmax(x, axis=axis)

def _gelu(x):
    return jax.nn.gelu(x, approximate=True)

def _silu(x):
    return jax.nn.silu(x)

def _sigmoid(x):
    return jax.nn.sigmoid(x)

def _layernorm(x, axis=-1, eps=1e-05):
    m = jnp.mean(x, axis=axis, keepdims=True)
    v = jnp.var(x, axis=axis, keepdims=True)
    return (x - m) / jnp.sqrt(v + eps)

def _scatter_add(tgt, idx, src, axis=0):
    return tgt.at[idx].add(src)

def _segment_sum(src, seg, n):
    return jax.ops.segment_sum(src, seg, n)
kernel_name = 'mk_decoder_preln_d1_seqx_r8_20c5a9'

def setup_inputs(seed: int=0):
    np.random.seed(seed)
    _w = jnp.asarray

    def _rec_inputs():
        import jax
        import jax.numpy as jnp
        _rk = jax.random.key(seed)
        x = -0.0002928 + 1 * jax.random.normal(jax.random.fold_in(_rk, 1), (8, 128, 128), jnp.float32)
        _lenS = 128 - jax.random.randint(jax.random.fold_in(_rk, 7), (8,), 0, max(1, 128 // 4) + 1, jnp.int32)
        _lenS2 = 128 - jax.random.randint(jax.random.fold_in(_rk, 8), (8,), 0, max(1, 128 // 4) + 1, jnp.int32)
        _ctx_1024P = jax.random.normal(jax.random.fold_in(_rk, 11), (8, 16, 128), jnp.float32)
        _ctx_1024c = jax.random.dirichlet(jax.random.fold_in(_rk, 511), 0.3 * jnp.ones((16,), jnp.float32), (8, 128))
        _ctx_1024t = jnp.einsum('bsk,bkd->bsd', _ctx_1024c, _ctx_1024P)
        _ctx_1024t = _ctx_1024t * jax.lax.rsqrt(jnp.mean(jnp.square(_ctx_1024t)) + 1e-12) * 0.953939
        ctx_1024 = -1.39393e-06 + 0.999914 * (_ctx_1024t + 0.3 * jax.random.normal(jax.random.fold_in(_rk, 611), (8, 128, 128), jnp.float32))
        return (x, ctx_1024)
    x, ctx_1024 = _rec_inputs()

    def _L0_attn_setup():
        import jax, jax.numpy as jnp
        import numpy as np
        NUM_HEADS = 16
        EPS = 1e-08

        def _hyperbolic_attention(q, k, v, c, beta, causal=True):
            qn = jnp.sum(q * q, axis=-1)
            kn = jnp.sum(k * k, axis=-1)
            qk = jnp.einsum('bhnd,bhmd->bhnm', q, k)
            diff_sq = jnp.maximum(qn[..., :, None] - 2.0 * qk + kn[..., None, :], 0.0)
            ed = jnp.sqrt(diff_sq + EPS)
            ns = qn[..., :, None] + kn[..., None, :]
            dist_taylor = ed * (1.0 + c * ns * 0.5 + c * c * ns * ns * 0.125)
            dist_asymp = 0.693 + jnp.log(ed + EPS) + c * ns * 0.25
            dist_standard = ed * jnp.sqrt(1.0 + c * ns)
            dist = jnp.where(ed < 0.1, dist_taylor, jnp.where(ed > 2.0, dist_asymp, dist_standard))
            scores = -beta * dist
            if causal:
                N = q.shape[2]
                cm = jnp.tril(jnp.ones((N, N), dtype=bool))
                scores = jnp.where(cm, scores, -jnp.inf)
            attn = jax.nn.softmax(scores, axis=-1)
            return jnp.einsum('bhnm,bhmd->bhnd', attn, v)
        key = jax.random.key(seed)
        ks = jax.random.split(key, 5)
        B, N, D = (2, 256, 128)
        s = 1.0 / np.sqrt(D)
        return {'x': jax.random.normal(ks[0], (B, N, D), jnp.float32), 'Wq': jax.random.normal(ks[1], (D, D), jnp.float32) * s, 'Wk': jax.random.normal(ks[2], (D, D), jnp.float32) * s, 'Wv': jax.random.normal(ks[3], (D, D), jnp.float32) * s, 'Wo': jax.random.normal(ks[4], (D, D), jnp.float32) * s, 'log_c': jnp.zeros((), jnp.float32), 'log_beta': jnp.zeros((), jnp.float32)}
    _L0_attn_all = _L0_attn_setup()
    _L0_attn_in = {k: v for k, v in _L0_attn_all.items() if k in ('Wq', 'Wk', 'Wv', 'Wo', 'log_c', 'log_beta')}
    del _L0_attn_all

    def _L0_xattn_setup():
        import jax, jax.numpy as jnp
        import numpy as np
        B, S, H, NH = (2, 256, 128, 4)
        DH = H // NH
        EPS_BACKEND = 1e-06
        EPS_LN = 1e-06

        def _mlstm_parallel_stabilized(q, k, v, igate_preact, fgate_preact):
            b, nh, s, dh = q.shape
            log_fg = jax.nn.log_sigmoid(fgate_preact)
            cs = jnp.concatenate([jnp.zeros((b, nh, 1), q.dtype), jnp.cumsum(log_fg[..., 0], axis=2)], axis=2)
            fg_matrix = cs[:, :, :, None] - cs[:, :, None, :]
            fg_matrix = fg_matrix[:, :, 1:, 1:]
            causal = jnp.tril(jnp.ones((s, s), dtype=bool))
            log_fg_matrix = jnp.where(causal, fg_matrix, -jnp.inf)
            log_D = log_fg_matrix + jnp.swapaxes(igate_preact, -2, -1)
            max_log_D = jnp.max(log_D, axis=-1, keepdims=True)
            D = jnp.exp(log_D - max_log_D)
            qk = jnp.einsum('bhsd,bhtd->bhst', q, k) / jnp.sqrt(jnp.asarray(dh, q.dtype))
            C = qk * D
            normalizer = jnp.maximum(jnp.abs(jnp.sum(C, axis=-1, keepdims=True)), jnp.exp(-max_log_D))
            C_norm = C / (normalizer + EPS_BACKEND)
            return jnp.einsum('bhst,bhtd->bhsd', C_norm, v)

        def _multihead_layernorm(x, scale):
            mean = jnp.mean(x, axis=-1, keepdims=True)
            var = jnp.var(x, axis=-1, keepdims=True)
            xn = (x - mean) * jax.lax.rsqrt(var + EPS_LN)
            return xn * scale.reshape(NH, 1, DH)
        key = jax.random.key(seed)
        kq, kk, kv, kib = jax.random.split(key, 4)
        q = jax.random.normal(kq, (B, S, H), dtype=jnp.float32)
        k = jax.random.normal(kk, (B, S, H), dtype=jnp.float32)
        v = jax.random.normal(kv, (B, S, H), dtype=jnp.float32)
        igate_kernel = jnp.zeros((3 * H, NH), dtype=jnp.float32)
        igate_bias = 0.1 * jax.random.normal(kib, (NH,), dtype=jnp.float32)
        fgate_kernel = jnp.zeros((3 * H, NH), dtype=jnp.float32)
        fgate_bias = jnp.linspace(3.0, 6.0, NH, dtype=jnp.float32)
        outnorm_scale = jnp.ones((H,), dtype=jnp.float32)
        return {'q': q, 'k': k, 'v': v, 'igate_kernel': igate_kernel, 'igate_bias': igate_bias, 'fgate_kernel': fgate_kernel, 'fgate_bias': fgate_bias, 'outnorm_scale': outnorm_scale}
    _L0_xattn_all = _L0_xattn_setup()
    _L0_xattn_in = {k: v for k, v in _L0_xattn_all.items() if k in ('igate_kernel', 'igate_bias', 'fgate_kernel', 'fgate_bias', 'outnorm_scale')}
    del _L0_xattn_all

    def _L0_ffn_setup():
        import jax, jax.numpy as jnp
        import numpy as np
        D_MODEL, D_FF, N_EXPERTS, TOP_K = (128, 256, 8, 2)
        B, S = (2, 256)
        key = jax.random.key(seed)
        ks = jax.random.split(key, 6)
        sd = 1.0 / np.sqrt(D_MODEL)
        sf = 1.0 / np.sqrt(D_FF)
        return {'x': jax.random.normal(ks[0], (B, S, D_MODEL), jnp.float32), 'router_w': jax.random.normal(ks[1], (N_EXPERTS, D_MODEL), jnp.float32) * sd, 'gate_w': jax.random.normal(ks[2], (N_EXPERTS, D_MODEL, D_FF), jnp.float32) * sd, 'gate_b': jnp.zeros((N_EXPERTS, D_FF), jnp.float32), 'up_w': jax.random.normal(ks[3], (N_EXPERTS, D_MODEL, D_FF), jnp.float32) * sd, 'up_b': jnp.zeros((N_EXPERTS, D_FF), jnp.float32), 'down_w': jax.random.normal(ks[4], (N_EXPERTS, D_FF, D_MODEL), jnp.float32) * sf, 'down_b': jnp.zeros((N_EXPERTS, D_MODEL), jnp.float32)}
    _L0_ffn_all = _L0_ffn_setup()
    _L0_ffn_in = {k: v for k, v in _L0_ffn_all.items() if k in ('router_w', 'gate_w', 'gate_b', 'up_w', 'up_b', 'down_w', 'down_b')}
    del _L0_ffn_all
    return {'x': x, 'ctx_1024': ctx_1024, 'L0_attn_Wq': _L0_attn_in['Wq'], 'L0_attn_Wk': _L0_attn_in['Wk'], 'L0_attn_Wv': _L0_attn_in['Wv'], 'L0_attn_Wo': _L0_attn_in['Wo'], 'L0_attn_log_c': _L0_attn_in['log_c'], 'L0_attn_log_beta': _L0_attn_in['log_beta'], 'L0_xattn_igate_kernel': _L0_xattn_in['igate_kernel'], 'L0_xattn_igate_bias': _L0_xattn_in['igate_bias'], 'L0_xattn_fgate_kernel': _L0_xattn_in['fgate_kernel'], 'L0_xattn_fgate_bias': _L0_xattn_in['fgate_bias'], 'L0_xattn_outnorm_scale': _L0_xattn_in['outnorm_scale'], 'L0_ffn_router_w': _L0_ffn_in['router_w'], 'L0_ffn_gate_w': _L0_ffn_in['gate_w'], 'L0_ffn_gate_b': _L0_ffn_in['gate_b'], 'L0_ffn_up_w': _L0_ffn_in['up_w'], 'L0_ffn_up_b': _L0_ffn_in['up_b'], 'L0_ffn_down_w': _L0_ffn_in['down_w'], 'L0_ffn_down_b': _L0_ffn_in['down_b']}

def reference(x, ctx_1024, L0_attn_Wq, L0_attn_Wk, L0_attn_Wv, L0_attn_Wo, L0_attn_log_c, L0_attn_log_beta, L0_xattn_igate_kernel, L0_xattn_igate_bias, L0_xattn_fgate_kernel, L0_xattn_fgate_bias, L0_xattn_outnorm_scale, L0_ffn_router_w, L0_ffn_gate_w, L0_ffn_gate_b, L0_ffn_up_w, L0_ffn_up_b, L0_ffn_down_w, L0_ffn_down_b):
    import jax
    import jax.numpy as jnp

    def _L0_attn_ref(x, Wq, Wk, Wv, Wo, log_c, log_beta):
        import jax, jax.numpy as jnp
        import numpy as np
        NUM_HEADS = 16
        EPS = 1e-08

        def _hyperbolic_attention(q, k, v, c, beta, causal=True):
            qn = jnp.sum(q * q, axis=-1)
            kn = jnp.sum(k * k, axis=-1)
            qk = jnp.einsum('bhnd,bhmd->bhnm', q, k)
            diff_sq = jnp.maximum(qn[..., :, None] - 2.0 * qk + kn[..., None, :], 0.0)
            ed = jnp.sqrt(diff_sq + EPS)
            ns = qn[..., :, None] + kn[..., None, :]
            dist_taylor = ed * (1.0 + c * ns * 0.5 + c * c * ns * ns * 0.125)
            dist_asymp = 0.693 + jnp.log(ed + EPS) + c * ns * 0.25
            dist_standard = ed * jnp.sqrt(1.0 + c * ns)
            dist = jnp.where(ed < 0.1, dist_taylor, jnp.where(ed > 2.0, dist_asymp, dist_standard))
            scores = -beta * dist
            if causal:
                N = q.shape[2]
                cm = jnp.tril(jnp.ones((N, N), dtype=bool))
                scores = jnp.where(cm, scores, -jnp.inf)
            attn = jax.nn.softmax(scores, axis=-1)
            return jnp.einsum('bhnm,bhmd->bhnd', attn, v)
        B, N, D = x.shape
        H = NUM_HEADS
        Dh = D // H

        def proj(W):
            return (x @ W.T).reshape(B, N, H, Dh).transpose(0, 2, 1, 3)
        q, k, v = (proj(Wq), proj(Wk), proj(Wv))
        c = jax.nn.softplus(log_c)
        beta = jax.nn.softplus(log_beta) + 0.5
        o = _hyperbolic_attention(q, k, v, c, beta, causal=True)
        o = o.transpose(0, 2, 1, 3).reshape(B, N, D)
        return o @ Wo.T

    def _L0_xattn_ref(q, k, v, igate_kernel, igate_bias, fgate_kernel, fgate_bias, outnorm_scale):
        import jax, jax.numpy as jnp
        import numpy as np
        B, S, H, NH = (2, 256, 128, 4)
        DH = H // NH
        EPS_BACKEND = 1e-06
        EPS_LN = 1e-06

        def _mlstm_parallel_stabilized(q, k, v, igate_preact, fgate_preact):
            b, nh, s, dh = q.shape
            log_fg = jax.nn.log_sigmoid(fgate_preact)
            cs = jnp.concatenate([jnp.zeros((b, nh, 1), q.dtype), jnp.cumsum(log_fg[..., 0], axis=2)], axis=2)
            fg_matrix = cs[:, :, :, None] - cs[:, :, None, :]
            fg_matrix = fg_matrix[:, :, 1:, 1:]
            causal = jnp.tril(jnp.ones((s, s), dtype=bool))
            log_fg_matrix = jnp.where(causal, fg_matrix, -jnp.inf)
            log_D = log_fg_matrix + jnp.swapaxes(igate_preact, -2, -1)
            max_log_D = jnp.max(log_D, axis=-1, keepdims=True)
            D = jnp.exp(log_D - max_log_D)
            qk = jnp.einsum('bhsd,bhtd->bhst', q, k) / jnp.sqrt(jnp.asarray(dh, q.dtype))
            C = qk * D
            normalizer = jnp.maximum(jnp.abs(jnp.sum(C, axis=-1, keepdims=True)), jnp.exp(-max_log_D))
            C_norm = C / (normalizer + EPS_BACKEND)
            return jnp.einsum('bhst,bhtd->bhsd', C_norm, v)

        def _multihead_layernorm(x, scale):
            mean = jnp.mean(x, axis=-1, keepdims=True)
            var = jnp.var(x, axis=-1, keepdims=True)
            xn = (x - mean) * jax.lax.rsqrt(var + EPS_LN)
            return xn * scale.reshape(NH, 1, DH)
        b, s, h = q.shape
        gate_in = jnp.concatenate([q, k, v], axis=-1)
        ig = gate_in @ igate_kernel + igate_bias
        fg = gate_in @ fgate_kernel + fgate_bias
        ig = jnp.transpose(ig, (0, 2, 1))[..., None]
        fg = jnp.transpose(fg, (0, 2, 1))[..., None]
        qh = jnp.transpose(q.reshape(b, s, NH, DH), (0, 2, 1, 3))
        kh = jnp.transpose(k.reshape(b, s, NH, DH), (0, 2, 1, 3))
        vh = jnp.transpose(v.reshape(b, s, NH, DH), (0, 2, 1, 3))
        hs = _mlstm_parallel_stabilized(qh, kh, vh, ig, fg)
        hn = _multihead_layernorm(hs, outnorm_scale)
        return jnp.transpose(hn, (0, 2, 1, 3)).reshape(b, s, h)

    def _L0_ffn_ref(x, router_w, gate_w, gate_b, up_w, up_b, down_w, down_b):
        import jax, jax.numpy as jnp
        import numpy as np
        D_MODEL, D_FF, N_EXPERTS, TOP_K = (128, 256, 8, 2)
        B, S = (2, 256)
        b, s, d = x.shape
        xf = x.reshape(b * s, d)
        n = xf.shape[0]
        router_logits = xf @ router_w.T
        probs = jax.nn.softmax(router_logits, axis=-1)
        topv, topi = jax.lax.top_k(probs, TOP_K)
        mask = jnp.zeros_like(probs).at[jnp.arange(n)[:, None], topi].set(1.0)
        probs = probs * mask
        probs = probs / (probs.sum(axis=-1, keepdims=True) + 1e-09)
        g = jnp.einsum('nd,edf->nef', xf, gate_w) + gate_b
        u = jnp.einsum('nd,edf->nef', xf, up_w) + up_b
        h = jax.nn.silu(g) * u
        expert_out = jnp.einsum('nef,efd->ned', h, down_w) + down_b
        y = jnp.einsum('ne,ned->nd', probs, expert_out)
        return y.reshape(b, s, d)
    x = x + _L0_attn_ref(_layernorm(x, axis=-1), L0_attn_Wq, L0_attn_Wk, L0_attn_Wv, L0_attn_Wo, L0_attn_log_c, L0_attn_log_beta)
    x = x + _L0_xattn_ref(_layernorm(x, axis=-1), ctx_1024, ctx_1024, L0_xattn_igate_kernel, L0_xattn_igate_bias, L0_xattn_fgate_kernel, L0_xattn_fgate_bias, L0_xattn_outnorm_scale)
    x = x + _L0_ffn_ref(_layernorm(x, axis=-1), L0_ffn_router_w, L0_ffn_gate_w, L0_ffn_gate_b, L0_ffn_up_w, L0_ffn_up_b, L0_ffn_down_w, L0_ffn_down_b)
    return x

_drawn_inputs = setup_inputs


def setup_inputs(seed=0):
    import zlib

    import numpy as np

    out = dict(_drawn_inputs(seed))
    spreads = {'L0_xattn_igate_kernel': (0.0, 0.1),
     'L0_xattn_fgate_kernel': (0.0, 0.1),
     'L0_xattn_outnorm_scale': (1.0, 0.2),
     'L0_ffn_gate_b': (0.0, 0.311),
     'L0_ffn_up_b': (0.0, 0.31),
     'L0_ffn_down_b': (0.0, 0.1)}
    factors = {'L0_xattn_igate_bias': 181.692}
    for name, (base, spread) in spreads.items():
        noise = np.random.default_rng([zlib.crc32(name.encode()), seed]).standard_normal(out[name].shape)
        drawn = base * np.exp(spread * noise) if base else spread * noise
        out[name] = jnp.asarray(drawn.astype(out[name].dtype))
    for name, factor in factors.items():
        out[name] = (out[name] * factor).astype(out[name].dtype)
    return out
```

```python
import numpy as np
import concourse.bass as bass
from concourse import mybir
from contextlib import ExitStack

B, S, D = 8, 128, 128
NT = B * S
H, DH = 16, 8
XH, XD = 4, 32
E, F, FC = 8, 256, 2
CB = 4
NCH = B // CB
CT = CB * S
PB = 2
NP = B // PB
PT_ = PB * S
HALF = S // 2
NU = 2 * B
UW = 768
SLOTS = 8
LN_EPS, ATT_EPS, HEAD_EPS = 1e-5, 1e-8, 1e-6
FAR = 1e30

C_ID = 0
C_BLK = 128
C_CM = 256
C_NSEL = 320
C_COL = C_NSEL + XH * S
(K_ONE, K_C, K_G1, K_G2, K_M3, K_M36, K_EPS, K_SEPS, K_R8, K_HALF, K_1, K_HEPS, K_EPSB) = range(13)
C_IOTA = C_COL + 16
C_TOT = C_IOTA + CB * E
B_ID = 0
B_SEL = 128
B_MASK = B_SEL + 6 * S
B_SLOT = B_MASK + S
B_TOT = B_SLOT + 4

LN_SHIFT = float(np.exp(2 * (0.693 - 0.25)))


def constants():
    c = np.zeros((128, C_TOT), np.float32)
    p = np.arange(128)
    d = p % DH
    c[:, C_ID:C_ID + 128] = np.eye(128)
    c[:, C_BLK:C_BLK + 128] = (p[:, None] // DH == p[None, :] // DH)
    c[:, C_CM:C_CM + HALF] = np.where(np.arange(HALF)[None, :] > (p % HALF)[:, None], FAR, 0.0)
    for h in range(XH):
        c[h, C_NSEL + h * S:C_NSEL + (h + 1) * S] = -1.0
    col = c[:, C_COL:C_COL + 16]
    col[:, K_ONE] = d < 3
    col[:, K_C] = (d >= 3) & (d < 6)
    col[:, K_G1] = -1.0 * ((d < 6) & (d % 3 >= 1))
    col[:, K_G2] = -1.0 * ((d < 6) & (d % 3 == 2))
    col[:, K_M3] = d < 3
    col[:, K_M36] = (d >= 3) & (d < 6)
    col[:, K_EPS] = LN_EPS
    col[:, K_SEPS] = LN_SHIFT * ATT_EPS
    col[:, K_R8] = 8 ** -0.5
    col[:, K_HALF] = 0.5
    col[:, K_1] = 1.0
    col[:, K_HEPS] = HEAD_EPS
    c[:, C_IOTA:] = np.tile(np.arange(E), CB)[None, :]
    b = np.zeros((128, B_TOT), np.float32)
    b[:, B_ID:B_ID + 128] = np.eye(128)
    sel = b[:, B_SEL:B_SEL + 6 * S].reshape(128, 2, 3, S)
    for part in range(3):
        for i in range(2):
            for j in range(2):
                sel[8 * part + 4 * i + j, i, j, :] = 1.0
                sel[8 * part + 4 * i + 2 + j, i, 2, j * HALF:(j + 1) * HALF] = 1.0
    b[:, B_MASK:B_MASK + S] = np.where(p[:, None] > p[None, :], -FAR, 0.0)
    b[:, B_SLOT] = d < 6
    b[:, B_SLOT + 1] = d < 3
    return c, b.astype(mybir.dt.np(mybir.dt.bfloat16))


def stack_rows():
    r = np.zeros((128, 4, PT_), np.float32)
    row = np.arange(128)
    r[(row % SLOTS == 6) & (row // SLOTS % DH >= 3) & (row // SLOTS % DH < 6)] = 1.0
    return r.astype(mybir.dt.np(mybir.dt.bfloat16))


def decoder_layer(nc, x, ctx, ctx_t, wq_t, wk_t, wv_t, wo_t, log_c, log_beta, ig_k, ig_b, fg_k, fg_b,
                  norm_scale, router_t, gate_w, gate_b, up_w, up_b, down_w, down_b,
                  const_f, const_b, stack_init, out):
    fp32, bf16, fp32r = mybir.dt.float32, mybir.dt.bfloat16, mybir.dt.float32r
    u8, u32 = mybir.dt.uint8, mybir.dt.uint32
    ALU, ACT, AX = mybir.AluOpType, mybir.ActivationFunctionType, mybir.AxisListType

    es = ExitStack()
    with es:
        def sb(name, shape, dt=fp32):
            return es.enter_context(nc.sbuf_tensor(name, shape, dt))

        def over(old, shape, dt=fp32, at=0):
            n = int(np.prod(shape[1:]))
            axes = " ".join("abcd"[:len(shape) - 1])
            flat = old[0:shape[0], at:at + n]
            flat = flat if dt == fp32 else flat.bitcast(dt)
            return flat.rearrange(f"p ({axes}) -> p {axes}", **dict(zip("abcd", shape[1:])))

        def sem(name):
            return es.enter_context(nc.semaphore(name))

        q_dram = nc.dram_tensor("q_split", [NP, 128, SLOTS, PT_], bf16, kind="Internal").ap()
        k_dram = nc.dram_tensor("k_split", [NP, 128, SLOTS, PT_], bf16, kind="Internal").ap()
        n_dram = nc.dram_tensor("n_split", [NP, 128, PT_], bf16, kind="Internal").ap()

        cf = sb("cf", [128, C_TOT])
        cb = sb("cb", [128, B_TOT], bf16)
        ident = cf[:, C_ID:C_ID + 128]
        ident_b = cb[:, B_ID:B_ID + 128]
        headblk = cf[:, C_BLK:C_BLK + 128]
        col = lambda k, p=slice(0, 128): cf[p, C_COL + k:C_COL + k + 1]
        x_sb = sb("x_sb", [128, B, D])
        x1 = x_sb
        x2 = x_sb
        wq_sb, wk_sb, wv_sb, wo_sb = (sb(n, [128, 128]) for n in ("wq_sb", "wk_sb", "wv_sb", "wo_sb"))
        par = sb("par", [128, 2])
        par_w = sb("par_w", [128, 4, 2])
        coef = sb("coef", [128, 1])
        nbeta = sb("nbeta", [128, 1])
        ctx_sb = sb("ctx_sb", [128, B, D])
        acc = ctx_sb
        ctx1 = sb("ctx1", [128, B, XH, XD + 1])
        wg_raw = sb("wg_raw", [128, 3, 36])
        wg = sb("wg", [128, 2, 36])
        gb = sb("gb", [36, 1])
        scale_row = sb("scale_row", [128, D])
        rw = sb("rw", [128, E])
        wgu = sb("wgu", [128, E, 2, F])
        gub = sb("gub", [128, 2, E * FC])
        db = sb("db", [E, D])
        bst = sb("bst", [128, 2, CB, 6])
        mv = sb("mv", [128, 2, CB, 2])
        rs = sb("rs", [128, 2, 5, CB])
        xn = sb("xn", [128, CB, D])
        xT = sb("xT", [128, NT])
        proj_mem = sb("proj_mem", [128, 8 * CT])
        qkf = over(proj_mem, [128, 2, CT])
        qk_sq = over(proj_mem, [128, 2, CT], at=2 * CT)
        wn = over(proj_mem, [128, 2, CT], at=4 * CT)
        r1 = over(proj_mem, [128, 2, CT], at=6 * CT)
        w1 = sb("w1", [128, 2, CT])
        wd = over(proj_mem, [128, E * FC, D])
        u0 = sb("u0", [128, 2, CT], bf16)
        u1 = sb("u1", [128, 2, CT], bf16)
        split_mem = sb("split_mem", [128, NCH * SLOTS * CT])
        split = [split_mem[:, n * SLOTS * CT:(n + 1) * SLOTS * CT].bitcast(bf16)
                 .rearrange("p (s n t) -> p s n t", s=2, n=SLOTS) for n in range(NCH)]
        ctxT = over(split_mem, [128, NT], at=2048)
        ksl = sb("ksl", [128, CT], bf16)
        nsl = sb("nsl", [128, NCH, CT], bf16)
        vab = sb("vab", [128, B, 2, 144])
        sq_, sk_, sn_ = ([sb(f"{n}{k}", [128, 4, PT_], bf16) for k in range(2)] for n in ("stq", "stk", "stn"))
        v_st = [sb(f"v_st{k}", [128, PB, 144]) for k in range(2)]
        dist_mem = sb("dist_mem", [128, 10 * UW])
        e2 = over(dist_mem, [128, 2, UW])
        l1 = over(dist_mem, [128, 2, UW], at=2 * UW)
        sqn = sb("sqn", [128, UW])
        wt = over(dist_mem, [128, 2, UW], at=4 * UW)
        da = over(dist_mem, [128, 2, UW], at=6 * UW)
        prod = over(dist_mem, [128, 2, UW], at=8 * UW)
        lp = sb("lp", [128, UW])
        m_ge = sb("m_ge", [128, 2, UW], u8)
        m_gt = sb("m_gt", [128, 2, UW], u8)
        dist = sb("dist", [128, 4, UW])
        nm = sb("nm", [128, 8])
        nmr = sb("nmr", [128, 2, 8])
        nmp = sb("nmp", [128, 3, 8], bf16)
        shift = sb("shift", [128, 128], bf16)
        pT = sb("pT", [128, 2, UW])
        o_sb = sb("o_sb", [128, H, DH + 1])
        o_rec = sb("o_rec", [128, H])
        o_n = sb("o_n", [128, H, DH])
        oT = sb("oT", [128, 128])
        xblk = over(split_mem, [128, CB, XH, S])
        frow = over(dist_mem, [36, 4, CT], at=NT)
        lf = over(proj_mem, [4, CT], at=4 * CT)
        cs = over(proj_mem, [4, CT], at=5 * CT)
        runmax = over(proj_mem, [4, CT], at=6 * CT)
        ones_row = sb("ones_row", [4, S])
        arow = over(proj_mem, [36, CT], at=7 * CT)
        aT = sb("aT", [128, CB, 36])
        enm = sb("enm", [128, CB, XH])
        dT = over(split_mem, [128, 2, XH, S], at=4096)
        cT = over(split_mem, [128, 2, XH, S], at=5120)
        hs = over(dist_mem, [128, CB, XH, XD + 1], at=6 * NT)
        hden = sb("hden", [128, 3, CB * XH])
        hn = over(split_mem, [128, CB * XH, XD], at=6144)
        hc = over(split_mem, [128, CB * XH, XD], at=6656)
        hq = over(split_mem, [128, CB * XH, XD], at=7168)
        hst = sb("hst", [128, 8, CB * XH])
        lg = sb("lg", [128, CB, E])
        top = sb("top", [128, CB, 8])
        topi = sb("topi", [128, CB, 8], u32)
        rt = sb("rt", [128, 5, CB, E])
        rsum = sb("rsum", [128, 4, CB])
        wts = sb("wts", [128, B, E])
        wtsT = sb("wtsT", [E, CT])
        x3T = over(dist_mem, [128, NT])
        xhi = sb("xhi", [128, NT], fp32r)
        xlo = sb("xlo", [128, NT], fp32r)
        whi = sb("whi", [128, 2, 2, F], fp32r)
        wlo = sb("wlo", [128, 2, 2, F], fp32r)
        sil = over(dist_mem, [128, 2, CT], at=3 * NT)
        hT = over(dist_mem, [128, 4, CT], at=4 * NT)

        P1 = es.enter_context(nc.psum_tensor("P1", [128, 2, 512], fp32))
        P2 = es.enter_context(nc.psum_tensor("P2", [128, 2, 512], fp32))
        P3 = es.enter_context(nc.psum_tensor("P3", [128, 2, 512], fp32))
        PO = es.enter_context(nc.psum_tensor("PO", [128, 512], fp32))
        PM = es.enter_context(nc.psum_tensor("PM", [128, 512], fp32))

        names = ("const_in wqkv_in misc_in ctx_in exp_in stack0 v0_in v1_in out_done "
                 "bn_done mv_done lnv_done r0_done nt_done xn_done tr_full xT_done "
                 "v_full nrm_full qkf_done sq_done v_done wn_done split_b split_c split_done dup_done "
                 "par_a coef_done init_done chain_a chain_d chain_p "
                 "d2_full n1_full e2_done l1_done sqn_done wt_done lp_done ds_done pT_done shift_done oT_done "
                 "ge_done da_done sel_done prod_done dist_done nm_done o_copied o_done x1_done "
                 "gt_done causal_done nmT_full t_full pv_done oT_full wo_full "
                 "g_full abs_done l1p_done a_done rT_full aT_done enm_done ex_full dT_done cT_done "
                 "hs_done hq_done hr_done "
                 "lg_full lg_done re_done rexp_done wts_done wT_full wT_done bias_full acc_done xhl_done "
                 "w_ready whi_done gu_full sil_done h_done y_full y_done qk_full par_ln o_rec_done nm0_done nm1_done nm2_done nm3_done "
                 "qk2_full hh_full hc_done hvar_done xhi_done wg_done xblk0 passed").split()
        sm = {n: sem(n) for n in names}
        x_in = [sem(f"x_in{c}") for c in range(NCH)]
        stored = [sem(f"stored{p}") for p in range(NP)]
        stack_in = [sem(f"stack_in{k}") for k in range(2)]
        block = es.enter_context(nc.Block())

        NO = {(0, 0): 0, (0, 1): 1, (1, 0): 2, (2, 0): 3, (1, 1): 4, (2, 1): 5}

        def chunk(t, c):
            return t[:, c * CB:(c + 1) * CB, :]

        class At:

            def __init__(self, i, k):
                self.i, self.k = i, k

            def __add__(self, d):
                return At(self.i, self.k + d)

            def __sub__(self, d):
                return At(self.i, self.k - d)

            def there(self):
                return self.i is not None or 0 <= self.k < NU

            def n(self, more=0):
                v = self.k + more
                if self.i is None:
                    return v if v > 0 else None
                assert v > 0, "a wait on a register stays above zero"
                return self.i * 4 + v

            def batch(self, more=0):
                v = 2 * (self.k // 4) + (self.k % 2) + more
                if self.i is None:
                    return v
                assert v > 0, "a wait on a register stays above zero"
                return self.i * 2 + v

            def ends_batch(self):
                return self.k % 4 >= 2 and self.there()

        def wait(eng, name, n):
            if n is None or (isinstance(n, int) and n <= 0):
                return
            eng.wait_ge(sm[name], n)

        def pass_waits(eng):
            eng.sem_inc(sm["passed"], 1)

        def steps(eng, step, first, last, lo, hi):
            for s in range(first, lo):
                step(At(None, s))
            with eng.Fori(0, (hi - lo + 1) // 4) as i:
                for j in range(4):
                    step(At(i, lo + j))
            for s in range(hi + 1, last + 1):
                step(At(None, s))

        def linker(eng, name):
            count = [0]

            def link(ins):
                count[0] += 1
                ins.then_inc(sm[name], 1)
                eng.wait_ge(sm[name], count[0])
            return link

        NO = {(0, 0): 0, (0, 1): 1, (1, 0): 2, (2, 0): 3, (1, 1): 4, (2, 1): 5}

        def chunk(t, c):
            return t[:, c * CB:(c + 1) * CB, :]

        def tok(t, c, b=None):
            return t[:, c * CT:(c + 1) * CT] if b is None else t[:, c * CT + b * S:c * CT + (b + 1) * S]

        def wide(t, *shape):
            return t.broadcast_to(list(shape))

        def load_stack(sp, bp, k):
            here = [t[bass.ds(bp, 1)].rearrange("a r s t -> (a r) s t")[k * 64:(k + 1) * 64]
                    .rearrange("(g q) s t -> (q s) g t", g=4) for t in (q_dram, k_dram)]
            sp.dma_start(sq_[k][:, :, :], here[0]).then_inc(stack_in[k], 16)
            sp.dma_start(sk_[k][:, :, :], here[1]).then_inc(stack_in[k], 16)
            norms = n_dram[bass.ds(bp, 1)].rearrange("a r t -> (a r) t")[k * 64:(k + 1) * 64]
            sp.dma_start(sn_[k][SLOTS - 1:128:SLOTS, :, :],
                         norms.rearrange("(g q) t -> q g t", g=4)).then_inc(stack_in[k], 16)

        def load_values(sp, bp, k):
            sp.dma_start(v_st[k][:, :, :], vab[:, bass.ds(bp * PB, PB), k, :]).then_inc(sm[f"v{k}_in"], 16)

        @block.sync
        def _(sp):
            xv = x.rearrange("b s d -> s b d")
            sp.dma_start(chunk(x_sb, 0), xv[:, 0:CB, :]).then_inc(x_in[0], 16)
            sp.dma_start(cf[:, :], const_f).then_inc(sm["const_in"], 16)
            sp.dma_start(par[:, 0:1], log_c.to_broadcast([128, 1])).then_inc(sm["const_in"], 16)
            sp.dma_start(par[:, 1:2], log_beta.to_broadcast([128, 1])).then_inc(sm["const_in"], 16)
            sp.dma_start(cb[:, :], const_b).then_inc(sm["const_in"], 16)
            sp.dma_start(wq_sb[:, :], wq_t).then_inc(sm["wqkv_in"], 16)
            sp.dma_start(wk_sb[:, :], wk_t).then_inc(sm["wqkv_in"], 16)
            sp.dma_start(wv_sb[:, :], wv_t).then_inc(sm["wqkv_in"], 16)
            sp.dma_start(chunk(x_sb, 1), xv[:, CB:B, :]).then_inc(x_in[1], 16)
            for k in range(2):
                sp.dma_start(sn_[k][:, :, :], stack_init).then_inc(sm["stack0"], 16)
            sp.dma_start(wo_sb[:, :], wo_t).then_inc(sm["misc_in"], 16)
            sp.dma_start(rw[:, :], router_t).then_inc(sm["misc_in"], 16)
            sp.dma_start(db[:, :], down_b).then_inc(sm["misc_in"], 16)
            sp.dma_start(gub[:, 0, :], gate_b).then_inc(sm["misc_in"], 16)
            sp.dma_start(gub[:, 1, :], up_b).then_inc(sm["misc_in"], 16)
            sp.dma_start(gb[0:4, :], ig_b).then_inc(sm["misc_in"], 16)
            sp.dma_start(gb[32:36, :], fg_b).then_inc(sm["misc_in"], 16)
            sp.dma_start(scale_row[:, :], norm_scale.to_broadcast([128, D])).then_inc(sm["misc_in"], 16)
            sp.wait_ge(sm["init_done"], 1)
            sp.dma_start(wg_raw[:, :, 0:4], ig_k.rearrange("(t p) h -> p t h", p=128)).then_inc(sm["misc_in"], 16)
            sp.dma_start(wg_raw[:, :, 32:36], fg_k.rearrange("(t p) h -> p t h", p=128)).then_inc(sm["misc_in"], 16)
            sp.wait_ge(sm["stack0"], 32)
            for c in range(NCH):
                sp.wait_ge(sm["split_done"], c + 1)
                sp.wait_ge(sm["dup_done"], c + 1)
                for p in range(2):
                    cols = slice(p * PT_, (p + 1) * PT_)
                    n = 2 * c + p
                    sp.dma_start(q_dram[n], split[c][:, 0, :, cols]).then_inc(stored[n], 16)
                    sp.dma_start(k_dram[n], split[c][:, 1, :, cols]).then_inc(stored[n], 16)
                    sp.dma_start(n_dram[n], nsl[:, c, cols]).then_inc(stored[n], 16)
                if c == 0:
                    sp.wait_ge(stored[0], 48)
                    sp.wait_ge(sm["v_done"], 1)
                    for k in range(2):
                        load_stack(sp, 0, k)
                        load_values(sp, 0, k)
            sp.dma_start(ctx_sb[:, :, :], ctx.rearrange("b s d -> s b d")).then_inc(sm["ctx_in"], 16)
            sp.dma_start(wgu[:, :, 0, :], gate_w.rearrange("e d f -> d e f")).then_inc(sm["exp_in"], 16)
            sp.dma_start(wgu[:, :, 1, :], up_w.rearrange("e d f -> d e f")).then_inc(sm["exp_in"], 16)
            sp.dma_start(wd[:, :, :], down_w.rearrange("e (c f) d -> f (e c) d", c=FC)).then_inc(sm["exp_in"], 16)
            for n in range(1, NP):
                sp.wait_ge(stored[n], 48)
            sp.dma_start(ctxT[:, :], ctx_t).then_inc(sm["ctx_in"], 16)
            sp.wait_ge(sm["v_done"], 2)

            def next_stack(bp, k):
                sp.wait_ge(sm["d2_full"], bp * 4 + (2 * k - 2))
                sp.wait_ge(sm["n1_full"], bp * 4 + (2 * k - 2))
                load_stack(sp, bp, k)

            def next_values(bp, k):
                sp.wait_ge(sm["pv_done"], bp * 4 + (2 * k - 2))
                load_values(sp, bp, k)

            for k in range(2):
                next_stack(1, k)
            with sp.Fori(2, NP) as bp:
                for k in range(2):
                    next_stack(bp, k)
                    next_values(bp - 1, k)
            for k in range(2):
                next_values(NP - 1, k)
            for c in range(NCH):
                sp.wait_ge(sm["y_done"], 2 * (E - 1) + c + 1)
                sp.dma_start(out.rearrange("b s d -> s b d")[:, c * CB:(c + 1) * CB, :],
                             chunk(acc, c)).then_inc(sm["out_done"], 16)
            sp.wait_ge(sm["out_done"], 16 * NCH)

        @block.gpsimd
        def _(pool):
            link = linker(pool, "chain_p")
            pool.memset(wg_raw[:, :, :], 0.0).then_inc(sm["init_done"], 1)
            link(pool.memset(vab[:, :, :, :], 0.0))
            for k in range(2):
                va = vab[:, :, k, 0:72].rearrange("p b (h n) -> p b h n", n=DH + 1)
                link(pool.memset(va[:, :, :, DH], 1.0))
                vb = vab[:, :, k, 72:144].rearrange("p b (i q n) -> p b i q n", i=4, q=2)
                link(pool.memset(vb[0:HALF, :, :, 0, DH], 1.0))
                link(pool.memset(vb[HALF:128, :, :, 1, DH], 1.0))
            pool.memset(shift[:, :], 0.0)
            pool.memset(ones_row[:, :], 1.0)
            pool.memset(ctx1[:, :, :, XD], 1.0).then_inc(sm["init_done"], 1)
            pool.wait_ge(sm["const_in"], 64)
            for c in range(NCH):
                pool.tensor_copy(split[c][:, 0, 7, :], cb[:, B_SLOT:B_SLOT + 1].to_broadcast([128, CT]))
                pool.tensor_copy(split[c][:, 1, 6, :], cb[:, B_SLOT + 1:B_SLOT + 2].to_broadcast([128, CT]))
            for c in range(NCH):
                q, k = split[c][:, 0], split[c][:, 1]
                pool.wait_ge(sm["split_c"], 2 * c + 1)
                pool.tensor_copy(q[:, 1, :], q[:, 0, :])
                pool.tensor_copy(q[:, 2, :], q[:, 0, :])
                pool.tensor_copy(q[:, 4, :], q[:, 3, :])
                pool.wait_ge(sm["split_c"], 2 * c + 2)
                pool.tensor_copy(k[:, 3, :], k[:, 0, :])
                pool.tensor_copy(k[:, 4, :], k[:, 1, :])
                pool.tensor_copy(k[:, 5, :], k[:, 0, :]).then_inc(sm["dup_done"], 1)

            def step(s):
                g = s + 1
                if g.there():
                    wait(pool, "e2_done", g.n(1))
                    wait(pool, "dist_done", g.n(-1))
                    pass_waits(pool)
                    pool.tensor_scalar(m_gt[:, g.k % 2, :], e2[:, g.k % 2, :], 4.0 - ATT_EPS, None,
                                       ALU.is_gt).then_inc(sm["gt_done"], 1)
                g = s - 1
                if g.there():
                    wait(pool, "dist_done", g.n(1))
                    for i in range(2):
                        row = dist[:, g.k % 4, i * 384:(i + 1) * 384]
                        wideq = row[:, 0:256].rearrange("p (j n) -> p j n", j=2)[:, :, HALF:128]
                        near = row[:, 256:384].rearrange("p (j n) -> p j n", j=2)
                        cm = cf[:, C_CM:C_CM + HALF].unsqueeze(1).broadcast_to([128, 2, HALF])
                        pool.tensor_tensor(wideq, wideq, cm, ALU.add)
                        last = pool.tensor_tensor(near, near, cm, ALU.add)
                    last.then_inc(sm["causal_done"], 1)

            steps(pool, step, -1, NU, 3, 14)
            for n in range(NP):
                pool.wait_ge(stored[n], 48)
            pool.memset(arow[:, :], 0.0)
            pool.memset(xblk[:, :, :, :], 0.0).then_inc(sm["xblk0"], 1)
            pool.wait_ge(sm["ctx_in"], 32)
            pool.tensor_copy(ctx1[:, :, :, 0:XD], ctx_sb[:, :, :].rearrange("p b (h d) -> p b h d", h=XH)).then_inc(sm["par_a"], 1)

            pool.wait_ge(sm["exp_in"], 48)

            def prepare(e, slot):
                w = wgu[:, bass.ds(e, 1), :, :].rearrange("p a g f -> p (a g f)")
                hi = whi[:, slot].rearrange("p g f -> p (g f)")
                lo = wlo[:, slot].rearrange("p g f -> p (g f)")
                if not isinstance(e, int):
                    pool.wait_ge(sm["gu_full"], e * 4 - 4)
                pool.tensor_copy(hi, w).then_inc(sm["whi_done"], 1)
                pool.wait_ge(sm["whi_done"], e + 1)
                pass_waits(pool)
                pool.tensor_tensor(lo, w, hi, ALU.subtract).then_inc(sm["w_ready"], 1)

            prepare(0, 0)
            prepare(1, 1)
            with pool.Fori(1, E // 2) as i:
                for j in range(2):
                    prepare(i * 2 + j, j)

        @block.scalar
        def _(act):
            link = linker(act, "chain_a")
            A = act.activation
            act.preload_act_table_set("natural_log_exp_and_others")
            act.wait_ge(sm["const_in"], 64)
            link(A(par_w[:, 0, :], par[:, :], ACT.Abs))
            link(A(par_w[:, 1, :], par_w[:, 0, :], ACT.Exp, scale=-1.0))
            A(par_w[:, 2, :], par_w[:, 1, :], ACT.Ln, bias=col(K_1)).then_inc(sm["par_ln"], 1)

            def rstd_start(n, var, eps, done, before, store):
                act.wait_ge(sm[before], n)
                link(A(store[0], var, ACT.Ln, bias=eps))
                A(store[1], store[0], ACT.Exp, scale=-0.5).then_inc(sm[done], 1)

            def norm_rstd(n):
                wait(act, "xn_done", CB * (n - 1))
                rstd_start(CB * (n + 1), mv[:, n % 2, :, 1], col(K_EPS), "r0_done", "mv_done",
                           (rs[:, n % 2, 0, :], rs[:, n % 2, 1, :]))

            def evacuate_xT(n, dst):
                act.wait_ge(sm["tr_full"], n + 1)
                A(dst, PM[:, :], ACT.Copy).then_inc(sm["xT_done"], 1)

            for c in range(NCH):
                n = NO[0, c]
                norm_rstd(n)
                evacuate_xT(n, tok(xT, c))
                wait(act, "split_b", 2 * c)
                wait(act, "nrm_full", 2 * c)
                for s in range(2):
                    act.wait_ge(sm["qk_full"], 2 * c + s + 1)
                    A(qkf[:, s, :], P1[:, s, :], ACT.Copy, scale=1.0 if s == 0 else -2.0).then_inc(sm["qkf_done"], 1)
                    A(qk_sq[:, s, :], P1[:, s, :], ACT.Square).then_inc(sm["sq_done"], 1)
                act.wait_ge(sm["v_full"], c + 1)
                act.wait_ge(sm["init_done"], 2)
                for k in range(2):
                    va = vab[:, c * CB:(c + 1) * CB, k, 0:72].rearrange("p b (h n) -> p b h n", n=DH + 1)
                    A(va[:, :, :, 0:DH], P3[:, 0, :].rearrange("p (b k h n) -> p b k h n", b=CB, k=2, h=8)[:, :, k, :, :],
                      ACT.Copy)
                    for i in range(2):
                        vb = vab[:, c * CB:(c + 1) * CB, k, 72 + 36 * i:108 + 36 * i].rearrange(
                            "p b (j q n) -> p b j q n", j=2, q=2)
                        lo = P3[0:HALF, 0, :].rearrange("p (b m q j n) -> p b m q j n", b=CB, m=4, q=2, j=2)
                        hi = P3[HALF:128, 1, 0:256].rearrange("p (b m j n) -> p b m j n", b=CB, m=4, j=2)
                        A(vb[0:HALF, :, :, 0, 0:DH], lo[:, :, 2 * k + i, 0, :, :], ACT.Copy)
                        last = A(vb[HALF:128, :, :, 1, 0:DH], hi[:, :, 2 * k + i, :, :], ACT.Copy)
                last.then_inc(sm["v_done"], 1)
                act.wait_ge(sm["coef_done"], 1)
                wait(act, "split_done", c)
                for s in range(2):
                    act.wait_ge(sm["nrm_full"], 2 * c + s + 1)
                    bias = {} if s == 0 else {"bias": col(K_C)}
                    A(wn[:, s, :], P2[:, s, :], ACT.Identity, scale=coef[:, :], **bias).then_inc(sm["wn_done"], 1)

            def step(s):
                u = s + 1
                p = u.k % 2
                ps1, ps2 = (P[:, :, 0:384] for P in (P1, P2))
                def row(t, w=None):
                    r = t[:, :] if w is None else t[:, w, :]
                    return r.rearrange("p (i n) -> p i n", i=2)
                if u.there():
                    wait(act, "d2_full", u.n(1))
                    for w in ("l1_done", "ge_done", "prod_done", "gt_done"):
                        wait(act, w, u.n(-1))
                    A(row(e2, p), ps1, ACT.Relu).then_inc(sm["e2_done"], 1)
                    wait(act, "e2_done", u.n(1))
                    wait(act, "da_done", u.n(-1))
                    A(l1[:, p, :], e2[:, p, :], ACT.Ln, scale=LN_SHIFT, bias=col(K_SEPS)).then_inc(sm["l1_done"], 1)
                t = s - 3
                if t.there():
                    wait(act, "t_full", t.n(1))
                    wait(act, "pv_done", t.n(-1))
                    A(row(pT, t.k % 2), P3[:, :, 0:384], ACT.Exp, scale=nbeta[:, :]).then_inc(sm["pT_done"], 1)
                if u.there():
                    wait(act, "n1_full", u.n(1))
                    wait(act, "wt_done", u.n())
                    A(row(sqn), ps2, ACT.Square, scale=col(K_R8), bias=col(K_R8)).then_inc(sm["sqn_done"], 1)
                    wait(act, "sqn_done", u.n(1))
                    wait(act, "prod_done", u.n(-1))
                    A(wt[:, p, :], sqn[:, :], ACT.Square, bias=col(K_HALF)).then_inc(sm["wt_done"], 1)
                t = s - 2
                if t.there():
                    wait(act, "nmT_full", t.n(1))
                    wait(act, "t_full", t.n())
                    A(shift[0:24, :], PM[0:24, 0:64].bitcast(bf16), ACT.Copy).then_inc(sm["shift_done"], 1)
                if s.there():
                    wait(act, "prod_done", s.n(1))
                    wait(act, "ds_done", s.n())
                    A(lp[:, :], prod[:, s.k % 2, :], ACT.Ln, scale=16.0).then_inc(sm["lp_done"], 1)
                    wait(act, "lp_done", s.n(1))
                    wait(act, "t_full", s.n(-3))
                    A(dist[:, s.k % 4, :], lp[:, :], ACT.Exp, scale=0.5).then_inc(sm["ds_done"], 1)
                t = s - 4
                if t.ends_batch():
                    act.wait_ge(sm["oT_full"], t.batch(1))
                    A(oT[:, :], PM[:, 0:128], ACT.Copy).then_inc(sm["oT_done"], 1)

            steps(act, step, -1, NU + 3, 5, 12)

            for c in range(NCH):
                n = NO[1, c]
                norm_rstd(n)
                if c == 0:
                    act.wait_ge(sm["xblk0"], 1)
                act.wait_ge(sm["tr_full"], n + 1)
                wait(act, "qk2_full", CB * c)
                A(tok(xT, c), PM[:, :], ACT.Copy)
                for h in range(XH):
                    r = slice(h * XD, (h + 1) * XD)
                    last = A(xblk[r, :, h, :], PM[r, :].rearrange("p (b s) -> p b s", b=CB), ACT.Copy)
                last.then_inc(sm["xT_done"], 1)
                act.wait_ge(sm["g_full"], c + 1)
                fr = slice(32, 36)
                wait(act, "a_done", c)
                A(frow[fr, 0, :], PO[fr, :], ACT.Abs, bias=gb[fr, :]).then_inc(sm["abs_done"], 1)
                act.wait_ge(sm["abs_done"], c + 1)
                link(A(frow[fr, 1, :], frow[fr, 0, :], ACT.Exp, scale=-1.0))
                A(frow[fr, 2, :], frow[fr, 1, :], ACT.Ln, bias=col(K_1, fr)).then_inc(sm["l1p_done"], 1)
                act.wait_ge(sm["rT_full"], c + 1)
                wait(act, "dT_done", CB * c)
                link(A(aT[:, :, :], PM[:, 0:144].rearrange("p (b n) -> p b n", b=CB), ACT.Copy))
                wait(act, "hs_done", CB * c)
                A(enm[:, :, :], aT[:, :, 32:36], ACT.Exp, scale=-1.0).then_inc(sm["enm_done"], 1)
                for b in range(CB):
                    m = c * CB + b
                    act.wait_ge(sm["ex_full"], m + 1)
                    wait(act, "cT_done", m - 1)
                    for h in range(XH):
                        last = A(dT[:, m % 2, h, :], P3[:, m % 2, h * S:(h + 1) * S], ACT.Exp, bias=aT[:, b, h:h + 1])
                    last.then_inc(sm["dT_done"], 1)
                act.wait_ge(sm["hc_done"], c + 1)
                A(hq[:, :, :], hc[:, :, :], ACT.Square).then_inc(sm["hq_done"], 1)
                rstd_start(c + 1, hst[:, 2, :], col(K_HEPS), "hr_done", "hvar_done", (hst[:, 3, :], hst[:, 4, :]))
                n = NO[2, c]
                norm_rstd(n)
                evacuate_xT(n, tok(x3T, c))
                act.wait_ge(sm["xT_done"], n + 1)
                A(tok(xhi, c), tok(x3T, c), ACT.Copy).then_inc(sm["xhi_done"], 1)
                act.wait_ge(sm["re_done"], c + 1)
                A(rt[:, 2, :, :], rt[:, 1, :, :], ACT.Exp).then_inc(sm["rexp_done"], 1)
                act.wait_ge(sm["wT_full"], c + 1)
                wait(act, "bias_full", c)
                A(wtsT[:, :], PM[0:E, :], ACT.Copy).then_inc(sm["wT_done"], 1)

            def expert(e, c, z):
                for f in range(FC):
                    n = e * 4 + (2 * c + f + 1)
                    act.wait_ge(sm["gu_full"], n)
                    wait(act, "h_done", n - 2 if not isinstance(n, int) or n > 2 else 0)
                    P = (P1, P2)[f]
                    pass_waits(act)
                    A(sil[:, f, :], P[:, 0, :], ACT.Silu,
                      bias=gub[:, 0, bass.ds(e * FC + f, 1)]).then_inc(sm["sil_done"], 1)

            for z in range(2):
                expert(0, z, z)
            with act.Fori(1, E) as e:
                for c in range(NCH):
                    expert(e, c, c)

        @block.vector
        def _(dve):
            link = linker(dve, "chain_d")
            V = dve
            dve.wait_ge(sm["const_in"], 64)
            link(V.tensor_scalar(par_w[:, 3, :], par[:, :], 0.0, None, ALU.max))
            dve.wait_ge(sm["par_ln"], 1)
            link(V.tensor_tensor(par_w[:, 3, :], par_w[:, 3, :], par_w[:, 2, :], ALU.add))
            V.tensor_scalar(nbeta[:, :], par_w[:, 3, 1:2], 0.5, -0.25, ALU.add, ALU.mult)
            V.scalar_tensor_tensor(coef[:, :], par_w[:, 3, 0:1], col(K_C), col(K_ONE), ALU.mult,
                                   ALU.add).then_inc(sm["coef_done"], 1)

            def refine(var, eps, r0, t, r):
                link(V.tensor_tensor(t, r0, r0, ALU.mult))
                link(V.scalar_tensor_tensor(t, var, eps, t, ALU.add, ALU.mult))
                link(V.tensor_scalar(t, t, -0.5, 1.5, ALU.mult, ALU.add))
                link(V.tensor_tensor(r, r0, t, ALU.mult))

            def layer_norm(n, src, c):
                p = n % 2
                for b in range(CB):
                    last = V.bn_stats(bst[:, p, b, :], src[:, c * CB + b, :])
                link(last)
                for b in range(CB):
                    V.bn_aggr(mv[:, p, b, :], bst[:, p, b, :]).then_inc(sm["mv_done"], 1)
                dve.wait_ge(sm["r0_done"], n + 1)
                refine(mv[:, p, :, 1], LN_EPS, rs[:, p, 1, :], rs[:, p, 2, :], rs[:, p, 4, :])
                wait(dve, "tr_full", n)
                for b in range(CB):
                    V.tensor_scalar(xn[:, b, :], src[:, c * CB + b, :], mv[:, p, b, 0:1], rs[:, p, 4, b:b + 1],
                                    ALU.subtract, ALU.mult).then_inc(sm["xn_done"], 1)

            for c in range(NCH):
                dve.wait_ge(x_in[c], 16)
                layer_norm(NO[0, c], x_sb, c)
                for s in range(2):
                    mid, low = ((3, 5), (1, 2))[s]
                    sp_ = split[c][:, s]
                    dve.wait_ge(sm["qkf_done"], 2 * c + s + 1)
                    link(V.tensor_copy(sp_[:, 0, :], qkf[:, s, :]))
                    V.tensor_tensor(r1[:, s, :], qkf[:, s, :], sp_[:, 0, :], ALU.subtract).then_inc(sm["split_b"], 1)
                    dve.wait_ge(sm["split_b"], 2 * c + s + 1)
                    V.tensor_copy(sp_[:, mid, :], r1[:, s, :]).then_inc(sm["split_c"], 1)
                    dve.wait_ge(sm["split_c"], 2 * c + s + 1)
                    V.tensor_tensor(sp_[:, low, :], r1[:, s, :], sp_[:, mid, :], ALU.subtract)
                for s in range(2):
                    dve.wait_ge(sm["wn_done"], 2 * c + s + 1)
                    link(V.tensor_copy(u0[:, s, :], wn[:, s, :]))
                    link(V.scalar_tensor_tensor(w1[:, s, :], u0[:, s, :], col(K_G1), wn[:, s, :], ALU.mult, ALU.add))
                    link(V.tensor_copy(u1[:, s, :], w1[:, s, :]))
                    dst = split[c][:, 0, 6, :] if s == 0 else ksl[:, :]
                    link(V.scalar_tensor_tensor(dst, u1[:, s, :], col(K_G2), w1[:, s, :], ALU.mult, ALU.add))
                V.tensor_scalar(split[c][:, 1, 7, :], ksl[:, :], col(K_M3), None, ALU.mult)
                V.tensor_scalar(nsl[:, c, :], ksl[:, :], col(K_M36), None, ALU.mult).then_inc(sm["split_done"], 1)

            def step(s):
                def row(t, w):
                    return t[:, w, :].rearrange("p (i n) -> p i n", i=2)
                n1 = P2[:, :, 0:384]
                if s.there():
                    p = s.k % 2
                    wait(dve, "l1_done", s.n(1))
                    wait(dve, "sqn_done", s.n(1))
                    wait(dve, "dist_done", s.n(-1))
                    V.scalar_tensor_tensor(row(da, p), row(l1, p), 2.0, n1, ALU.mult, ALU.add).then_inc(sm["da_done"], 1)
                    wait(dve, "ge_done", s.n(1))
                    wait(dve, "wt_done", s.n(1))
                    pass_waits(dve)
                    V.copy_predicated(row(wt, p), row(m_ge, p), n1).then_inc(sm["sel_done"], 1)
                    wait(dve, "sel_done", s.n(1))
                    wait(dve, "lp_done", s.n(-1))
                    V.scalar_tensor_tensor(prod[:, p, :], e2[:, p, :], ATT_EPS, wt[:, p, :], ALU.add,
                                           ALU.mult).then_inc(sm["prod_done"], 1)
                t = s - 5
                if t.ends_batch():
                    dve.wait_ge(sm["wo_full"], t.batch(1))
                    b = bass.ds(t.batch(1) - 1, 1)
                    V.tensor_tensor(x1[:, b, :].rearrange("p a d -> p (a d)"), PM[:, 0:128],
                                    x_sb[:, b, :].rearrange("p a d -> p (a d)"), ALU.add).then_inc(sm["x1_done"], 1)
                t = s - 4
                if t.ends_batch():
                    wait(dve, "pv_done", t.n(1))
                    bl = t.k % 2
                    o = PO[:, bl * 144:(bl + 1) * 144].rearrange("p (h n) -> p h n", n=DH + 1)
                    V.tensor_copy(o_sb[:, :, :], o).then_inc(sm["o_copied"], 1)
                    dve.wait_ge(sm["o_copied"], t.batch(1))
                    V.reciprocal(o_rec[:, :], o_sb[:, :, DH]).then_inc(sm["o_rec_done"], 1)
                    dve.wait_ge(sm["o_rec_done"], t.batch(1))
                    V.tensor_tensor(o_n[:, :, :], o_sb[:, :, 0:DH],
                                    o_rec[:, :].unsqueeze(2).broadcast_to([128, H, DH]), ALU.mult).then_inc(sm["o_done"], 1)
                t = s - 2
                if t.there():
                    wait(dve, "causal_done", t.n(1))
                    d = row(dist, t.k % 4)
                    m = nm[:, :].rearrange("p (i q) -> p i q", i=2)
                    V.tensor_reduce(m[:, :, 0:2], d[:, :, 0:256].rearrange("p i (j n) -> p i j n", j=2), AX.X, ALU.min,
                                    negate=True)
                    V.tensor_reduce(m[:, :, 2:4], d[:, :, 256:384].rearrange("p i (j n) -> p i j n", j=2), AX.X, ALU.min,
                                    negate=True).then_inc(sm["nm0_done"], 1)
                    wait(dve, "nm0_done", t.n(1))
                    wait(dve, "nmT_full", t.n())
                    V.tensor_copy(nmp[:, 0, :], nm[:, :]).then_inc(sm["nm1_done"], 1)
                    wait(dve, "nm1_done", t.n(1))
                    V.tensor_tensor(nmr[:, 0, :], nm[:, :], nmp[:, 0, :], ALU.subtract).then_inc(sm["nm2_done"], 1)
                    wait(dve, "nm2_done", t.n(1))
                    V.tensor_copy(nmp[:, 1, :], nmr[:, 0, :]).then_inc(sm["nm3_done"], 1)
                    wait(dve, "nm3_done", t.n(1))
                    V.tensor_tensor(nmp[:, 2, :], nmr[:, 0, :], nmp[:, 1, :], ALU.subtract).then_inc(sm["nm_done"], 1)
                t = s - 1
                if t.there():
                    wait(dve, "ds_done", t.n(1))
                    wait(dve, "gt_done", t.n(1))
                    wait(dve, "da_done", t.n(1))
                    pass_waits(dve)
                    V.copy_predicated(dist[:, t.k % 4, :], m_gt[:, t.k % 2, :], da[:, t.k % 2, :]).then_inc(sm["dist_done"], 1)
                t = s + 1
                if t.there():
                    wait(dve, "e2_done", t.n(1))
                    wait(dve, "sel_done", t.n(-1))
                    V.tensor_scalar(m_ge[:, t.k % 2, :], e2[:, t.k % 2, :], ATT_EPS, 0.01, ALU.add,
                                    ALU.is_ge).then_inc(sm["ge_done"], 1)

            steps(dve, step, -1, NU + 4, 5, 12)

            dve.wait_ge(sm["misc_in"], 160)
            link(V.tensor_copy(wg[:, 0, :], wg_raw[:, 0, :]))
            V.tensor_tensor(wg[:, 1, :], wg_raw[:, 1, :], wg_raw[:, 2, :], ALU.add).then_inc(sm["wg_done"], 1)
            dve.wait_ge(sm["x1_done"], B)
            for c in range(NCH):
                layer_norm(NO[1, c], x1, c)
                fr = slice(32, 36)
                dve.wait_ge(sm["abs_done"], c + 1)
                link(V.tensor_scalar(frow[fr, 3, :], PO[fr, :], gb[fr, :], 0.0, ALU.add, ALU.min))
                dve.wait_ge(sm["l1p_done"], c + 1)
                link(V.tensor_tensor(lf[:, :], frow[fr, 3, :], frow[fr, 2, :], ALU.subtract))
                for b in range(CB):
                    cols = slice(b * S, (b + 1) * S)
                    last = V.tensor_tensor_scan(cs[:, cols], ones_row[:, :], lf[:, cols], 0.0, ALU.mult, ALU.add)
                link(last)
                wait(dve, "rT_full", c)
                if c == 0:
                    dve.wait_ge(sm["xblk0"], 1)
                wait(dve, "ex_full", CB * c)
                link(V.scalar_tensor_tensor(arow[0:4, :], PO[0:4, :], gb[0:4, :], cs[:, :], ALU.add, ALU.subtract))
                for b in range(CB):
                    cols = slice(b * S, (b + 1) * S)
                    last = V.tensor_tensor_scan(runmax[:, cols], arow[0:4, cols], arow[0:4, cols], -3e38, ALU.max, ALU.max)
                link(last)
                V.tensor_tensor(arow[32:36, :], cs[:, :], runmax[:, :], ALU.add).then_inc(sm["a_done"], 1)
                for b in range(CB + 1):
                    m = c * CB + b
                    if b < CB:
                        dve.wait_ge(sm["qk2_full"], m + 1)
                        dve.wait_ge(sm["dT_done"], m + 1)
                        wait(dve, "hh_full", m - 1)
                        V.scalar_tensor_tensor(cT[:, m % 2].rearrange("p h s -> p (h s)"), P2[:, m % 2, :], XD ** -0.5,
                                               dT[:, m % 2].rearrange("p h s -> p (h s)"), ALU.mult,
                                               ALU.mult).then_inc(sm["cT_done"], 1)
                    if b > 0:
                        dve.wait_ge(sm["hh_full"], m)
                        V.tensor_copy(hs[:, b - 1, :, :], P1[:, (m - 1) % 2, 0:132].rearrange("p (h n) -> p h n", h=XH)).then_inc(sm["hs_done"], 1)
                dve.wait_ge(sm["hs_done"], CB * (c + 1))
                dve.wait_ge(sm["enm_done"], c + 1)
                hall = hs[:, :, :, :].rearrange("p b h n -> p (b h) n")
                enm_ = enm[:, :, :].rearrange("p b h -> p (b h)")
                link(V.scalar_tensor_tensor(hden[:, 0, :], hall[:, :, XD], -1.0, enm_, ALU.mult, ALU.max))
                link(V.tensor_tensor(hden[:, 0, :], hden[:, 0, :], hall[:, :, XD], ALU.max))
                link(V.tensor_scalar(hden[:, 1, :], hden[:, 0, :], 1e-6, None, ALU.add))
                link(V.reciprocal(hden[:, 2, :], hden[:, 1, :]))
                full = [128, CB * XH, XD]
                link(V.tensor_tensor(hn[:, :, :], hall[:, :, 0:XD], hden[:, 2, :].unsqueeze(2).broadcast_to(full), ALU.mult))
                link(V.tensor_reduce(hst[:, 0, :], hn[:, :, :], AX.X, ALU.add))
                link(V.tensor_scalar(hst[:, 1, :], hst[:, 0, :], 1.0 / XD, None, ALU.mult))
                V.tensor_tensor(hc[:, :, :], hn[:, :, :], hst[:, 1, :].unsqueeze(2).broadcast_to(full), ALU.subtract).then_inc(sm["hc_done"], 1)
                dve.wait_ge(sm["hq_done"], c + 1)
                link(V.tensor_reduce(hst[:, 5, :], hq[:, :, :], AX.X, ALU.add))
                V.tensor_scalar(hst[:, 2, :], hst[:, 5, :], 1.0 / XD, None, ALU.mult).then_inc(sm["hvar_done"], 1)
                dve.wait_ge(sm["hr_done"], c + 1)
                refine(hst[:, 2, :], HEAD_EPS, hst[:, 4, :], hst[:, 6, :], hst[:, 7, :])
                link(V.tensor_tensor(hn[:, :, :], hc[:, :, :], hst[:, 7, :].unsqueeze(2).broadcast_to(full), ALU.mult))
                hb = hn[:, :, :].rearrange("p (b h) n -> p b (h n)", b=CB)
                link(V.tensor_tensor(hb, hb, scale_row[:, :].unsqueeze(1).broadcast_to([128, CB, D]), ALU.mult))
                link(V.tensor_tensor(chunk(x2, c), chunk(x1, c), hb, ALU.add))

                layer_norm(NO[2, c], x2, c)
                dve.wait_ge(sm["xhi_done"], c + 1)
                V.tensor_tensor(tok(xlo, c), tok(x3T, c), tok(xhi, c), ALU.subtract).then_inc(sm["xhl_done"], 1)
                dve.wait_ge(sm["lg_full"], c + 1)
                link(V.tensor_copy(lg[:, :, :], PO[:, 0:CB * E].rearrange("p (b e) -> p b e", b=CB)))
                for b in range(CB):
                    last = V.max(top[:, b, :], lg[:, b, :])
                link(last)
                for b in range(CB):
                    V.max_index(topi[:, b, :], top[:, b, :], lg[:, b, :])
                all_ = [128, CB, E]
                link(V.tensor_tensor(rt[:, 1, :, :], lg[:, :, :], top[:, :, 0:1].broadcast_to(all_), ALU.subtract))
                V.tensor_copy(rt[:, 0, :, 0:2], topi[:, :, 0:2]).then_inc(sm["re_done"], 1)
                dve.wait_ge(sm["re_done"], c + 1)
                iota = cf[:, C_IOTA:C_IOTA + CB * E].rearrange("p (b e) -> p b e", b=CB)
                V.tensor_tensor(rt[:, 3, :, :], iota, rt[:, 0, :, 0:1].broadcast_to(all_), ALU.is_equal)
                link(V.tensor_tensor(rt[:, 4, :, :], iota, rt[:, 0, :, 1:2].broadcast_to(all_), ALU.is_equal))
                link(V.tensor_tensor(rt[:, 3, :, :], rt[:, 3, :, :], rt[:, 4, :, :], ALU.add))
                dve.wait_ge(sm["rexp_done"], c + 1)
                link(V.tensor_tensor(rt[:, 4, :, :], rt[:, 2, :, :], rt[:, 3, :, :], ALU.mult))
                V.tensor_reduce(rsum[:, 0, :], rt[:, 2, :, :], AX.X, ALU.add)
                link(V.tensor_reduce(rsum[:, 1, :], rt[:, 4, :, :], AX.X, ALU.add))
                link(V.scalar_tensor_tensor(rsum[:, 2, :], rsum[:, 0, :], 1e-9, rsum[:, 1, :], ALU.mult, ALU.add))
                link(V.reciprocal(rsum[:, 3, :], rsum[:, 2, :]))
                V.tensor_tensor(chunk(wts, c), rt[:, 4, :, :], rsum[:, 3, :].unsqueeze(2).broadcast_to(all_), ALU.mult).then_inc(sm["wts_done"], 1)
                dve.wait_ge(sm["bias_full"], c + 1)
                V.tensor_tensor(chunk(acc, c), chunk(x2, c), PO[:, :].rearrange("p (b d) -> p b d", b=CB), ALU.add).then_inc(sm["acc_done"], 1)

            def hidden(e, c):
                for f in range(FC):
                    n = e * 4 + (2 * c + f + 1)
                    dve.wait_ge(sm["sil_done"], n)
                    wait(dve, "y_full", e * 2 + (c - 1))
                    V.scalar_tensor_tensor(hT[:, 2 * c + f, :], (P1, P2)[f][:, 1, :],
                                           gub[:, 1, bass.ds(e * FC + f, 1)], sil[:, f, :], ALU.add,
                                           ALU.mult).then_inc(sm["h_done"], 1)

            def weigh(e, c):
                z = e * 2 + c
                dve.wait_ge(sm["y_full"], z + 1)
                wait(dve, "y_done", z - 1)
                P = (PO, PM)[c]
                for b in range(CB):
                    t = c * CB + b
                    last = V.scalar_tensor_tensor(acc[:, t, :], P[:, b * D:(b + 1) * D], wts[:, t, bass.ds(e, 1)],
                                                  acc[:, t, :], ALU.mult, ALU.add)
                last.then_inc(sm["y_done"], 1)

            dve.wait_ge(sm["acc_done"], NCH)
            hidden(0, 0)
            hidden(0, 1)
            weigh(0, 0)
            hidden(1, 0)
            weigh(0, 1)
            hidden(1, 1)
            weigh(1, 0)
            with dve.Fori(2, E) as e:
                hidden(e, 0)
                weigh(e - 1, 1)
                hidden(e, 1)
                weigh(e, 0)
            weigh(E - 1, 1)

        @block.tensor
        def _(pe):
            def mm(out_, lhsT, rhs, start=True, stop=True, **more):
                return nc.tensor.matmul(out_, lhsT, rhs, start=start, stop=stop, **more)

            def transpose_rows(n):
                pe.wait_ge(sm["xn_done"], CB * (n + 1))
                for b in range(CB):
                    last = mm(PM[:, b * S:(b + 1) * S], xn[:, b, :], ident, is_transpose=True)
                last.then_inc(sm["tr_full"], 1)
                pe.wait_ge(sm["xT_done"], n + 1)

            pe.wait_ge(sm["const_in"], 64)
            pe.wait_ge(sm["wqkv_in"], 48)
            for c in range(NCH):
                transpose_rows(NO[0, c])
                for s, w in enumerate((wq_sb, wk_sb)):
                    wait(pe, "sq_done", 2 * c)
                    mm(P1[:, s, :], w[:, :], tok(xT, c)).then_inc(sm["qk_full"], 1)
                wait(pe, "v_done", c)
                others = wv_sb[:, :].rearrange("p (m q n) -> p m q n", m=4, q=2)[:, :, 1, :]
                for b in range(CB):
                    mm(P3[:, 0, b * S:(b + 1) * S], tok(xT, c, b), wv_sb[:, :])
                for b in range(CB):
                    last = mm(P3[HALF:128, 1, b * 64:(b + 1) * 64], tok(xT, c, b)[:, 0:HALF], others)
                last.then_inc(sm["v_full"], 1)
                wait(pe, "wn_done", 2 * c)
                for s in range(2):
                    pe.wait_ge(sm["sq_done"], 2 * c + s + 1)
                    mm(P2[:, s, :], headblk, qk_sq[:, s, :]).then_inc(sm["nrm_full"], 1)

            def scores(u, P, right, done):
                k, bl = u.k % 4 // 2, u.k % 2
                keys = bl * S
                for g in range(4):
                    i, j = g // 2, g % 2
                    for h in range(2):
                        r = slice(h * HALF, (h + 1) * HALF)
                        mm(P[r, i, j * S:(j + 1) * S], sq_[k][r, g, keys + HALF:keys + S], right[k][r, g, keys:keys + S])
                        last = mm(P[r, i, 2 * S + j * HALF:2 * S + (j + 1) * HALF], sq_[k][r, g, keys:keys + HALF],
                                  right[k][r, g, keys:keys + HALF])
                last.then_inc(sm[done], 1)

            def pair_count(u, each):
                m = (u.k // 4 + 1) * each
                return m if u.i is None else u.i * each + m

            def step(s):
                u = s + 1
                if u.there():
                    wait(pe, "sel_done", u.n())
                    wait(pe, "wn_done", 4)
                    k = u.k % 4 // 2
                    pe.wait_ge(stack_in[k], pair_count(u, 48))
                    pass_waits(pe)
                    scores(u, P2, sn_, "n1_full")
                u = s + 2
                if u.there():
                    wait(pe, "e2_done", u.n())
                    k = u.k % 4 // 2
                    pe.wait_ge(stack_in[k], pair_count(u, 48))
                    pass_waits(pe)
                    scores(u, P1, sk_, "d2_full")
                t = s - 5
                if t.ends_batch():
                    pe.wait_ge(sm["oT_done"], t.batch(1))
                    mm(PM[:, 0:128], oT[:, :], wo_sb[:, :]).then_inc(sm["wo_full"], 1)
                t = s - 3
                if t.there():
                    wait(pe, "pT_done", t.n(1))
                    k, bl = t.k % 4 // 2, t.k % 2
                    pe.wait_ge(sm[f"v{k}_in"], pair_count(t, 16))
                    v = t.k % 4
                    if v == 0:
                        o = t.batch()
                    elif v == 3:
                        o = t.batch()
                    else:
                        o = None
                    if o is not None:
                        wait(pe, "o_copied", o)
                    out_ = PO[:, bl * 144:(bl + 1) * 144]
                    for i in range(2):
                        for j in range(2):
                            for h in range(2):
                                head = 2 * (4 * k + 2 * i + j) + h
                                hl = 2 * (2 * i + j) + h
                                w = pT[:, t.k % 2, i * 384 + j * S + h * HALF:i * 384 + j * S + (h + 1) * HALF]
                                mm(out_[HALF:128, head * 9:head * 9 + 9], w, v_st[k][:, bl, hl * 9:hl * 9 + 9])
                        for h in range(2):
                            w = pT[:, t.k % 2, i * 384 + 2 * S + h * HALF:i * 384 + 2 * S + (h + 1) * HALF]
                            first = 2 * (4 * k + 2 * i) + h
                            dst = out_[0:HALF, first * 9:first * 9 + 36].rearrange("p (q n) -> p q n", n=18)[:, :, 0:9] \
                                if first * 9 + 36 <= 144 else None
                            if dst is None:
                                dst = out_[0:HALF, (first - 1) * 9:(first - 1) * 9 + 36].rearrange(
                                    "p (q n) -> p q n", n=18)[:, :, 9:18]
                            at = 72 + 36 * i + 18 * h
                            last = mm(dst, w, v_st[k][:, bl, at:at + 18].rearrange("p (q n) -> p q n", q=2))
                    last.then_inc(sm["pv_done"], 1)
                t = s - 2
                if t.there():
                    wait(pe, "nm_done", t.n(1))
                    wait(pe, "shift_done", t.n())
                    x_ = s - 5
                    if x_.ends_batch():
                        wait(pe, "x1_done", x_.batch(1))
                    mm(PM[0:24, 0:64].bitcast(bf16), nmp[:, :, :].rearrange("p a b -> p (a b)"), ident_b,
                       is_transpose=True).then_inc(sm["nmT_full"], 1)
                    wait(pe, "shift_done", t.n(1))
                    wait(pe, "pT_done", t.n())
                    for i in range(2):
                        for q in range(3):
                            cols = slice(q * S, (q + 1) * S)
                            mm(P3[:, i, cols], dist[:, t.k % 4, i * 384 + q * S:i * 384 + (q + 1) * S], ident,
                               stop=False, is_transpose=True)
                            at = B_SEL + (3 * i + q) * S
                            last = mm(P3[:, i, cols], cb[:, at:at + S], shift[:, :], start=False)
                    last.then_inc(sm["t_full"], 1)
                t = s - 4
                if t.ends_batch():
                    pe.wait_ge(sm["o_done"], t.batch(1))
                    u2 = s - 2
                    if u2.there():
                        wait(pe, "shift_done", u2.n(1))
                    xd = s - 5
                    if t.k % 4 == 3:
                        pe.wait_ge(sm["x1_done"], t.batch())
                    mm(PM[:, 0:128], o_n[:, :, :].rearrange("p h n -> p (h n)"), ident, is_transpose=True).then_inc(sm["oT_full"], 1)

            pe.wait_ge(sm["init_done"], 2)
            pe.wait_ge(sm["misc_in"], 160)
            steps(pe, step, -2, NU + 4, 5, 12)

            pe.wait_ge(sm["ctx_in"], 32)
            for c in range(NCH):
                n = NO[1, c]
                if c == 0:
                    pe.wait_ge(sm["x1_done"], B)
                    pe.wait_ge(sm["wg_done"], 1)
                    pe.wait_ge(sm["xblk0"], 1)
                transpose_rows(n)
                wait(pe, "acc_done", c)
                mm(PO[0:36, :], wg[:, 0, :], tok(xT, c), stop=False)
                mm(PO[0:36, :], wg[:, 1, :], tok(ctxT, c), start=False).then_inc(sm["g_full"], 1)
                pe.wait_ge(sm["a_done"], c + 1)
                for b in range(CB):
                    last = mm(PM[:, b * 36:(b + 1) * 36], arow[:, b * S:(b + 1) * S], ident[0:36, 0:36], is_transpose=True)
                last.then_inc(sm["rT_full"], 1)
                if c == 0:
                    pe.wait_ge(sm["par_a"], 1)
                for b in range(CB + 1):
                    m = c * CB + b
                    if b < CB:
                        wait(pe, "dT_done", m - 1)
                        for h in range(XH):
                            mm(P3[:, m % 2, h * S:(h + 1) * S], ident_b, cb[:, B_MASK:B_MASK + S], stop=False)
                            at = C_NSEL + h * S
                            last = mm(P3[:, m % 2, h * S:(h + 1) * S], cf[0:4, at:at + S], runmax[:, b * S:(b + 1) * S],
                                      start=False)
                        last.then_inc(sm["ex_full"], 1)
                        wait(pe, "cT_done", m - 1)
                        mm(P2[:, m % 2, :], tok(ctxT, c, b), xblk[:, b].rearrange("p h s -> p (h s)")).then_inc(sm["qk2_full"], 1)
                    if b > 0:
                        k = m - 1
                        pe.wait_ge(sm["cT_done"], k + 1)
                        wait(pe, "hs_done", k - 1)
                        for h in range(XH):
                            last = mm(P1[:, k % 2, h * 33:(h + 1) * 33], cT[:, k % 2, h, :], ctx1[:, k, h, :])
                        last.then_inc(sm["hh_full"], 1)
                n = NO[2, c]
                transpose_rows(n)
                for b in range(CB):
                    last = mm(PO[:, b * E:(b + 1) * E], tok(x3T, c, b), rw[:, :])
                last.then_inc(sm["lg_full"], 1)
                pe.wait_ge(sm["wts_done"], c + 1)
                for b in range(CB):
                    last = mm(PM[0:E, b * S:(b + 1) * S], wts[:, c * CB + b, :], ident, is_transpose=True)
                last.then_inc(sm["wT_full"], 1)
                pe.wait_ge(sm["wT_done"], c + 1)
                for b in range(CB):
                    last = mm(PO[:, b * D:(b + 1) * D], wtsT[:, b * S:(b + 1) * S], db[:, :])
                last.then_inc(sm["bias_full"], 1)

            def gate_up(e, slot, c):
                pe.wait_ge(sm["w_ready"], e + 1)
                for f in range(FC):
                    wait(pe, "h_done", e * 4 + (2 * c + f - 1))
                    P = (P1, P2)[f]
                    for g in range(2):
                        cols = slice(f * 128, (f + 1) * 128)
                        mm(P[:, g, :], whi[:, slot, g, cols], tok(xhi, c), stop=False)
                        mm(P[:, g, :], whi[:, slot, g, cols], tok(xlo, c), start=False, stop=False)
                        last = mm(P[:, g, :], wlo[:, slot, g, cols], tok(xhi, c), start=False)
                    last.then_inc(sm["gu_full"], 1)

            def down(e, c):
                z = e * 2 + c
                pe.wait_ge(sm["h_done"], z * 2 + 2)
                wait(pe, "y_done", z - 1)
                P = (PO, PM)[c]
                for b in range(CB):
                    for f in range(FC):
                        last = mm(P[:, b * D:(b + 1) * D], hT[:, 2 * c + f, b * S:(b + 1) * S],
                                  wd[:, bass.ds(e * FC + f, 1), :].rearrange("p a d -> p (a d)"),
                                  start=(f == 0), stop=(f == FC - 1))
                last.then_inc(sm["y_full"], 1)

            pe.wait_ge(sm["exp_in"], 48)
            pe.wait_ge(sm["xhl_done"], NCH)
            pe.wait_ge(sm["acc_done"], NCH)
            gate_up(0, 0, 0)
            gate_up(0, 0, 1)
            down(0, 0)
            gate_up(1, 1, 0)
            down(0, 1)
            gate_up(1, 1, 1)
            down(1, 0)
            with pe.Fori(1, E // 2) as i:
                for j in range(2):
                    e = i * 2 + j
                    gate_up(e, j, 0)
                    down(e - 1, 1)
                    gate_up(e, j, 1)
                    down(e, 0)
            down(E - 1, 1)


def kernel(**inputs):
    import concourse.bacc as bacc
    from concourse.bass_utils import run_bass_kernel_spmd as run

    a = {n: np.asarray(v) for n, v in inputs.items()}
    att = lambda n: np.ascontiguousarray(a["L0_attn_" + n].T)
    const_f, const_b = constants()
    by_unit = lambda t: np.ascontiguousarray(t.reshape(E, FC, 128).transpose(2, 0, 1).reshape(128, E * FC))
    arrays = {
        "x": a["x"], "ctx": a["ctx_1024"],
        "ctx_t": np.ascontiguousarray(a["ctx_1024"].transpose(2, 0, 1).reshape(D, NT)),
        "wq_t": att("Wq"), "wk_t": att("Wk"), "wv_t": att("Wv"), "wo_t": att("Wo"),
        "log_c": a["L0_attn_log_c"].reshape(1, 1), "log_beta": a["L0_attn_log_beta"].reshape(1, 1),
        "ig_k": a["L0_xattn_igate_kernel"], "ig_b": a["L0_xattn_igate_bias"].reshape(XH, 1),
        "fg_k": a["L0_xattn_fgate_kernel"], "fg_b": a["L0_xattn_fgate_bias"].reshape(XH, 1),
        "norm_scale": a["L0_xattn_outnorm_scale"].reshape(1, D),
        "router_t": np.ascontiguousarray(a["L0_ffn_router_w"].T),
        "gate_w": a["L0_ffn_gate_w"], "gate_b": by_unit(a["L0_ffn_gate_b"]),
        "up_w": a["L0_ffn_up_w"], "up_b": by_unit(a["L0_ffn_up_b"]),
        "down_w": a["L0_ffn_down_w"], "down_b": a["L0_ffn_down_b"],
        "const_f": const_f, "const_b": const_b, "stack_init": stack_rows(),
    }
    nc = bacc.Bacc("TRN2", target_bir_lowering=False, num_devices=1)
    args = [nc.dram_tensor(n, v.shape, mybir.dt.from_np(v.dtype), kind="ExternalInput").ap() for n, v in arrays.items()]
    out = nc.dram_tensor("out", (B, S, D), mybir.dt.float32, kind="ExternalOutput").ap()
    decoder_layer(nc, *args, out)
    r = run(nc, [arrays], core_ids=[0])
    return r.results[0]["out"]
```

```python
import numpy as np
import concourse.bass as bass
from concourse import mybir
from contextlib import ExitStack

B, S, D = 8, 128, 128
NT = B * S
H, DH = 16, 8
XH, XD = 4, 32
E, F, FC = 8, 256, 2
CB = 4
NCH = B // CB
CT = CB * S
PB = 2
NP = B // PB
PT_ = PB * S
FRONT_AT = 13
HALF = S // 2
NU = 2 * B
UW = 768
SLOTS = 8
LN_EPS, ATT_EPS, HEAD_EPS = 1e-5, 1e-8, 1e-6
FAR = 1e30

C_ID = 0
C_BLK = 128
C_CM = 256
C_NSEL = 320
C_COL = C_NSEL + XH
(K_ONE, K_C, K_G1, K_G2, K_M3, K_M36, K_EPS, K_SEPS, K_R8, K_HALF, K_1, K_HEPS, K_EPSB) = range(13)
C_IOTA = C_COL + 16
C_TOT = C_IOTA + CB * E
B_ID = 0
B_SEL = 128
B_SEL2 = B_SEL + 8
B_MASK = B_SEL2 + 2 * S
B_SLOT = B_MASK + S
B_TOT = B_SLOT + 4

LN_SHIFT = float(np.exp(2 * (0.693 - 0.25)))


def constants():
    c = np.zeros((128, C_TOT), np.float32)
    p = np.arange(128)
    d = p // 4 % DH
    same = lambda f: f[:, None] == f[None, :]
    c[:, C_ID:C_ID + 128] = np.eye(128)
    c[:, C_BLK:C_BLK + 128] = same(p // 32) & same(p % 4)
    c[:, C_CM:C_CM + HALF] = np.where(np.arange(HALF)[None, :] > (p % HALF)[:, None], FAR, 0.0)
    for h in range(XH):
        c[h, C_NSEL + h] = -1.0
    col = c[:, C_COL:C_COL + 16]
    col[:, K_ONE] = d < 3
    col[:, K_C] = (d >= 3) & (d < 6)
    col[:, K_G1] = -1.0 * ((d < 6) & (d % 3 >= 1))
    col[:, K_G2] = -1.0 * ((d < 6) & (d % 3 == 2))
    col[:, K_M3] = d < 3
    col[:, K_M36] = (d >= 3) & (d < 6)
    col[:, K_EPS] = LN_EPS
    col[:, K_SEPS] = LN_SHIFT * ATT_EPS
    col[:, K_R8] = 8 ** -0.5
    col[:, K_HALF] = 0.5
    col[:, K_1] = 1.0
    col[:, K_HEPS] = HEAD_EPS
    c[:, C_IOTA:] = np.tile(np.arange(E), CB)[None, :]
    b = np.zeros((128, B_TOT), np.float32)
    b[:, B_ID:B_ID + 128] = np.eye(128)
    for part in range(3):
        b[8 * part:8 * part + 8, B_SEL:B_SEL + 8] = np.eye(8)
        for i in range(2):
            for j in range(2):
                at = B_SEL2 + i * S + j * HALF
                b[8 * part + 4 * i + 2 + j, at:at + HALF] = 1.0
    b[:, B_MASK:B_MASK + S] = np.where(p[:, None] > p[None, :], -FAR, 0.0)
    b[:, B_SLOT] = d < 6
    b[:, B_SLOT + 1] = d < 3
    return c, b.astype(mybir.dt.np(mybir.dt.bfloat16))


def head_rows():
    p = np.arange(128)
    return (8 * (p // 32 % 2) + 2 * (p % 4) + p // 64) * DH + p // 4 % DH


def stack_rows():
    r = np.zeros((128, 4, PT_), np.float32)
    row = np.arange(128)
    r[(row // DH % SLOTS == 6) & (row % DH >= 3) & (row % DH < 6)] = 1.0
    return r.astype(mybir.dt.np(mybir.dt.bfloat16))


def decoder_layer(nc, x, ctx, ctx_t, wq_t, wk_t, wv_t, wo_t, log_c, log_beta, ig_k, ig_b, fg_k, fg_b,
                  norm_scale, router_t, gate_w, gate_b, up_w, up_b, down_w, down_b,
                  const_f, const_b, stack_init, out):
    fp32, bf16, fp32r = mybir.dt.float32, mybir.dt.bfloat16, mybir.dt.float32r
    u8, u32 = mybir.dt.uint8, mybir.dt.uint32
    ALU, ACT, AX = mybir.AluOpType, mybir.ActivationFunctionType, mybir.AxisListType

    es = ExitStack()
    with es:
        def sb(name, shape, dt=fp32):
            return es.enter_context(nc.sbuf_tensor(name, shape, dt))

        def over(old, shape, dt=fp32, at=0):
            n = int(np.prod(shape[1:]))
            axes = " ".join("abcd"[:len(shape) - 1])
            flat = old[0:shape[0], at:at + n]
            flat = flat if dt == fp32 else flat.bitcast(dt)
            return flat.rearrange(f"p ({axes}) -> p {axes}", **dict(zip("abcd", shape[1:])))

        def sem(name):
            return es.enter_context(nc.semaphore(name))

        q_dram = nc.dram_tensor("q_split", [NP, 4, SLOTS, DH, 4, PT_], bf16, kind="Internal").ap()
        k_dram = nc.dram_tensor("k_split", [NP, SLOTS, 2, 2, DH, 4, PT_], bf16, kind="Internal").ap()
        n_dram = nc.dram_tensor("n_split", [NP, 2, 2, DH, 4, PT_], bf16, kind="Internal").ap()

        cf = sb("cf", [128, C_TOT])
        cb = sb("cb", [128, B_TOT], bf16)
        ident = cf[:, C_ID:C_ID + 128]
        ident_b = cb[:, B_ID:B_ID + 128]
        headblk = cf[:, C_BLK:C_BLK + 128]
        col = lambda k, p=slice(0, 128): cf[p, C_COL + k:C_COL + k + 1]
        x_sb = sb("x_sb", [128, B, D])
        x1 = x_sb
        x2 = x_sb
        wq_sb, wk_sb, wv_sb, wo_sb = (sb(n, [128, 128]) for n in ("wq_sb", "wk_sb", "wv_sb", "wo_sb"))
        par = sb("par", [128, 2])
        par_w = sb("par_w", [128, 4, 2])
        coef = sb("coef", [128, 1])
        eps_col = sb("eps_col", [128, 1])
        nbeta = sb("nbeta", [128, 1])
        ctx_sb = sb("ctx_sb", [128, B, D])
        acc = ctx_sb
        ctx1 = sb("ctx1", [128, B, XH, XD + 1])
        wg_raw = sb("wg_raw", [128, 3, 36])
        wg = sb("wg", [128, 2, 36])
        gb = sb("gb", [36, 1])
        scale_row = sb("scale_row", [128, D])
        rw = sb("rw", [128, E])
        wgu = sb("wgu", [128, E, 2, F])
        gub = sb("gub", [128, 2, E * FC])
        db = sb("db", [E, D])
        bst = sb("bst", [128, 2, CB, 6])
        mv = sb("mv", [128, 2, CB, 2])
        rs = sb("rs", [128, 2, 5, CB])
        xn = sb("xn", [128, CB, D])
        xT = sb("xT", [128, NT])
        proj_mem = sb("proj_mem", [128, 8 * CT])
        qkf = over(proj_mem, [128, 2, CT])
        qk_sq = over(proj_mem, [128, 2, CT], at=2 * CT)
        wn = over(proj_mem, [128, 2, CT], at=4 * CT)
        r1 = over(proj_mem, [128, 2, CT], at=6 * CT)
        w1_mem = sb("w1_mem", [128, 2 * CT])
        w1 = over(w1_mem, [128, 2, CT])
        wd = over(proj_mem, [128, E * FC, D])
        u0 = sb("u0", [128, 2, CT], bf16)
        u1 = sb("u1", [128, 2, CT], bf16)
        split_mem = sb("split_mem", [128, NCH * SLOTS * CT])
        split = [split_mem[:, n * SLOTS * CT:(n + 1) * SLOTS * CT].bitcast(bf16)
                 .rearrange("p (s n t) -> p s n t", s=2, n=SLOTS) for n in range(NCH)]
        ctxT = over(split_mem, [128, NT], at=2048)
        ksl = sb("ksl", [128, CT], bf16)
        nsl = sb("nsl", [128, NCH, CT], bf16)
        vab = sb("vab", [128, B, 2, 144])
        sk_, sn_ = ([sb(f"{n}{k}", [128, 4, PT_], bf16) for k in range(2)] for n in ("stk", "stn"))
        sq_ = [sb(f"stq{k}", [128, 8 * PB, 2, HALF], bf16) for k in range(2)]
        v_st = [sb(f"v_st{k}", [128, PB, 144]) for k in range(2)]
        dist_mem = sb("dist_mem", [128, 10 * UW])
        e2 = over(dist_mem, [128, 2, UW])
        l1 = over(dist_mem, [128, 2, UW], at=2 * UW)
        sqn = sb("sqn", [128, UW])
        wt = over(dist_mem, [128, 2, UW], at=4 * UW)
        da = over(dist_mem, [128, 2, UW], at=6 * UW)
        prod = over(dist_mem, [128, 2, UW], at=8 * UW)
        lp = sb("lp", [128, UW])
        m_ge = sb("m_ge", [128, 2, UW], u8)
        m_gt = sb("m_gt", [128, 2, UW], u8)
        dist = sb("dist", [128, 4, UW])
        nm = sb("nm", [128, 8])
        nmr = sb("nmr", [128, 2, 8])
        nmp = sb("nmp", [128, 3, 8], bf16)
        shift = sb("shift", [128, 128], bf16)
        pT = sb("pT", [128, 2, UW])
        o_sb = sb("o_sb", [128, H, DH + 1])
        o_rec = sb("o_rec", [128, H])
        o_n = sb("o_n", [128, PB, H, DH])
        oT = sb("oT", [128, 128])
        xblk = [over(split_mem, [128, CB, XH, S]), over(dist_mem, [128, CB, XH, S], at=4 * NT)]
        frow = over(split_mem, [36, 2, CT], at=3072)
        lf = over(proj_mem, [4, CT], at=4 * CT)
        cs = over(proj_mem, [4, CT], at=5 * CT)
        runmax_all = [over(w1_mem, [128, CT], at=c * CT) for c in range(NCH)]
        runmax = [t[0:4, :] for t in runmax_all]
        arow = over(proj_mem, [36, CT], at=7 * CT)
        aT = sb("aT", [128, NCH, CB, 36])
        enm = sb("enm", [128, NCH, CB, XH])
        dT = over(split_mem, [128, 2, XH, S], at=4096)
        cT = over(split_mem, [128, 2, XH, S], at=5120)
        hs = over(dist_mem, [128, CB, XH, XD + 1], at=6 * NT)
        hden = sb("hden", [128, 3, CB * XH])
        hn = over(split_mem, [128, CB * XH, XD], at=6144)
        hc = over(split_mem, [128, CB * XH, XD], at=6656)
        hq = over(split_mem, [128, CB * XH, XD], at=7168)
        hst = over(dist_mem, [128, 8, CB * XH], at=6 * NT + 640)
        lg = sb("lg", [128, CB, E])
        top = sb("top", [128, CB, 8])
        topi = sb("topi", [128, CB, 8], u32)
        rt = sb("rt", [128, 5, CB, E])
        rsum = sb("rsum", [128, 4, CB])
        wts = sb("wts", [128, B, E])
        wtsT = sb("wtsT", [E, CT])
        x3T = over(dist_mem, [128, NT])
        xhi = sb("xhi", [128, NT], fp32r)
        xlo = sb("xlo", [128, NT], fp32r)
        whi = sb("whi", [128, 2, 2, F], fp32r)
        wlo = sb("wlo", [128, 2, 2, F], fp32r)
        sil = over(dist_mem, [128, 2, CT], at=3 * NT)
        hT = over(dist_mem, [128, 4, CT], at=4 * NT)

        P1 = es.enter_context(nc.psum_tensor("P1", [128, 2, 512], fp32))
        P2 = es.enter_context(nc.psum_tensor("P2", [128, 2, 512], fp32))
        P3 = es.enter_context(nc.psum_tensor("P3", [128, 2, 512], fp32))
        PO = es.enter_context(nc.psum_tensor("PO", [128, 512], fp32))
        PM = es.enter_context(nc.psum_tensor("PM", [128, 512], fp32))

        names = ("cf_in par_in cb_in wqkv_in misc_in ctx_in exp_in stack0 v0_in v1_in out_done "
                 "bn_done mv_done lnv_done r0_done nt_done xn_done tr_full xT_done "
                 "v_full nrm_full qkf_done sq_done v_done wn_done split_b split_c split_done low_done "
                 "par_a coef_done init_done chain_a chain_d chain_p "
                 "d2_full n1_full e2_done l1_done sqn_done wt_done lp_done ds_done pT_done shift_done oT_done "
                 "ge_done da_done sel_done prod_done dist_done nm_done o_copied o_done x1_done "
                 "gt_done causal_done nmT_full t_full pv_done oT_full wo_full "
                 "g_full abs_done l1p_done a_done rT_full aT_done enm_done ex_full dT_done cT_done "
                 "hs_done hq_done hr_done "
                 "lg_full lg_done re_done rexp_done wts_done wT_full wT_done bias_full acc_done xhl_done "
                 "w_ready whi_done gu_full sil_done h_done y_full y_done qk_full par_ln o_rec_done nm0_done nm1_done nm2_done nm3_done "
                 "qk2_full hh_full hc_done hvar_done xhi_done wg_done xblk0 passed blk_done zeroed").split()
        sm = {n: sem(n) for n in names}
        x_in = [sem(f"x_in{c}") for c in range(NCH)]
        stored = [sem(f"stored{p}") for p in range(NP)]
        stack_in = [sem(f"stack_in{k}") for k in range(2)]
        block = es.enter_context(nc.Block())

        class At:

            def __init__(self, i, k):
                self.i, self.k = i, k

            def __add__(self, d):
                return At(self.i, self.k + d)

            def __sub__(self, d):
                return At(self.i, self.k - d)

            def there(self):
                return self.i is not None or 0 <= self.k < NU

            def n(self, more=0):
                v = self.k + more
                if self.i is None:
                    return v if v > 0 else None
                assert v > 0, "a wait on a register stays above zero"
                return self.i * 4 + v

            def batch(self, more=0):
                v = 2 * (self.k // 4) + (self.k % 2) + more
                if self.i is None:
                    return v
                assert v > 0, "a wait on a register stays above zero"
                return self.i * 2 + v

            def ends_batch(self):
                return self.k % 4 >= 2 and self.there()

        def wait(eng, name, n):
            if n is None or (isinstance(n, int) and n <= 0):
                return
            eng.wait_ge(sm[name], n)

        def pass_waits(eng):
            eng.sem_inc(sm["passed"], 1)

        def steps(eng, step, first, last, lo, hi, front):
            for s in range(first, lo):
                step(At(None, s))
            with eng.Fori(0, (hi - lo + 1) // 4) as i:
                for j in range(4):
                    step(At(i, lo + j))
            for s in range(hi + 1, NU + 5):
                if s <= last:
                    step(At(None, s))
                if 0 <= s - FRONT_AT < 5:
                    front(0, s - FRONT_AT)

        def cross_and_experts(front, row, back, gate, down):
            row(0)
            front(1, 0)
            row(1)
            front(1, 1)
            row(2)
            front(1, 2)
            front(1, 3)
            row(3)
            front(1, 4)
            row(4)
            back(0, 0)
            back(0, 1)
            row(5)
            back(0, 2)
            row(6)
            back(0, 3)
            row(7)
            back(0, 4)
            row(8)
            gate(0)
            back(0, 5)
            back(0, 6)
            back(0, 7)
            between = {1: (0, 1), 2: (2,), 3: (3,), 4: (4, 5), 5: (6,), 6: (7,)}
            for z in range(1, E):
                gate(z)
                down(z - 1)
                for k in between.get(z, ()):
                    back(1, k)

        def linker(eng, name):
            count = [0]

            def link(ins):
                count[0] += 1
                ins.then_inc(sm[name], 1)
                eng.wait_ge(sm[name], count[0])
            return link

        NO = {(k, c): 2 * k + c for k in range(3) for c in range(NCH)}

        def chunk(t, c):
            return t[:, c * CB:(c + 1) * CB, :]

        def tok(t, c, b=None):
            return t[:, c * CT:(c + 1) * CT] if b is None else t[:, c * CT + b * S:c * CT + (b + 1) * S]

        def wide(t, *shape):
            return t.broadcast_to(list(shape))

        def load_stack(sp, bp, k):
            n = bass.ds(bp, 1)
            for j in range(2):
                r = slice(j * HALF, (j + 1) * HALF)
                q = q_dram[n, 2 * j + k].rearrange("a s d g (m t) -> (a s d) (g m) t", t=HALF)
                sp.dma_start(sq_[k][r, :, j, :], q).then_inc(stack_in[k], 16)
                sp.dma_start(sk_[k][r, :, :], k_dram[n, :, j, k].rearrange("a s d g t -> (a s) d (g t)")).then_inc(stack_in[k], 16)
                last = slice(j * HALF + HALF - DH, (j + 1) * HALF)
                sp.dma_start(sn_[k][last, :, :], n_dram[n, j, k].rearrange("a d g t -> (a d) (g t)")).then_inc(stack_in[k], 16)

        def load_values(sp, bp, k):
            sp.dma_start(v_st[k][:, :, :], vab[:, bass.ds(bp * PB, PB), k, :]).then_inc(sm[f"v{k}_in"], 16)

        def cross_bank(m):
            return (PO, PM)[m % 2] if m < CB else P1[:, m % 2, :]

        def back_banks(c):
            return (PM[:, :], PO[:, :]) if c == 0 else (P3[:, 0, :], P3[:, 1, :])

        @block.sync
        def _(sp):
            xv = x.rearrange("b s d -> s b d")
            sp.dma_start(chunk(x_sb, 0), xv[:, 0:CB, :]).then_inc(x_in[0], 16)
            sp.dma_start(cf[:, :], const_f).then_inc(sm["cf_in"], 16)
            sp.dma_start(wq_sb[:, :], wq_t).then_inc(sm["wqkv_in"], 16)
            sp.dma_start(wk_sb[:, :], wk_t).then_inc(sm["wqkv_in"], 16)
            sp.dma_start(wv_sb[:, :], wv_t).then_inc(sm["wqkv_in"], 16)
            sp.dma_start(par[:, 0:1], log_c.to_broadcast([128, 1])).then_inc(sm["par_in"], 16)
            sp.dma_start(par[:, 1:2], log_beta.to_broadcast([128, 1])).then_inc(sm["par_in"], 16)
            sp.dma_start(cb[:, :], const_b).then_inc(sm["cb_in"], 16)
            sp.dma_start(chunk(x_sb, 1), xv[:, CB:B, :]).then_inc(x_in[1], 16)
            for k in range(2):
                sp.dma_start(sn_[k][:, :, :], stack_init).then_inc(sm["stack0"], 16)
            sp.dma_start(wo_sb[:, :], wo_t).then_inc(sm["misc_in"], 16)
            sp.dma_start(rw[:, :], router_t).then_inc(sm["misc_in"], 16)
            sp.dma_start(db[:, :], down_b).then_inc(sm["misc_in"], 16)
            sp.dma_start(gub[:, 0, :], gate_b).then_inc(sm["misc_in"], 16)
            sp.dma_start(gub[:, 1, :], up_b).then_inc(sm["misc_in"], 16)
            sp.dma_start(gb[0:4, :], ig_b).then_inc(sm["misc_in"], 16)
            sp.dma_start(gb[32:36, :], fg_b).then_inc(sm["misc_in"], 16)
            sp.dma_start(scale_row[:, :], norm_scale.to_broadcast([128, D])).then_inc(sm["misc_in"], 16)
            sp.wait_ge(sm["init_done"], 1)
            sp.dma_start(wg_raw[:, :, 0:4], ig_k.rearrange("(t p) h -> p t h", p=128)).then_inc(sm["misc_in"], 16)
            sp.dma_start(wg_raw[:, :, 32:36], fg_k.rearrange("(t p) h -> p t h", p=128)).then_inc(sm["misc_in"], 16)
            sp.wait_ge(sm["stack0"], 32)
            for c in range(NCH):
                sp.wait_ge(sm["split_done"], c + 1)
                sp.wait_ge(sm["low_done"], 2 * c + 2)
                for p in range(2):
                    cols = slice(p * PT_, (p + 1) * PT_)
                    n = 2 * c + p
                    for jk in range(4):
                        rows = slice(jk * 32, (jk + 1) * 32)
                        sp.dma_start(q_dram[n, jk].rearrange("s d g t -> (d g) s t"),
                                     split[c][rows, 0, :, cols]).then_inc(stored[n], 16)
                    sp.dma_start(k_dram[n].rearrange("s j k d g t -> (j k d g) s t"),
                                 split[c][:, 1, :, cols]).then_inc(stored[n], 16)
                    sp.dma_start(n_dram[n].rearrange("j k d g t -> (j k d g) t"), nsl[:, c, cols]).then_inc(stored[n], 16)
                if c == 0:
                    sp.wait_ge(stored[0], 96)
                    sp.wait_ge(sm["v_done"], 1)
                    sp.wait_ge(sm["zeroed"], 1)
                    for k in range(2):
                        load_stack(sp, 0, k)
                    for k in range(2):
                        load_values(sp, 0, k)
            sp.dma_start(ctx_sb[:, :, :], ctx.rearrange("b s d -> s b d")).then_inc(sm["ctx_in"], 16)
            sp.dma_start(wgu[:, :, 0, :], gate_w.rearrange("e d f -> d e f")).then_inc(sm["exp_in"], 16)
            sp.dma_start(wgu[:, :, 1, :], up_w.rearrange("e d f -> d e f")).then_inc(sm["exp_in"], 16)
            sp.dma_start(wd[:, :, :], down_w.rearrange("e (c f) d -> f (e c) d", c=FC)).then_inc(sm["exp_in"], 16)
            for n in range(1, NP):
                sp.wait_ge(stored[n], 96)
            sp.dma_start(ctxT[:, :], ctx_t).then_inc(sm["ctx_in"], 16)
            sp.wait_ge(sm["v_done"], 2)

            def next_stack(bp, k):
                sp.wait_ge(sm["d2_full"], bp * 4 + (2 * k - 2))
                sp.wait_ge(sm["n1_full"], bp * 4 + (2 * k - 2))
                load_stack(sp, bp, k)

            def next_values(bp, k):
                sp.wait_ge(sm["pv_done"], bp * 4 + (2 * k - 2))
                load_values(sp, bp, k)

            for k in range(2):
                next_stack(1, k)
            with sp.Fori(2, NP) as bp:
                for k in range(2):
                    next_stack(bp, k)
                    next_values(bp - 1, k)
            for k in range(2):
                next_values(NP - 1, k)
            for c in range(NCH):
                sp.wait_ge(sm["y_done"], E * (c + 1))
                sp.dma_start(out.rearrange("b s d -> s b d")[:, c * CB:(c + 1) * CB, :],
                             chunk(acc, c)).then_inc(sm["out_done"], 16)
            sp.wait_ge(sm["out_done"], 16 * NCH)

        @block.gpsimd
        def _(pool):
            link = linker(pool, "chain_p")
            pool.memset(eps_col[:, :], LN_EPS)
            pool.memset(wg_raw[:, :, :], 0.0).then_inc(sm["init_done"], 1)
            link(pool.memset(vab[:, :, :, :], 0.0))
            for k in range(2):
                va = vab[:, :, k, 0:72].rearrange("p b (h n) -> p b h n", n=DH + 1)
                link(pool.memset(va[:, :, :, DH], 1.0))
                vb = vab[:, :, k, 72:144].rearrange("p b (i q n) -> p b i q n", i=4, q=2)
                link(pool.memset(vb[0:HALF, :, :, 0, DH], 1.0))
                link(pool.memset(vb[HALF:128, :, :, 1, DH], 1.0))
            pool.memset(shift[:, :], 0.0)
            pool.memset(ctx1[:, :, :, XD], 1.0).then_inc(sm["init_done"], 1)
            pool.wait_ge(sm["cb_in"], 16)
            for c in range(NCH):
                pool.tensor_copy(split[c][:, 0, 7, :], cb[:, B_SLOT:B_SLOT + 1].to_broadcast([128, CT]))
                pool.tensor_copy(split[c][:, 1, 6, :], cb[:, B_SLOT + 1:B_SLOT + 2].to_broadcast([128, CT]))
            for c in range(NCH):
                for s in range(2):
                    pool.wait_ge(sm["split_c"], 2 * c + s + 1)
                    first_mid, low = ((3, 5), (2, 0))[s]
                    pool.tensor_tensor(split[c][:, s, low, :], r1[:, s, :], split[c][:, s, first_mid, :],
                                       ALU.subtract).then_inc(sm["low_done"], 1)
            pool.wait_ge(sm["cf_in"], 16)

            def step(s):
                g = s - 1
                if g.there():
                    wait(pool, "dist_done", g.n(1))
                    for i in range(2):
                        row = dist[:, g.k % 4, i * 384:(i + 1) * 384]
                        wideq = row[:, 0:256].rearrange("p (j n) -> p j n", j=2)[:, :, HALF:128]
                        near = row[:, 256:384].rearrange("p (j n) -> p j n", j=2)
                        cm = cf[:, C_CM:C_CM + HALF].unsqueeze(1).broadcast_to([128, 2, HALF])
                        pool.tensor_tensor(wideq, wideq, cm, ALU.add)
                        last = pool.tensor_tensor(near, near, cm, ALU.add)
                    last.then_inc(sm["causal_done"], 1)
                g = s + 1
                if g.there():
                    wait(pool, "e2_done", g.n(1))
                    wait(pool, "dist_done", g.n(-1))
                    pass_waits(pool)
                    pool.tensor_scalar(m_gt[:, g.k % 2, :], e2[:, g.k % 2, :], 4.0 - ATT_EPS, None,
                                       ALU.is_gt).then_inc(sm["gt_done"], 1)

            def zeros(s):
                if s == 5:
                    for n in range(NP):
                        pool.wait_ge(stored[n], 96)
                    pool.memset(arow[:, :], 0.0)
                    pool.memset(w1_mem[:, :], 0.0)
                    pool.memset(xblk[0][:, :, :, :], 0.0).then_inc(sm["xblk0"], 1)

            for s in range(-1, 7):
                step(At(None, s))
                zeros(s)
            with pool.Fori(0, 2) as i:
                for j in range(4):
                    step(At(i, 7 + j))
            for s in range(15, NU + 1):
                step(At(None, s))
            pool.memset(xblk[1][:, :, :, :], 0.0).then_inc(sm["xblk0"], 1)
            pool.wait_ge(sm["ctx_in"], 32)
            pool.tensor_copy(ctx1[:, :, :, 0:XD], ctx_sb[:, :, :].rearrange("p b (h d) -> p b h d", h=XH)).then_inc(sm["par_a"], 1)

            pool.wait_ge(sm["exp_in"], 48)

            def prepare(z, e, slot):
                w = wgu[:, bass.ds(e, 1), :, :].rearrange("p a g f -> p (a g f)")
                hi = whi[:, slot].rearrange("p g f -> p (g f)")
                lo = wlo[:, slot].rearrange("p g f -> p (g f)")
                if not isinstance(z, int) or z >= 2:
                    pool.wait_ge(sm["gu_full"], z * 2 - 2)
                pool.tensor_copy(hi, w).then_inc(sm["whi_done"], 1)
                pool.wait_ge(sm["whi_done"], z + 1)
                pass_waits(pool)
                pool.tensor_tensor(lo, w, hi, ALU.subtract).then_inc(sm["w_ready"], 1)

            prepare(0, 0, 0)
            prepare(1, 1, 1)
            with pool.Fori(1, E // 2) as i:
                for j in range(2):
                    prepare(i * 2 + j, i * 2 + j, j)
            with pool.Fori(0, E // 2) as i:
                for j in range(2):
                    prepare(i * 2 + (E + j), i * 2 + j, j)

        @block.scalar
        def _(act):
            link = linker(act, "chain_a")
            A = act.activation
            act.preload_act_table_set("natural_log_exp_and_others")
            def parameters():
                act.wait_ge(sm["cf_in"], 16)
                act.wait_ge(sm["par_in"], 32)
                link(A(par_w[:, 0, :], par[:, :], ACT.Abs))
                link(A(par_w[:, 1, :], par_w[:, 0, :], ACT.Exp, scale=-1.0))
                A(par_w[:, 2, :], par_w[:, 1, :], ACT.Ln, bias=col(K_1)).then_inc(sm["par_ln"], 1)

            def rstd_start(n, var, eps, done, before, store):
                act.wait_ge(sm[before], n)
                link(A(store[0], var, ACT.Ln, bias=eps))
                A(store[1], store[0], ACT.Exp, scale=-0.5).then_inc(sm[done], 1)

            def norm_rstd(n):
                wait(act, "xn_done", CB * (n - 1))
                rstd_start(CB * (n + 1), mv[:, n % 2, :, 1], eps_col[:, :], "r0_done", "mv_done",
                           (rs[:, n % 2, 0, :], rs[:, n % 2, 1, :]))

            def evacuate_xT(n, src, dst):
                act.wait_ge(sm["tr_full"], n + 1)
                A(dst, src, ACT.Copy).then_inc(sm["xT_done"], 1)

            act.wait_ge(sm["init_done"], 1)
            norm_rstd(NO[0, 0])
            parameters()
            evacuate_xT(NO[0, 0], PM[:, :], tok(xT, 0))
            norm_rstd(NO[0, 1])
            for c in range(NCH):
                wait(act, "split_b", 2 * c)
                wait(act, "nrm_full", 2 * c)
                for s in range(2):
                    act.wait_ge(sm["qk_full"], 2 * c + s + 1)
                    sign = 1.0 if s == 0 else -2.0
                    A(split[c][:, s, 0:3, :] if s == 0 else split[c][:, s, 1:6:2, :],
                      P1[:, s, :].unsqueeze(1).broadcast_to([128, 3, CT]), ACT.Copy, scale=sign)
                    A(qkf[:, s, :], P1[:, s, :], ACT.Copy, scale=sign).then_inc(sm["qkf_done"], 1)
                    A(qk_sq[:, s, :], P1[:, s, :], ACT.Square).then_inc(sm["sq_done"], 1)
                if c == 0:
                    evacuate_xT(NO[0, 1], PM[:, :], tok(xT, 1))
                act.wait_ge(sm["v_full"], c + 1)
                act.wait_ge(sm["init_done"], 2)
                for k in range(2):
                    va = vab[:, c * CB:(c + 1) * CB, k, 0:72].rearrange("p b (h n) -> p b h n", n=DH + 1)
                    A(va[:, :, :, 0:DH], P3[:, 0, :].rearrange("p (b k h n) -> p b k h n", b=CB, k=2, h=8)[:, :, k, :, :],
                      ACT.Copy)
                    for i in range(2):
                        vb = vab[:, c * CB:(c + 1) * CB, k, 72 + 36 * i:108 + 36 * i].rearrange(
                            "p b (j q n) -> p b j q n", j=2, q=2)
                        lo = P3[0:HALF, 0, :].rearrange("p (b m q j n) -> p b m q j n", b=CB, m=4, q=2, j=2)
                        hi = P3[HALF:128, 1, 0:256].rearrange("p (b m j n) -> p b m j n", b=CB, m=4, j=2)
                        A(vb[0:HALF, :, :, 0, 0:DH], lo[:, :, 2 * k + i, 0, :, :], ACT.Copy)
                        last = A(vb[HALF:128, :, :, 1, 0:DH], hi[:, :, 2 * k + i, :, :], ACT.Copy)
                last.then_inc(sm["v_done"], 1)
                act.wait_ge(sm["coef_done"], 1)
                wait(act, "split_done", c)
                for s in range(2):
                    act.wait_ge(sm["nrm_full"], 2 * c + s + 1)
                    bias = {} if s == 0 else {"bias": col(K_C)}
                    A(u0[:, s, :], P2[:, s, :], ACT.Identity, scale=coef[:, :], **bias)
                    A(wn[:, s, :], P2[:, s, :], ACT.Identity, scale=coef[:, :], **bias).then_inc(sm["wn_done"], 1)

            def step(s):
                u, t = s + 1, s - 3
                p = u.k % 2
                ps1, ps2 = (P[:, :, 0:384] for P in (P1, P2))
                def row(t, w=None):
                    r = t[:, :] if w is None else t[:, w, :]
                    return r.rearrange("p (i n) -> p i n", i=2)
                if u.there():
                    wait(act, "d2_full", u.n(1))
                    for w in ("l1_done", "ge_done", "prod_done", "gt_done"):
                        wait(act, w, u.n(-1))
                    A(row(e2, p), ps1, ACT.Relu).then_inc(sm["e2_done"], 1)
                if u.there():
                    wait(act, "e2_done", u.n(1))
                    wait(act, "da_done", u.n(-1))
                    A(l1[:, p, :], e2[:, p, :], ACT.Ln, scale=LN_SHIFT, bias=col(K_SEPS)).then_inc(sm["l1_done"], 1)
                if t.there():
                    wait(act, "t_full", t.n(1))
                    wait(act, "pv_done", t.n(-1))
                    A(row(pT, t.k % 2), P3[:, :, 0:384], ACT.Exp, scale=nbeta[:, :]).then_inc(sm["pT_done"], 1)
                x = s - 5
                if x.ends_batch():
                    act.wait_ge(sm["oT_full"], x.batch(1))
                    A(oT[:, :], PM[:, 0:128], ACT.Copy).then_inc(sm["oT_done"], 1)
                if u.there():
                    wait(act, "n1_full", u.n(1))
                    wait(act, "wt_done", u.n())
                    A(row(sqn), ps2, ACT.Square, scale=col(K_R8), bias=col(K_R8)).then_inc(sm["sqn_done"], 1)
                if s.there():
                    wait(act, "prod_done", s.n(1))
                    wait(act, "ds_done", s.n())
                    A(lp[:, :], prod[:, s.k % 2, :], ACT.Ln, scale=16.0).then_inc(sm["lp_done"], 1)
                if u.there():
                    wait(act, "sqn_done", u.n(1))
                    wait(act, "prod_done", u.n(-1))
                    A(wt[:, p, :], sqn[:, :], ACT.Square, bias=col(K_HALF)).then_inc(sm["wt_done"], 1)
                t = s - 2
                if t.there():
                    wait(act, "nmT_full", t.n(1))
                    wait(act, "t_full", t.n())
                    A(shift[0:24, :], PM[0:24, 0:64].bitcast(bf16), ACT.Copy).then_inc(sm["shift_done"], 1)
                if s.there():
                    wait(act, "lp_done", s.n(1))
                    wait(act, "t_full", s.n(-3))
                    A(dist[:, s.k % 4, :], lp[:, :], ACT.Exp, scale=0.5).then_inc(sm["ds_done"], 1)

            def front(c, k):
                n = NO[1, c]
                if k == 0:
                    norm_rstd(n)
                if k == 2:
                    act.wait_ge(sm["xblk0"], c + 1)
                    act.wait_ge(sm["tr_full"], n + 1)
                    A(tok(xT, c), P1[:, 0, :], ACT.Copy).then_inc(sm["xT_done"], 1)
                    for h in range(XH):
                        r = slice(h * XD, (h + 1) * XD)
                        last = A(xblk[c][r, :, h, :], P1[r, 0, :].rearrange("p (b s) -> p b s", b=CB), ACT.Copy)
                    last.then_inc(sm["blk_done"], 1)
                if k == 3:
                    act.wait_ge(sm["g_full"], c + 1)
                    fr = slice(32, 36)
                    wait(act, "a_done", c)
                    A(frow[fr, 0, :], P1[fr, 1, :], ACT.Abs, bias=gb[fr, :]).then_inc(sm["abs_done"], 1)
                    act.wait_ge(sm["abs_done"], c + 1)
                    link(A(frow[fr, 0, :], frow[fr, 0, :], ACT.Exp, scale=-1.0))
                    A(frow[fr, 0, :], frow[fr, 0, :], ACT.Ln, bias=col(K_1, fr)).then_inc(sm["l1p_done"], 1)
                if k == 4:
                    act.wait_ge(sm["rT_full"], c + 1)
                    A(aT[:, c, :, :], P1[:, 0, 0:144].rearrange("p (b n) -> p b n", b=CB), ACT.Copy).then_inc(sm["aT_done"], 1)
                    act.wait_ge(sm["aT_done"], c + 1)
                    A(enm[:, c, :, :], aT[:, c, :, 32:36], ACT.Exp, scale=-1.0).then_inc(sm["enm_done"], 1)

            def row(m):
                if m < B:
                    act.wait_ge(sm["ex_full"], m + 1)
                    wait(act, "cT_done", m - 1)
                    for h in range(XH):
                        last = A(dT[:, m % 2, h, :], P3[:, m % 2, h * S:(h + 1) * S], ACT.Exp,
                                 bias=aT[:, m // CB, m % CB, h:h + 1])
                    last.then_inc(sm["dT_done"], 1)

            def back(c, k):
                n = NO[2, c]
                if k == 0:
                    act.wait_ge(sm["hc_done"], c + 1)
                    A(hq[:, :, :], hc[:, :, :], ACT.Square).then_inc(sm["hq_done"], 1)
                if k == 1:
                    rstd_start(c + 1, hst[:, 2, :], col(K_HEPS), "hr_done", "hvar_done", (hst[:, 3, :], hst[:, 4, :]))
                if k == 2:
                    norm_rstd(n)
                if k == 4:
                    evacuate_xT(n, back_banks(c)[0], tok(x3T, c))
                    act.wait_ge(sm["xT_done"], n + 1)
                    A(tok(xhi, c), tok(x3T, c), ACT.Copy).then_inc(sm["xhi_done"], 1)
                if k == 5:
                    act.wait_ge(sm["re_done"], c + 1)
                    A(rt[:, 2, :, :], rt[:, 1, :, :], ACT.Exp).then_inc(sm["rexp_done"], 1)
                if k == 6:
                    act.wait_ge(sm["wT_full"], c + 1)
                    wait(act, "bias_full", c)
                    A(wtsT[:, :], back_banks(c)[0][0:E, :], ACT.Copy).then_inc(sm["wT_done"], 1)

            def silu(z, e):
                for f in range(FC):
                    n = z * 2 + (f + 1)
                    act.wait_ge(sm["gu_full"], n)
                    wait(act, "h_done", n - 2)
                    P = (P1, P2)[f]
                    pass_waits(act)
                    A(sil[:, f, :], P[:, 0, :], ACT.Silu,
                      bias=gub[:, 0, bass.ds(e * FC + f, 1)]).then_inc(sm["sil_done"], 1)

            steps(act, step, -1, NU + 4, 5, 12, front)
            cross_and_experts(front, row, back, lambda z: silu(z, z), lambda z: None)
            with act.Fori(0, E) as e:
                silu(e + E, e)

        @block.vector
        def _(dve):
            link = linker(dve, "chain_d")
            V = dve
            V.memset(sq_[0][:, :, :, :], 0.0)
            V.memset(sq_[1][:, :, :, :], 0.0).then_inc(sm["zeroed"], 1)

            def parameters():
                dve.wait_ge(sm["par_in"], 32)
                dve.wait_ge(sm["cf_in"], 16)
                link(V.tensor_scalar(par_w[:, 3, :], par[:, :], 0.0, None, ALU.max))
                dve.wait_ge(sm["par_ln"], 1)
                link(V.tensor_tensor(par_w[:, 3, :], par_w[:, 3, :], par_w[:, 2, :], ALU.add))
                V.tensor_scalar(nbeta[:, :], par_w[:, 3, 1:2], 0.5, -0.25, ALU.add, ALU.mult)
                V.scalar_tensor_tensor(coef[:, :], par_w[:, 3, 0:1], col(K_C), col(K_ONE), ALU.mult,
                                       ALU.add).then_inc(sm["coef_done"], 1)

            def refine(var, eps, r0, t, r):
                link(V.tensor_tensor(t, r0, r0, ALU.mult))
                link(V.scalar_tensor_tensor(t, var, eps, t, ALU.add, ALU.mult))
                link(V.tensor_scalar(t, t, -0.5, 1.5, ALU.mult, ALU.add))
                link(V.tensor_tensor(r, r0, t, ALU.mult))

            def norm_stats(n, src, c):
                p = n % 2
                for b in range(CB):
                    last = V.bn_stats(bst[:, p, b, :], src[:, c * CB + b, :])
                link(last)
                for b in range(CB):
                    V.bn_aggr(mv[:, p, b, :], bst[:, p, b, :]).then_inc(sm["mv_done"], 1)

            def norm_rows(n, src, c):
                p = n % 2
                dve.wait_ge(sm["r0_done"], n + 1)
                refine(mv[:, p, :, 1], LN_EPS, rs[:, p, 1, :], rs[:, p, 2, :], rs[:, p, 4, :])
                wait(dve, "tr_full", n)
                for b in range(CB):
                    V.tensor_scalar(xn[:, b, :], src[:, c * CB + b, :], mv[:, p, b, 0:1], rs[:, p, 4, b:b + 1],
                                    ALU.subtract, ALU.mult).then_inc(sm["xn_done"], 1)

            for c in range(NCH):
                dve.wait_ge(x_in[c], 16)
                norm_stats(NO[0, c], x_sb, c)
                norm_rows(NO[0, c], x_sb, c)
                if c == 0:
                    parameters()
            for c in range(NCH):
                for s in range(2):
                    sp_ = split[c][:, s]
                    first = sp_[:, s, :]
                    mid = sp_[:, 3:5, :] if s == 0 else sp_[:, 2:5:2, :]
                    dve.wait_ge(sm["qkf_done"], 2 * c + s + 1)
                    wait(dve, "low_done", 2 * c)
                    V.tensor_tensor(r1[:, s, :], qkf[:, s, :], first, ALU.subtract).then_inc(sm["split_b"], 1)
                    dve.wait_ge(sm["split_b"], 2 * c + s + 1)
                    V.tensor_copy(mid, r1[:, s, :].unsqueeze(1).broadcast_to([128, 2, CT])).then_inc(sm["split_c"], 1)
                for s in range(2):
                    dve.wait_ge(sm["wn_done"], 2 * c + s + 1)
                    link(V.scalar_tensor_tensor(w1[:, s, :], u0[:, s, :], col(K_G1), wn[:, s, :], ALU.mult, ALU.add))
                    link(V.tensor_copy(u1[:, s, :], w1[:, s, :]))
                    dst = split[c][:, 0, 6, :] if s == 0 else ksl[:, :]
                    link(V.scalar_tensor_tensor(dst, u1[:, s, :], col(K_G2), w1[:, s, :], ALU.mult, ALU.add))
                V.tensor_scalar(split[c][:, 1, 7, :], ksl[:, :], col(K_M3), None, ALU.mult)
                V.tensor_scalar(nsl[:, c, :], ksl[:, :], col(K_M36), None, ALU.mult).then_inc(sm["split_done"], 1)

            def step(s):
                def row(t, w):
                    return t[:, w, :].rearrange("p (i n) -> p i n", i=2)
                n1 = P2[:, :, 0:384]
                low, far, near = s - 2, s - 1, s + 1
                t = s - 4
                if t.ends_batch():
                    wait(dve, "pv_done", t.n(1))
                    bl = t.k % 2
                    if bl:
                        wait(dve, "o_done", t.batch())
                    o = PO[:, bl * 144:(bl + 1) * 144].rearrange("p (h n) -> p h n", n=DH + 1)
                    V.tensor_copy(o_sb[:, :, :], o).then_inc(sm["o_copied"], 1)
                if s.there():
                    p = s.k % 2
                    wait(dve, "l1_done", s.n(1))
                    wait(dve, "sqn_done", s.n(1))
                    wait(dve, "dist_done", s.n(-1))
                    V.scalar_tensor_tensor(row(da, p), row(l1, p), 2.0, n1, ALU.mult, ALU.add).then_inc(sm["da_done"], 1)
                    wait(dve, "ge_done", s.n(1))
                    wait(dve, "wt_done", s.n(1))
                    pass_waits(dve)
                    V.copy_predicated(row(wt, p), row(m_ge, p), n1).then_inc(sm["sel_done"], 1)
                if t.ends_batch():
                    dve.wait_ge(sm["o_copied"], t.batch(1))
                    V.reciprocal(o_rec[:, :], o_sb[:, :, DH]).then_inc(sm["o_rec_done"], 1)
                if s.there():
                    wait(dve, "sel_done", s.n(1))
                    wait(dve, "lp_done", s.n(-1))
                    V.scalar_tensor_tensor(prod[:, p, :], e2[:, p, :], ATT_EPS, wt[:, p, :], ALU.add,
                                           ALU.mult).then_inc(sm["prod_done"], 1)
                if low.there():
                    wait(dve, "causal_done", low.n(1))
                    d = row(dist, low.k % 4)
                    m = nm[:, :].rearrange("p (i q) -> p i q", i=2)
                    V.tensor_reduce(m[:, :, 0:2], d[:, :, 0:256].rearrange("p i (j n) -> p i j n", j=2), AX.X, ALU.min,
                                    negate=True)
                    V.tensor_reduce(m[:, :, 2:4], d[:, :, 256:384].rearrange("p i (j n) -> p i j n", j=2), AX.X, ALU.min,
                                    negate=True).then_inc(sm["nm0_done"], 1)
                if t.ends_batch():
                    dve.wait_ge(sm["o_rec_done"], t.batch(1))
                    V.tensor_tensor(o_n[:, bl, :, :], o_sb[:, :, 0:DH],
                                    o_rec[:, :].unsqueeze(2).broadcast_to([128, H, DH]), ALU.mult).then_inc(sm["o_done"], 1)
                if low.there():
                    wait(dve, "nm0_done", low.n(1))
                    wait(dve, "nmT_full", low.n())
                    V.tensor_copy(nmp[:, 0, :], nm[:, :]).then_inc(sm["nm1_done"], 1)
                t = s - 5
                if t.ends_batch():
                    dve.wait_ge(sm["wo_full"], t.batch(1))
                    b = bass.ds(t.batch(1) - 1, 1)
                    V.tensor_tensor(x1[:, b, :].rearrange("p a d -> p (a d)"), PM[:, 0:128],
                                    x_sb[:, b, :].rearrange("p a d -> p (a d)"), ALU.add).then_inc(sm["x1_done"], 1)
                if near.there():
                    wait(dve, "e2_done", near.n(1))
                    wait(dve, "sel_done", near.n(-1))
                    V.tensor_scalar(m_ge[:, near.k % 2, :], e2[:, near.k % 2, :], ATT_EPS, 0.01, ALU.add,
                                    ALU.is_ge).then_inc(sm["ge_done"], 1)
                if low.there():
                    wait(dve, "nm1_done", low.n(1))
                    V.tensor_tensor(nmr[:, 0, :], nm[:, :], nmp[:, 0, :], ALU.subtract).then_inc(sm["nm2_done"], 1)
                if low.there():
                    wait(dve, "nm2_done", low.n(1))
                    V.tensor_copy(nmp[:, 1, :], nmr[:, 0, :]).then_inc(sm["nm3_done"], 1)
                    wait(dve, "nm3_done", low.n(1))
                    V.tensor_tensor(nmp[:, 2, :], nmr[:, 0, :], nmp[:, 1, :], ALU.subtract).then_inc(sm["nm_done"], 1)
                if far.there():
                    wait(dve, "ds_done", far.n(1))
                    wait(dve, "gt_done", far.n(1))
                    wait(dve, "da_done", far.n(1))
                    pass_waits(dve)
                    V.copy_predicated(dist[:, far.k % 4, :], m_gt[:, far.k % 2, :], da[:, far.k % 2, :]).then_inc(sm["dist_done"], 1)

            def front(c, k):
                n = NO[1, c]
                if k == 0:
                    if c == 0:
                        dve.wait_ge(sm["misc_in"], 160)
                        link(V.tensor_copy(wg[:, 0, :], wg_raw[:, 0, :]))
                        V.tensor_tensor(wg[:, 1, :], wg_raw[:, 1, :], wg_raw[:, 2, :], ALU.add).then_inc(sm["wg_done"], 1)
                    dve.wait_ge(sm["x1_done"], CB * (c + 1))
                    norm_stats(n, x1, c)
                if k == 1:
                    norm_rows(n, x1, c)
                if k == 3:
                    fr = slice(32, 36)
                    dve.wait_ge(sm["abs_done"], c + 1)
                    link(V.tensor_scalar(frow[fr, 1, :], P1[fr, 1, :], gb[fr, :], 0.0, ALU.add, ALU.min))
                    dve.wait_ge(sm["l1p_done"], c + 1)
                    link(V.tensor_tensor(lf[:, :], frow[fr, 1, :], frow[fr, 0, :], ALU.subtract))
                    for b in range(CB):
                        cols = slice(b * S, (b + 1) * S)
                        last = V.tensor_tensor_scan(cs[:, cols], col(K_1, slice(0, 4)).to_broadcast([4, S]), lf[:, cols], 0.0, ALU.mult, ALU.add)
                    link(last)
                    wait(dve, "rT_full", c)
                    dve.wait_ge(sm["xblk0"], 1)
                    link(V.scalar_tensor_tensor(arow[0:4, :], P1[0:4, 1, :], gb[0:4, :], cs[:, :], ALU.add, ALU.subtract))
                    for b in range(CB):
                        cols = slice(b * S, (b + 1) * S)
                        last = V.tensor_tensor_scan(runmax[c][:, cols], arow[0:4, cols], arow[0:4, cols], -3e38, ALU.max, ALU.max)
                    link(last)
                    V.tensor_tensor(arow[32:36, :], cs[:, :], runmax[c][:, :], ALU.add).then_inc(sm["a_done"], 1)

            def row(m):
                if m < B:
                    dve.wait_ge(sm["qk2_full"], m + 1)
                    dve.wait_ge(sm["dT_done"], m + 1)
                    wait(dve, "hh_full", m - 1)
                    V.scalar_tensor_tensor(cT[:, m % 2].rearrange("p h s -> p (h s)"), P2[:, m % 2, :], XD ** -0.5,
                                           dT[:, m % 2].rearrange("p h s -> p (h s)"), ALU.mult,
                                           ALU.mult).then_inc(sm["cT_done"], 1)
                if m > 0:
                    dve.wait_ge(sm["hh_full"], m)
                    V.tensor_copy(hs[:, (m - 1) % CB, :, :],
                                  cross_bank(m - 1)[:, 0:132].rearrange("p (h n) -> p h n", h=XH)).then_inc(sm["hs_done"], 1)

            def back(c, k):
                n = NO[2, c]
                full = [128, CB * XH, XD]
                if k == 0:
                    dve.wait_ge(sm["hs_done"], CB * (c + 1))
                    dve.wait_ge(sm["enm_done"], c + 1)
                    hall = hs[:, :, :, :].rearrange("p b h n -> p (b h) n")
                    enm_ = enm[:, c, :, :].rearrange("p b h -> p (b h)")
                    link(V.scalar_tensor_tensor(hden[:, 0, :], hall[:, :, XD], -1.0, enm_, ALU.mult, ALU.max))
                    link(V.tensor_tensor(hden[:, 0, :], hden[:, 0, :], hall[:, :, XD], ALU.max))
                    link(V.tensor_scalar(hden[:, 1, :], hden[:, 0, :], 1e-6, None, ALU.add))
                    link(V.reciprocal(hden[:, 2, :], hden[:, 1, :]))
                    link(V.tensor_tensor(hn[:, :, :], hall[:, :, 0:XD], hden[:, 2, :].unsqueeze(2).broadcast_to(full), ALU.mult))
                    link(V.tensor_reduce(hst[:, 0, :], hn[:, :, :], AX.X, ALU.add))
                    link(V.tensor_scalar(hst[:, 1, :], hst[:, 0, :], 1.0 / XD, None, ALU.mult))
                    V.tensor_tensor(hc[:, :, :], hn[:, :, :], hst[:, 1, :].unsqueeze(2).broadcast_to(full), ALU.subtract).then_inc(sm["hc_done"], 1)
                if k == 1:
                    dve.wait_ge(sm["hq_done"], c + 1)
                    link(V.tensor_reduce(hst[:, 5, :], hq[:, :, :], AX.X, ALU.add))
                    V.tensor_scalar(hst[:, 2, :], hst[:, 5, :], 1.0 / XD, None, ALU.mult).then_inc(sm["hvar_done"], 1)
                if k == 2:
                    dve.wait_ge(sm["hr_done"], c + 1)
                    refine(hst[:, 2, :], HEAD_EPS, hst[:, 4, :], hst[:, 6, :], hst[:, 7, :])
                    link(V.tensor_tensor(hn[:, :, :], hc[:, :, :], hst[:, 7, :].unsqueeze(2).broadcast_to(full), ALU.mult))
                    hb = hn[:, :, :].rearrange("p (b h) n -> p b (h n)", b=CB)
                    link(V.tensor_tensor(hb, hb, scale_row[:, :].unsqueeze(1).broadcast_to([128, CB, D]), ALU.mult))
                    link(V.tensor_tensor(chunk(x2, c), chunk(x1, c), hb, ALU.add))
                    norm_stats(n, x2, c)
                if k == 3:
                    norm_rows(n, x2, c)
                if k == 4:
                    dve.wait_ge(sm["xhi_done"], c + 1)
                    V.tensor_tensor(tok(xlo, c), tok(x3T, c), tok(xhi, c), ALU.subtract).then_inc(sm["xhl_done"], 1)
                if k == 5:
                    dve.wait_ge(sm["lg_full"], c + 1)
                    V.tensor_copy(lg[:, :, :], back_banks(c)[1][:, 0:CB * E].rearrange("p (b e) -> p b e", b=CB)).then_inc(sm["lg_done"], 1)
                    dve.wait_ge(sm["lg_done"], c + 1)
                    for b in range(CB):
                        last = V.max(top[:, b, :], lg[:, b, :])
                    link(last)
                    for b in range(CB):
                        V.max_index(topi[:, b, :], top[:, b, :], lg[:, b, :])
                    all_ = [128, CB, E]
                    link(V.tensor_tensor(rt[:, 1, :, :], lg[:, :, :], top[:, :, 0:1].broadcast_to(all_), ALU.subtract))
                    V.tensor_copy(rt[:, 0, :, 0:2], topi[:, :, 0:2]).then_inc(sm["re_done"], 1)
                    dve.wait_ge(sm["re_done"], c + 1)
                    iota = cf[:, C_IOTA:C_IOTA + CB * E].rearrange("p (b e) -> p b e", b=CB)
                    V.tensor_tensor(rt[:, 3, :, :], iota, rt[:, 0, :, 0:1].broadcast_to(all_), ALU.is_equal)
                    link(V.tensor_tensor(rt[:, 4, :, :], iota, rt[:, 0, :, 1:2].broadcast_to(all_), ALU.is_equal))
                    link(V.tensor_tensor(rt[:, 3, :, :], rt[:, 3, :, :], rt[:, 4, :, :], ALU.add))
                    dve.wait_ge(sm["rexp_done"], c + 1)
                    link(V.tensor_tensor(rt[:, 4, :, :], rt[:, 2, :, :], rt[:, 3, :, :], ALU.mult))
                    V.tensor_reduce(rsum[:, 0, :], rt[:, 2, :, :], AX.X, ALU.add)
                    link(V.tensor_reduce(rsum[:, 1, :], rt[:, 4, :, :], AX.X, ALU.add))
                    link(V.scalar_tensor_tensor(rsum[:, 2, :], rsum[:, 0, :], 1e-9, rsum[:, 1, :], ALU.mult, ALU.add))
                    link(V.reciprocal(rsum[:, 3, :], rsum[:, 2, :]))
                    V.tensor_tensor(chunk(wts, c), rt[:, 4, :, :], rsum[:, 3, :].unsqueeze(2).broadcast_to(all_), ALU.mult).then_inc(sm["wts_done"], 1)
                if k == 7:
                    dve.wait_ge(sm["bias_full"], c + 1)
                    V.tensor_tensor(chunk(acc, c), chunk(x2, c), back_banks(c)[1].rearrange("p (b d) -> p b d", b=CB),
                                    ALU.add).then_inc(sm["acc_done"], 1)

            def hidden(z, e, slot):
                for f in range(FC):
                    dve.wait_ge(sm["sil_done"], z * 2 + (f + 1))
                    if not isinstance(z, int) or z >= 2:
                        dve.wait_ge(sm["y_full"], z - 1)
                    V.scalar_tensor_tensor(hT[:, 2 * slot + f, :], (P1, P2)[f][:, 1, :],
                                           gub[:, 1, bass.ds(e * FC + f, 1)], sil[:, f, :], ALU.add,
                                           ALU.mult).then_inc(sm["h_done"], 1)

            def weigh(z, e, c, slot):
                dve.wait_ge(sm["y_full"], z + 1)
                if not isinstance(z, int) or z >= 1:
                    dve.wait_ge(sm["y_done"], z)
                P = (PO, PM)[slot]
                for b in range(CB):
                    t = c * CB + b
                    last = V.scalar_tensor_tensor(acc[:, t, :], P[:, b * D:(b + 1) * D], wts[:, t, bass.ds(e, 1)],
                                                  acc[:, t, :], ALU.mult, ALU.add)
                last.then_inc(sm["y_done"], 1)

            steps(dve, step, -1, NU + 4, 5, 12, front)
            cross_and_experts(front, row, back, lambda z: hidden(z, z, z % 2), lambda z: weigh(z, z, 0, z % 2))
            hidden(E, 0, 0)
            weigh(E - 1, E - 1, 0, 1)
            with dve.Fori(0, E // 2 - 1) as i:
                for j in range(2):
                    hidden(i * 2 + (E + 1 + j), i * 2 + (1 + j), (1 + j) % 2)
                    weigh(i * 2 + (E + j), i * 2 + j, 1, j)
            hidden(2 * E - 1, E - 1, 1)
            weigh(2 * E - 2, E - 2, 1, 0)
            weigh(2 * E - 1, E - 1, 1, 1)

        @block.tensor
        def _(pe):
            def mm(out_, lhsT, rhs, start=True, stop=True, **more):
                return nc.tensor.matmul(out_, lhsT, rhs, start=start, stop=stop, **more)

            def transpose_rows(n, P):
                pe.wait_ge(sm["xn_done"], CB * (n + 1))
                for b in range(CB):
                    last = mm(P[:, b * S:(b + 1) * S], xn[:, b, :], ident, is_transpose=True)
                last.then_inc(sm["tr_full"], 1)

            pe.wait_ge(sm["cf_in"], 16)
            pe.wait_ge(sm["wqkv_in"], 48)
            others = wv_sb[:, :].rearrange("p (m q n) -> p m q n", m=4, q=2)[:, :, 1, :]
            for c in range(NCH):
                if c == 0:
                    transpose_rows(NO[0, 0], PM)
                pe.wait_ge(sm["xT_done"], NO[0, c] + 1)
                for s, w in enumerate((wq_sb, wk_sb)):
                    wait(pe, "sq_done", 2 * c)
                    mm(P1[:, s, :], w[:, :], tok(xT, c)).then_inc(sm["qk_full"], 1)
                if c == 0:
                    transpose_rows(NO[0, 1], PM)
                wait(pe, "v_done", c)
                for b in range(CB):
                    mm(P3[:, 0, b * S:(b + 1) * S], tok(xT, c, b), wv_sb[:, :])
                for b in range(CB):
                    last = mm(P3[HALF:128, 1, b * 64:(b + 1) * 64], tok(xT, c, b)[:, 0:HALF], others)
                last.then_inc(sm["v_full"], 1)
                wait(pe, "wn_done", 2 * c)
                for s in range(2):
                    pe.wait_ge(sm["sq_done"], 2 * c + s + 1)
                    mm(P2[:, s, :], headblk, qk_sq[:, s, :]).then_inc(sm["nrm_full"], 1)

            def scores(u, P, right, done):
                k, bl = u.k % 4 // 2, u.k % 2
                keys = bl * S
                for g in range(4):
                    i, j = g // 2, g % 2
                    q = [sq_[k][:, (g * PB + bl) * 2 + m].rearrange("p h t -> p (h t)") for m in range(2)]
                    mm(P[:, i, j * S:(j + 1) * S], q[1], right[k][:, g, keys:keys + S])
                    last = mm(P[:, i, 2 * S + j * HALF:2 * S + (j + 1) * HALF], q[0], right[k][:, g, keys:keys + HALF])
                last.then_inc(sm[done], 1)

            def pair_count(u, each):
                m = (u.k // 4 + 1) * each
                return m if u.i is None else u.i * each + m

            def step(s):
                u = s + 1
                if u.there():
                    wait(pe, "sel_done", u.n())
                    wait(pe, "wn_done", 4)
                    k = u.k % 4 // 2
                    pe.wait_ge(stack_in[k], pair_count(u, 96))
                    pass_waits(pe)
                    scores(u, P2, sn_, "n1_full")
                u = s + 2
                if u.there():
                    wait(pe, "e2_done", u.n())
                    k = u.k % 4 // 2
                    pe.wait_ge(stack_in[k], pair_count(u, 96))
                    pass_waits(pe)
                    scores(u, P1, sk_, "d2_full")
                t = s - 5
                if t.ends_batch():
                    pe.wait_ge(sm["oT_done"], t.batch(1))
                    mm(PM[:, 0:128], oT[:, :], wo_sb[:, :]).then_inc(sm["wo_full"], 1)
                t = s - 3
                if t.there():
                    wait(pe, "pT_done", t.n(1))
                    k, bl = t.k % 4 // 2, t.k % 2
                    pe.wait_ge(sm[f"v{k}_in"], pair_count(t, 16))
                    v = t.k % 4
                    if v == 0:
                        o = t.batch()
                    elif v == 3:
                        o = t.batch()
                    else:
                        o = None
                    if o is not None:
                        wait(pe, "o_copied", o)
                    out_ = PO[:, bl * 144:(bl + 1) * 144]
                    for i in range(2):
                        for j in range(2):
                            for h in range(2):
                                head = 2 * (4 * k + 2 * i + j) + h
                                hl = 2 * (2 * i + j) + h
                                w = pT[:, t.k % 2, i * 384 + j * S + h * HALF:i * 384 + j * S + (h + 1) * HALF]
                                mm(out_[HALF:128, head * 9:head * 9 + 9], w, v_st[k][:, bl, hl * 9:hl * 9 + 9])
                        for h in range(2):
                            w = pT[:, t.k % 2, i * 384 + 2 * S + h * HALF:i * 384 + 2 * S + (h + 1) * HALF]
                            first = 2 * (4 * k + 2 * i) + h
                            dst = out_[0:HALF, first * 9:first * 9 + 36].rearrange("p (q n) -> p q n", n=18)[:, :, 0:9] \
                                if first * 9 + 36 <= 144 else None
                            if dst is None:
                                dst = out_[0:HALF, (first - 1) * 9:(first - 1) * 9 + 36].rearrange(
                                    "p (q n) -> p q n", n=18)[:, :, 9:18]
                            at = 72 + 36 * i + 18 * h
                            last = mm(dst, w, v_st[k][:, bl, at:at + 18].rearrange("p (q n) -> p q n", q=2))
                    last.then_inc(sm["pv_done"], 1)
                t = s - 2
                if t.there():
                    wait(pe, "nm_done", t.n(1))
                    wait(pe, "shift_done", t.n())
                    x_ = s - 5
                    if x_.ends_batch():
                        wait(pe, "x1_done", x_.batch(1))
                    mm(PM[0:24, 0:64].bitcast(bf16), nmp[:, :, :].rearrange("p a b -> p (a b)"), ident_b,
                       is_transpose=True).then_inc(sm["nmT_full"], 1)
                t = s - 2
                if t.there():
                    wait(pe, "shift_done", t.n(1))
                    wait(pe, "pT_done", t.n())
                    for i in range(2):
                        for q in range(3):
                            cols = slice(q * S, (q + 1) * S)
                            mm(P3[:, i, cols], dist[:, t.k % 4, i * 384 + q * S:i * 384 + (q + 1) * S], ident,
                               stop=False, is_transpose=True)
                            at = B_SEL + 4 * i + q
                            pick = cb[:, at:at + 1].to_broadcast([128, S]) if q < 2 \
                                else cb[:, B_SEL2 + i * S:B_SEL2 + (i + 1) * S]
                            last = mm(P3[:, i, cols], pick, shift[:, :], start=False)
                    last.then_inc(sm["t_full"], 1)
                t = s - 4
                if t.ends_batch():
                    pe.wait_ge(sm["o_done"], t.batch(1))
                    u2 = s - 2
                    if u2.there():
                        wait(pe, "shift_done", u2.n(1))
                    xd = s - 5
                    if t.k % 4 == 3:
                        pe.wait_ge(sm["x1_done"], t.batch())
                    mm(PM[:, 0:128], o_n[:, t.k % 2, :, :].rearrange("p h n -> p (h n)"), ident, is_transpose=True).then_inc(sm["oT_full"], 1)

            pe.wait_ge(sm["init_done"], 2)
            pe.wait_ge(sm["cb_in"], 16)
            pe.wait_ge(sm["misc_in"], 160)
            def front(c, k):
                if k == 1:
                    wait(pe, "e2_done", NU)
                    wait(pe, "aT_done", c)
                    transpose_rows(NO[1, c], P1[:, 0, :])
                if k == 2:
                    pe.wait_ge(sm["ctx_in"], 32)
                    pe.wait_ge(sm["wg_done"], 1)
                    pe.wait_ge(sm["xT_done"], NO[1, c] + 1)
                    wait(pe, "a_done", c)
                    mm(P1[0:36, 1, :], wg[:, 0, :], tok(xT, c), stop=False)
                    mm(P1[0:36, 1, :], wg[:, 1, :], tok(ctxT, c), start=False).then_inc(sm["g_full"], 1)
                if k == 4:
                    pe.wait_ge(sm["blk_done"], c + 1)
                    pe.wait_ge(sm["a_done"], c + 1)
                    for b in range(CB):
                        last = mm(P1[:, 0, b * 36:(b + 1) * 36], arow[:, b * S:(b + 1) * S], ident[0:36, 0:36], is_transpose=True)
                    last.then_inc(sm["rT_full"], 1)

            def row(m):
                c, b = m // CB, m % CB
                if m < B:
                    if m == 0:
                        pe.wait_ge(sm["pT_done"], NU)
                        pe.wait_ge(sm["sel_done"], NU)
                        pe.wait_ge(sm["par_a"], 1)
                        pe.wait_ge(sm["o_copied"], B)
                        pe.wait_ge(sm["x1_done"], B)
                    wait(pe, "dT_done", m - 1)
                    for h in range(XH):
                        mm(P3[:, m % 2, h * S:(h + 1) * S], ident_b, cb[:, B_MASK:B_MASK + S], stop=False)
                        pick = cf[:, C_NSEL + h:C_NSEL + h + 1].to_broadcast([128, S])
                        last = mm(P3[:, m % 2, h * S:(h + 1) * S], pick, runmax_all[c][:, b * S:(b + 1) * S],
                                  start=False)
                    last.then_inc(sm["ex_full"], 1)
                    wait(pe, "cT_done", m - 1)
                    mm(P2[:, m % 2, :], tok(ctxT, c, b), xblk[c][:, b].rearrange("p h s -> p (h s)")).then_inc(sm["qk2_full"], 1)
                if m > 0:
                    k = m - 1
                    if k == CB:
                        pe.wait_ge(sm["aT_done"], NCH)
                    pe.wait_ge(sm["cT_done"], k + 1)
                    wait(pe, "hs_done", k - 1)
                    for h in range(XH):
                        last = mm(cross_bank(k)[:, h * 33:(h + 1) * 33], cT[:, k % 2, h, :], ctx1[:, k, h, :])
                    last.then_inc(sm["hh_full"], 1)

            def back(c, k):
                T, U = back_banks(c)
                if k == 3:
                    pe.wait_ge(sm["hs_done"] if c == 0 else sm["dT_done"], CB if c == 0 else B)
                    transpose_rows(NO[2, c], T)
                if k == 4:
                    pe.wait_ge(sm["xT_done"], NO[2, c] + 1)
                    for b in range(CB):
                        last = mm(U[:, b * E:(b + 1) * E], tok(x3T, c, b), rw[:, :])
                    last.then_inc(sm["lg_full"], 1)
                if k == 6:
                    pe.wait_ge(sm["wts_done"], c + 1)
                    for b in range(CB):
                        last = mm(T[0:E, b * S:(b + 1) * S], wts[:, c * CB + b, :], ident, is_transpose=True)
                    last.then_inc(sm["wT_full"], 1)
                if k == 7:
                    pe.wait_ge(sm["lg_done"], c + 1)
                    pe.wait_ge(sm["wT_done"], c + 1)
                    for b in range(CB):
                        last = mm(U[:, b * D:(b + 1) * D], wtsT[:, b * S:(b + 1) * S], db[:, :])
                    last.then_inc(sm["bias_full"], 1)

            def gate_up(z, c, slot):
                pe.wait_ge(sm["w_ready"], z + 1)
                if isinstance(z, int) and z == 0:
                    pe.wait_ge(sm["exp_in"], 48)
                    pe.wait_ge(sm["hs_done"], B)
                if isinstance(z, int) and z == c * E:
                    pe.wait_ge(sm["xhl_done"], c + 1)
                for f in range(FC):
                    wait(pe, "h_done", z * 2 + (f - 1))
                    P = (P1, P2)[f]
                    for g in range(2):
                        cols = slice(f * 128, (f + 1) * 128)
                        mm(P[:, g, :], whi[:, slot, g, cols], tok(xhi, c), stop=False)
                        mm(P[:, g, :], whi[:, slot, g, cols], tok(xlo, c), start=False, stop=False)
                        last = mm(P[:, g, :], wlo[:, slot, g, cols], tok(xhi, c), start=False)
                    last.then_inc(sm["gu_full"], 1)

            def down(z, e, slot):
                pe.wait_ge(sm["h_done"], z * 2 + 2)
                if isinstance(z, int) and z == 0:
                    pe.wait_ge(sm["acc_done"], 1)
                if not isinstance(z, int) or z >= 2:
                    pe.wait_ge(sm["y_done"], z - 1)
                P = (PO, PM)[slot]
                for b in range(CB):
                    for f in range(FC):
                        last = mm(P[:, b * D:(b + 1) * D], hT[:, 2 * slot + f, b * S:(b + 1) * S],
                                  wd[:, bass.ds(e * FC + f, 1), :].rearrange("p a d -> p (a d)"),
                                  start=(f == 0), stop=(f == FC - 1))
                last.then_inc(sm["y_full"], 1)

            steps(pe, step, -2, NU + 4, 5, 12, front)
            cross_and_experts(front, row, back, lambda z: gate_up(z, 0, z % 2), lambda z: down(z, z, z % 2))
            gate_up(E, 1, 0)
            down(E - 1, E - 1, 1)
            with pe.Fori(0, E // 2 - 1) as i:
                for j in range(2):
                    gate_up(i * 2 + (E + 1 + j), 1, (1 + j) % 2)
                    down(i * 2 + (E + j), i * 2 + j, j)
            gate_up(2 * E - 1, 1, 1)
            down(2 * E - 2, E - 2, 0)
            down(2 * E - 1, E - 1, 1)


def kernel(**inputs):
    import concourse.bacc as bacc
    from concourse.bass_utils import run_bass_kernel_spmd as run

    a = {n: np.asarray(v) for n, v in inputs.items()}
    att = lambda n: np.ascontiguousarray(a["L0_attn_" + n].T)
    const_f, const_b = constants()
    by_unit = lambda t: np.ascontiguousarray(t.reshape(E, FC, 128).transpose(2, 0, 1).reshape(128, E * FC))
    arrays = {
        "x": a["x"], "ctx": a["ctx_1024"],
        "ctx_t": np.ascontiguousarray(a["ctx_1024"].transpose(2, 0, 1).reshape(D, NT)),
        "wq_t": np.ascontiguousarray(att("Wq")[:, head_rows()]), "wk_t": np.ascontiguousarray(att("Wk")[:, head_rows()]),
        "wv_t": att("Wv"), "wo_t": att("Wo"),
        "log_c": a["L0_attn_log_c"].reshape(1, 1), "log_beta": a["L0_attn_log_beta"].reshape(1, 1),
        "ig_k": a["L0_xattn_igate_kernel"], "ig_b": a["L0_xattn_igate_bias"].reshape(XH, 1),
        "fg_k": a["L0_xattn_fgate_kernel"], "fg_b": a["L0_xattn_fgate_bias"].reshape(XH, 1),
        "norm_scale": a["L0_xattn_outnorm_scale"].reshape(1, D),
        "router_t": np.ascontiguousarray(a["L0_ffn_router_w"].T),
        "gate_w": a["L0_ffn_gate_w"], "gate_b": by_unit(a["L0_ffn_gate_b"]),
        "up_w": a["L0_ffn_up_w"], "up_b": by_unit(a["L0_ffn_up_b"]),
        "down_w": a["L0_ffn_down_w"], "down_b": a["L0_ffn_down_b"],
        "const_f": const_f, "const_b": const_b, "stack_init": stack_rows(),
    }
    nc = bacc.Bacc("TRN2", target_bir_lowering=False, num_devices=1)
    args = [nc.dram_tensor(n, v.shape, mybir.dt.from_np(v.dtype), kind="ExternalInput").ap() for n, v in arrays.items()]
    out = nc.dram_tensor("out", (B, S, D), mybir.dt.float32, kind="ExternalOutput").ap()
    decoder_layer(nc, *args, out)
    r = run(nc, [arrays], core_ids=[0])
    return r.results[0]["out"]
```

```python
import numpy as np
import concourse.bass as bass
from concourse import mybir
from contextlib import ExitStack

B, S, D = 8, 128, 128
NT = B * S
H, DH = 16, 8
XH, XD = 4, 32
E, F, FC = 8, 256, 2
CB = 4
NCH = B // CB
CT = CB * S
PB = 2
NP = B // PB
PT_ = PB * S
ACT_AFTER = {2: (0,), 5: (6,), 6: (7,), 7: (8,)}
DVE_MID = {2: (1,), 3: (3,), 6: (7,), 9: (9,)}
DVE_AFTER = {0: (0,), 2: (2,), 3: (4, 5,), 5: (6,)}
PE_AFTER = {4: (5,), 5: (6,), 7: (8,), 8: (9,)}
ACT_TAIL = {13: [("front", 0, 0)], 15: [("front", 0, 2)], 16: [("front", 0, 3)], 19: [("front", 0, 4), ("rows", 0)]}
DVE_TAIL = {13: [("front", 0, 0)], 14: [("front", 0, 1)], 18: [("front", 0, 3)], 19: [("rows", 0)]}
PE_TAIL = {14: [("front", 0, 1)], 15: [("front", 0, 2)], 19: [("front", 0, 4), ("rows", 0)]}
HALF = S // 2
NU = 2 * B
UW = 768
SLOTS = 8
LN_EPS, ATT_EPS, HEAD_EPS = 1e-5, 1e-8, 1e-6
FAR = 1e30

C_ID = 0
C_BLK = 128
C_CM = 256
C_NSEL = 320
C_COL = C_NSEL + XH
(K_ONE, K_C, K_G1, K_G2, K_M3, K_M36, K_EPS, K_SEPS, K_R8, K_HALF, K_1, K_HEPS, K_EPSB) = range(13)
C_IOTA = C_COL + 16
C_TOT = C_IOTA + CB * E
B_ID = 0
B_SEL = 128
B_SEL2 = B_SEL + 8
B_MASK = B_SEL2 + 2 * S
B_SLOT = B_MASK + S
B_TOT = B_SLOT + 4

LN_SHIFT = float(np.exp(2 * (0.693 - 0.25)))


def constants():
    c = np.zeros((128, C_TOT), np.float32)
    p = np.arange(128)
    d = p // 4 % DH
    same = lambda f: f[:, None] == f[None, :]
    c[:, C_ID:C_ID + 128] = np.eye(128)
    c[:, C_BLK:C_BLK + 128] = same(p // 32) & same(p % 4)
    c[:, C_CM:C_CM + HALF] = np.where(np.arange(HALF)[None, :] > (p % HALF)[:, None], FAR, 0.0)
    for h in range(XH):
        c[h, C_NSEL + h] = -1.0
    col = c[:, C_COL:C_COL + 16]
    col[:, K_ONE] = d < 3
    col[:, K_C] = (d >= 3) & (d < 6)
    col[:, K_G1] = -1.0 * ((d < 6) & (d % 3 >= 1))
    col[:, K_G2] = -1.0 * ((d < 6) & (d % 3 == 2))
    col[:, K_M3] = d < 3
    col[:, K_M36] = (d >= 3) & (d < 6)
    col[:, K_EPS] = LN_EPS
    col[:, K_SEPS] = LN_SHIFT * ATT_EPS
    col[:, K_R8] = 8 ** -0.5
    col[:, K_HALF] = 0.5
    col[:, K_1] = 1.0
    col[:, K_HEPS] = HEAD_EPS
    c[:, C_IOTA:] = np.tile(np.arange(E), CB)[None, :]
    b = np.zeros((128, B_TOT), np.float32)
    b[:, B_ID:B_ID + 128] = np.eye(128)
    for part in range(3):
        b[8 * part:8 * part + 8, B_SEL:B_SEL + 8] = np.eye(8)
        for i in range(2):
            for j in range(2):
                at = B_SEL2 + i * S + j * HALF
                b[8 * part + 4 * i + 2 + j, at:at + HALF] = 1.0
    b[:, B_MASK:B_MASK + S] = np.where(p[:, None] > p[None, :], -FAR, 0.0)
    b[:, B_SLOT] = d < 6
    b[:, B_SLOT + 1] = d < 3
    return c, b.astype(mybir.dt.np(mybir.dt.bfloat16))


def head_rows():
    p = np.arange(128)
    return (8 * (p // 32 % 2) + 2 * (p % 4) + p // 64) * DH + p // 4 % DH


def stack_rows():
    r = np.zeros((128, 4, PT_), np.float32)
    row = np.arange(128)
    r[(row // DH % SLOTS == 6) & (row % DH >= 3) & (row % DH < 6)] = 1.0
    return r.astype(mybir.dt.np(mybir.dt.bfloat16))


def decoder_layer(nc, x, ctx, ctx_t, wq_t, wk_t, wv_t, wo_t, log_c, log_beta, ig_k, ig_b, fg_k, fg_b,
                  norm_scale, router_t, gate_w, gate_b, up_w, up_b, down_w, down_b,
                  const_f, const_b, stack_init, out):
    fp32, bf16, fp32r = mybir.dt.float32, mybir.dt.bfloat16, mybir.dt.float32r
    u8, u32 = mybir.dt.uint8, mybir.dt.uint32
    ALU, ACT, AX = mybir.AluOpType, mybir.ActivationFunctionType, mybir.AxisListType

    es = ExitStack()
    with es:
        def sb(name, shape, dt=fp32):
            return es.enter_context(nc.sbuf_tensor(name, shape, dt))

        def over(old, shape, dt=fp32, at=0):
            n = int(np.prod(shape[1:]))
            axes = " ".join("abcd"[:len(shape) - 1])
            flat = old[0:shape[0], at:at + n]
            flat = flat if dt == fp32 else flat.bitcast(dt)
            return flat.rearrange(f"p ({axes}) -> p {axes}", **dict(zip("abcd", shape[1:])))

        def sem(name):
            return es.enter_context(nc.semaphore(name))

        q_dram = nc.dram_tensor("q_split", [NP, 4, SLOTS, DH, 4, PT_], bf16, kind="Internal").ap()
        k_dram = nc.dram_tensor("k_split", [NP, SLOTS, 2, 2, DH, 4, PT_], bf16, kind="Internal").ap()
        n_dram = nc.dram_tensor("n_split", [NP, 2, 2, DH, 4, PT_], bf16, kind="Internal").ap()

        cf = sb("cf", [128, C_TOT])
        cb = sb("cb", [128, B_TOT], bf16)
        ident = cf[:, C_ID:C_ID + 128]
        ident_b = cb[:, B_ID:B_ID + 128]
        headblk = cf[:, C_BLK:C_BLK + 128]
        col = lambda k, p=slice(0, 128): cf[p, C_COL + k:C_COL + k + 1]
        x_sb = sb("x_sb", [128, B, D])
        x1 = x_sb
        x2 = x_sb
        wq_sb, wk_sb, wv_sb, wo_sb = (sb(n, [128, 128]) for n in ("wq_sb", "wk_sb", "wv_sb", "wo_sb"))
        par = sb("par", [128, 2])
        par_w = sb("par_w", [128, 4, 2])
        coef = sb("coef", [128, 1])
        eps_col = sb("eps_col", [128, 1])
        nbeta = sb("nbeta", [128, 1])
        ctx_sb = sb("ctx_sb", [128, B, D])
        acc = ctx_sb
        ctx1 = sb("ctx1", [128, B, XH, XD + 1])
        wg_raw = sb("wg_raw", [128, 3, 36])
        wg = sb("wg", [128, 2, 36])
        gb = sb("gb", [36, 1])
        scale_row = sb("scale_row", [128, D])
        rw = sb("rw", [128, E])
        wgu = sb("wgu", [128, E, 2, F])
        gub = sb("gub", [128, 2, E * FC])
        db = sb("db", [E, D])
        bst = sb("bst", [128, 2, CB, 6])
        mv = sb("mv", [128, 2, CB, 2])
        rs = sb("rs", [128, 2, 5, CB])
        xn = sb("xn", [128, CB, D])
        xT = sb("xT", [128, NT])
        proj_mem = sb("proj_mem", [128, 8 * CT])
        qkf = over(proj_mem, [128, 2, CT])
        qk_sq = over(proj_mem, [128, 2, CT], at=2 * CT)
        wn = over(proj_mem, [128, 2, CT], at=4 * CT)
        r1 = over(proj_mem, [128, 2, CT], at=6 * CT)
        w1_mem = sb("w1_mem", [128, 2 * CT])
        w1 = over(w1_mem, [128, 2, CT])
        wd = over(proj_mem, [128, E * FC, D])
        u0 = sb("u0", [128, 2, CT], bf16)
        u1 = sb("u1", [128, 2, CT], bf16)
        split_mem = sb("split_mem", [128, NCH * SLOTS * CT])
        split = [split_mem[:, n * SLOTS * CT:(n + 1) * SLOTS * CT].bitcast(bf16)
                 .rearrange("p (s n t) -> p s n t", s=2, n=SLOTS) for n in range(NCH)]
        ctxT = over(split_mem, [128, NT], at=2048)
        ksl = sb("ksl", [128, CT], bf16)
        nsl = sb("nsl", [128, NCH, CT], bf16)
        vab = sb("vab", [128, B, 2, 144])
        sk_, sn_ = ([sb(f"{n}{k}", [128, 4, PT_], bf16) for k in range(2)] for n in ("stk", "stn"))
        sq_ = [sb(f"stq{k}", [128, 8 * PB, 2, HALF], bf16) for k in range(2)]
        v_st = [sb(f"v_st{k}", [128, PB, 144]) for k in range(2)]
        dist_mem = sb("dist_mem", [128, 10 * UW])
        e2 = over(dist_mem, [128, 2, UW])
        l1 = over(dist_mem, [128, 2, UW], at=2 * UW)
        sqn = sb("sqn", [128, UW])
        wt = over(dist_mem, [128, 2, UW], at=4 * UW)
        da = over(dist_mem, [128, 2, UW], at=6 * UW)
        prod = over(dist_mem, [128, 2, UW], at=8 * UW)
        lp = sb("lp", [128, UW])
        m_ge = sb("m_ge", [128, 2, UW], u8)
        m_gt = sb("m_gt", [128, 2, UW], u8)
        dist = sb("dist", [128, 4, UW])
        nm = sb("nm", [128, 8])
        nmr = sb("nmr", [128, 2, 8])
        nmp = sb("nmp", [128, 3, 8], bf16)
        shift = sb("shift", [128, 128], bf16)
        pT = sb("pT", [128, 2, UW])
        o_sb = sb("o_sb", [128, H, DH + 1])
        o_rec = sb("o_rec", [128, H])
        o_n = sb("o_n", [128, PB, H, DH])
        oT = sb("oT", [128, 128])
        xblk = [over(split_mem, [128, CB, XH, S]), over(dist_mem, [128, CB, XH, S], at=4 * NT)]
        frow = over(split_mem, [36, 2, CT], at=3072)
        lf = over(proj_mem, [4, CT], at=4 * CT)
        cs = over(proj_mem, [4, CT], at=5 * CT)
        runmax_all = [over(w1_mem, [128, CT], at=c * CT) for c in range(NCH)]
        runmax = [t[0:4, :] for t in runmax_all]
        arow = over(proj_mem, [36, CT], at=7 * CT)
        aT = sb("aT", [128, NCH, CB, 36])
        enm = sb("enm", [128, NCH, CB, XH])
        dT = over(split_mem, [128, 2, XH, S], at=4096)
        cT = over(split_mem, [128, 2, XH, S], at=5120)
        hs = over(dist_mem, [128, CB, XH, XD + 1], at=6 * NT)
        hden = sb("hden", [128, 3, CB * XH])
        hn = over(split_mem, [128, CB * XH, XD], at=6144)
        hc = over(split_mem, [128, CB * XH, XD], at=6656)
        hq = over(split_mem, [128, CB * XH, XD], at=7168)
        hst = over(dist_mem, [128, 8, CB * XH], at=6 * NT + 640)
        lg = sb("lg", [128, CB, E])
        top = sb("top", [128, CB, 8])
        topi = sb("topi", [128, CB, 8], u32)
        rt = sb("rt", [128, 5, CB, E])
        rsum = sb("rsum", [128, 4, CB])
        wts = sb("wts", [128, B, E])
        wtsT = sb("wtsT", [E, CT])
        x3T = over(dist_mem, [128, NT])
        xhi = sb("xhi", [128, NT], fp32r)
        xlo = sb("xlo", [128, NT], fp32r)
        whi = sb("whi", [128, 2, 2, F], fp32r)
        wlo = sb("wlo", [128, 2, 2, F], fp32r)
        sil = over(dist_mem, [128, 2, CT], at=3 * NT)
        hT = over(dist_mem, [128, 4, CT], at=4 * NT)

        P1 = es.enter_context(nc.psum_tensor("P1", [128, 2, 512], fp32))
        P2 = es.enter_context(nc.psum_tensor("P2", [128, 2, 512], fp32))
        P3 = es.enter_context(nc.psum_tensor("P3", [128, 2, 512], fp32))
        PO = es.enter_context(nc.psum_tensor("PO", [128, 512], fp32))
        PM = es.enter_context(nc.psum_tensor("PM", [128, 512], fp32))

        names = ("cf_in par_in cb_in wqkv_in misc_in ctx_in exp_in stack0 v0_in v1_in out_done qsplit_done "
                 "q0_stored k0_stored n0_stored mv_done r0_done xn_done tr_full xT_done v_full nrm_full qkf_done "
                 "sq_done v_done wn_done split_b split_c split_done low_done par_a coef_done init_done chain_a "
                 "chain_d chain_p d2_full n1_full e2_done l1_done sqn_done wt_done lp_done ds_done pT_done "
                 "shift_done oT_done ge_done da_done sel_done prod_done dist_done nm_done o_copied o_done "
                 "x1_done gt_done causal_done nmT_full t_full pv_done oT_full wo_full g_full abs_done l1p_done "
                 "a_done rT_full aT_done enm_done ex_full dT_done cT_done hs_done hq_done hr_done lg_full "
                 "lg_done re_done rexp_done wts_done wT_full wT_done bias_full acc_done xhl_done w_ready "
                 "whi_done gu_full sil_done h_done y_full y_done qk_full par_ln o_rec_done nm0_done nm1_done "
                 "nm2_done nm3_done qk2_full hh_full hc_done hvar_done xhi_done wg_done xblk0 passed blk_done "
                 "zeroed").split()
        sm = {n: sem(n) for n in names}
        x_in = [sem(f"x_in{c}") for c in range(NCH)]
        stored = [sem(f"stored{p}") for p in range(NP)]
        stack_in = [sem(f"stack_in{k}") for k in range(2)]
        block = es.enter_context(nc.Block())

        class At:

            def __init__(self, i, k):
                self.i, self.k = i, k

            def __add__(self, d):
                return At(self.i, self.k + d)

            def __sub__(self, d):
                return At(self.i, self.k - d)

            def there(self):
                return self.i is not None or 0 <= self.k < NU

            def n(self, more=0):
                v = self.k + more
                if self.i is None:
                    return v if v > 0 else None
                assert v > 0, "a wait on a register stays above zero"
                return self.i * 4 + v

            def batch(self, more=0):
                v = 2 * (self.k // 4) + (self.k % 2) + more
                if self.i is None:
                    return v
                assert v > 0, "a wait on a register stays above zero"
                return self.i * 2 + v

            def ends_batch(self):
                return self.k % 4 >= 2 and self.there()

        def wait(eng, name, n):
            if n is None or (isinstance(n, int) and n <= 0):
                return
            eng.wait_ge(sm[name], n)

        def pass_waits(eng):
            eng.sem_inc(sm["passed"], 1)

        def steps(eng, step, first, last, lo, hi, after):
            for s in range(first, lo):
                step(At(None, s))
            with eng.Fori(0, (hi - lo + 1) // 4) as i:
                for j in range(4):
                    step(At(i, lo + j))
            for s in range(hi + 1, NU + 5):
                if s <= last:
                    step(At(None, s))
                after(s)

        def linker(eng, name):
            count = [0]

            def link(ins):
                count[0] += 1
                ins.then_inc(sm[name], 1)
                eng.wait_ge(sm[name], count[0])
            return link

        NO = {(k, c): 2 * k + c for k in range(3) for c in range(NCH)}

        def chunk(t, c):
            return t[:, c * CB:(c + 1) * CB, :]

        def tok(t, c, b=None):
            return t[:, c * CT:(c + 1) * CT] if b is None else t[:, c * CT + b * S:c * CT + (b + 1) * S]

        def wide(t, *shape):
            return t.broadcast_to(list(shape))

        def load_stack(sp, bp, k, first=False):
            n = bass.ds(bp, 1)
            half = [slice(j * HALF, (j + 1) * HALF) for j in range(2)]
            if first:
                sp.wait_ge(sm["q0_stored"], 64)
            for j in range(2):
                q = q_dram[n, 2 * j + k].rearrange("a s d g (m t) -> (a s d) (g m) t", t=HALF)
                sp.dma_start(sq_[k][half[j], :, j, :], q).then_inc(stack_in[k], 16)
            if first:
                sp.wait_ge(sm["k0_stored"], 16)
            for j in range(2):
                sp.dma_start(sk_[k][half[j], :, :], k_dram[n, :, j, k].rearrange("a s d g t -> (a s) d (g t)")).then_inc(stack_in[k], 16)
            if first:
                sp.wait_ge(sm["n0_stored"], 16)
            for j in range(2):
                last = slice(j * HALF + HALF - DH, (j + 1) * HALF)
                sp.dma_start(sn_[k][last, :, :], n_dram[n, j, k].rearrange("a d g t -> (a d) (g t)")).then_inc(stack_in[k], 16)

        def load_values(sp, bp, k):
            sp.dma_start(v_st[k][:, :, :], vab[:, bass.ds(bp * PB, PB), k, :]).then_inc(sm[f"v{k}_in"], 16)

        def front_banks(c):
            return (P1[:, 0, :], P1[:, 1, :]) if c == 0 else (P3[:, 0, :], P3[:, 1, :])

        def exp_bank(m):
            return (P1 if m < CB else P3)[:, m % 2, :]

        def cross_bank(m):
            return (PO, PM)[m % 2][:, :] if m < CB else P1[:, m % 2, :]

        def back_banks(c):
            return (PM[:, :], PO[:, :]) if c == 0 else (P3[:, 0, :], P3[:, 1, :])

        @block.sync
        def _(sp):
            xv = x.rearrange("b s d -> s b d")
            sp.dma_start(chunk(x_sb, 0), xv[:, 0:CB, :]).then_inc(x_in[0], 16)
            sp.dma_start(cf[:, :], const_f).then_inc(sm["cf_in"], 16)
            sp.dma_start(wq_sb[:, :], wq_t).then_inc(sm["wqkv_in"], 16)
            sp.dma_start(wk_sb[:, :], wk_t).then_inc(sm["wqkv_in"], 16)
            sp.dma_start(wv_sb[:, :], wv_t).then_inc(sm["wqkv_in"], 16)
            sp.dma_start(par[:, 0:1], log_c.to_broadcast([128, 1])).then_inc(sm["par_in"], 16)
            sp.dma_start(par[:, 1:2], log_beta.to_broadcast([128, 1])).then_inc(sm["par_in"], 16)
            sp.dma_start(cb[:, :], const_b).then_inc(sm["cb_in"], 16)
            sp.dma_start(chunk(x_sb, 1), xv[:, CB:B, :]).then_inc(x_in[1], 16)
            for k in range(2):
                sp.dma_start(sn_[k][:, :, :], stack_init).then_inc(sm["stack0"], 16)
            sp.dma_start(wo_sb[:, :], wo_t).then_inc(sm["misc_in"], 16)
            sp.dma_start(rw[:, :], router_t).then_inc(sm["misc_in"], 16)
            sp.dma_start(db[:, :], down_b).then_inc(sm["misc_in"], 16)
            sp.dma_start(gub[:, 0, :], gate_b).then_inc(sm["misc_in"], 16)
            sp.dma_start(gub[:, 1, :], up_b).then_inc(sm["misc_in"], 16)
            sp.dma_start(gb[0:4, :], ig_b).then_inc(sm["misc_in"], 16)
            sp.dma_start(gb[32:36, :], fg_b).then_inc(sm["misc_in"], 16)
            sp.dma_start(scale_row[:, :], norm_scale.to_broadcast([128, D])).then_inc(sm["misc_in"], 16)
            sp.wait_ge(sm["init_done"], 1)
            sp.dma_start(wg_raw[:, :, 0:4], ig_k.rearrange("(t p) h -> p t h", p=128)).then_inc(sm["misc_in"], 16)
            sp.dma_start(wg_raw[:, :, 32:36], fg_k.rearrange("(t p) h -> p t h", p=128)).then_inc(sm["misc_in"], 16)
            sp.wait_ge(sm["stack0"], 32)
            def store_q(n, done):
                sp.wait_ge(sm["qsplit_done"], n // 2 + 1)
                sp.wait_ge(sm["low_done"], n // 2 * 2 + 2)
                cols = slice(n % 2 * PT_, (n % 2 + 1) * PT_)
                for jk in range(4):
                    rows = slice(jk * 32, (jk + 1) * 32)
                    sp.dma_start(q_dram[n, jk].rearrange("s d g t -> (d g) s t"),
                                 split[n // 2][rows, 0, :, cols]).then_inc(done, 16)

            def store_kn(n, k_done, n_done):
                sp.wait_ge(sm["split_done"], n // 2 + 1)
                cols = slice(n % 2 * PT_, (n % 2 + 1) * PT_)
                sp.dma_start(k_dram[n].rearrange("s j k d g t -> (j k d g) s t"),
                             split[n // 2][:, 1, :, cols]).then_inc(k_done, 16)
                sp.dma_start(n_dram[n].rearrange("j k d g t -> (j k d g) t"), nsl[:, n // 2, cols]).then_inc(n_done, 16)

            def next_stack(bp, k):
                sp.wait_ge(sm["d2_full"], bp * 4 + (2 * k - 2))
                sp.wait_ge(sm["n1_full"], bp * 4 + (2 * k - 2))
                load_stack(sp, bp, k)

            def next_values(bp, k):
                sp.wait_ge(sm["pv_done"], bp * 4 + (2 * k - 2))
                load_values(sp, bp, k)

            store_q(0, sm["q0_stored"])
            store_kn(0, sm["k0_stored"], sm["n0_stored"])
            sp.wait_ge(sm["zeroed"], 1)
            for k in range(2):
                load_stack(sp, 0, k, first=True)
            store_q(1, stored[1])
            store_kn(1, stored[1], stored[1])
            sp.wait_ge(sm["v_done"], 1)
            for k in range(2):
                load_values(sp, 0, k)
            sp.wait_ge(stored[1], 96)
            next_stack(1, 0)
            for n in range(2, NP):
                store_q(n, stored[n])
                store_kn(n, stored[n], stored[n])
            next_stack(1, 1)
            for n in range(2, NP):
                sp.wait_ge(stored[n], 96)
            sp.wait_ge(sm["v_done"], 2)
            sp.dma_start(ctx_sb[:, :, :], ctx.rearrange("b s d -> s b d")).then_inc(sm["ctx_in"], 16)
            sp.dma_start(ctxT[:, :], ctx_t).then_inc(sm["ctx_in"], 16)
            sp.dma_start(wgu[:, :, 0, :], gate_w.rearrange("e d f -> d e f")).then_inc(sm["exp_in"], 16)
            sp.dma_start(wgu[:, :, 1, :], up_w.rearrange("e d f -> d e f")).then_inc(sm["exp_in"], 16)
            sp.dma_start(wd[:, :, :], down_w.rearrange("e (c f) d -> f (e c) d", c=FC)).then_inc(sm["exp_in"], 16)

            with sp.Fori(2, NP) as bp:
                for k in range(2):
                    next_stack(bp, k)
                    next_values(bp - 1, k)
            for k in range(2):
                next_values(NP - 1, k)
            for c in range(NCH):
                sp.wait_ge(sm["y_done"], E * (c + 1))
                sp.dma_start(out.rearrange("b s d -> s b d")[:, c * CB:(c + 1) * CB, :],
                             chunk(acc, c)).then_inc(sm["out_done"], 16)
            sp.wait_ge(sm["out_done"], 16 * NCH)

        @block.gpsimd
        def _(pool):
            link = linker(pool, "chain_p")
            pool.memset(eps_col[:, :], LN_EPS)
            pool.memset(wg_raw[:, :, :], 0.0).then_inc(sm["init_done"], 1)
            link(pool.memset(vab[:, :, :, :], 0.0))
            for k in range(2):
                va = vab[:, :, k, 0:72].rearrange("p b (h n) -> p b h n", n=DH + 1)
                link(pool.memset(va[:, :, :, DH], 1.0))
                vb = vab[:, :, k, 72:144].rearrange("p b (i q n) -> p b i q n", i=4, q=2)
                link(pool.memset(vb[0:HALF, :, :, 0, DH], 1.0))
                link(pool.memset(vb[HALF:128, :, :, 1, DH], 1.0))
            pool.memset(shift[:, :], 0.0)
            pool.memset(ctx1[:, :, :, XD], 1.0).then_inc(sm["init_done"], 1)
            pool.wait_ge(sm["cb_in"], 16)
            for c in range(NCH):
                pool.tensor_copy(split[c][:, 0, 7, :], cb[:, B_SLOT:B_SLOT + 1].to_broadcast([128, CT]))
                pool.tensor_copy(split[c][:, 1, 6, :], cb[:, B_SLOT + 1:B_SLOT + 2].to_broadcast([128, CT]))
            for c in range(NCH):
                for s in range(2):
                    pool.wait_ge(sm["split_c"], 2 * c + s + 1)
                    first_mid, low = ((3, 5), (2, 0))[s]
                    pool.tensor_tensor(split[c][:, s, low, :], r1[:, s, :], split[c][:, s, first_mid, :],
                                       ALU.subtract).then_inc(sm["low_done"], 1)
            pool.wait_ge(sm["cf_in"], 16)

            def step(s):
                g = s - 1
                if g.there():
                    wait(pool, "dist_done", g.n(1))
                    for i in range(2):
                        row = dist[:, g.k % 4, i * 384:(i + 1) * 384]
                        wideq = row[:, 0:256].rearrange("p (j n) -> p j n", j=2)[:, :, HALF:128]
                        near = row[:, 256:384].rearrange("p (j n) -> p j n", j=2)
                        cm = cf[:, C_CM:C_CM + HALF].unsqueeze(1).broadcast_to([128, 2, HALF])
                        pool.tensor_tensor(wideq, wideq, cm, ALU.add)
                        last = pool.tensor_tensor(near, near, cm, ALU.add)
                    last.then_inc(sm["causal_done"], 1)
                g = s + 1
                if g.there():
                    wait(pool, "e2_done", g.n(1))
                    wait(pool, "dist_done", g.n(-1))
                    pass_waits(pool)
                    pool.tensor_scalar(m_gt[:, g.k % 2, :], e2[:, g.k % 2, :], 4.0 - ATT_EPS, None,
                                       ALU.is_gt).then_inc(sm["gt_done"], 1)

            def zeros(s):
                if s == 5:
                    for n in range(NP):
                        if n == 0:
                            pool.wait_ge(sm["q0_stored"], 64)
                            pool.wait_ge(sm["k0_stored"], 16)
                            pool.wait_ge(sm["n0_stored"], 16)
                        else:
                            pool.wait_ge(stored[n], 96)
                    pool.memset(arow[:, :], 0.0)
                    pool.memset(w1_mem[:, :], 0.0)
                    pool.memset(xblk[0][:, :, :, :], 0.0).then_inc(sm["xblk0"], 1)

            for s in range(-1, 7):
                step(At(None, s))
                zeros(s)
            with pool.Fori(0, 2) as i:
                for j in range(4):
                    step(At(i, 7 + j))
            for s in range(15, NU + 1):
                step(At(None, s))
            pool.memset(xblk[1][:, :, :, :], 0.0).then_inc(sm["xblk0"], 1)
            pool.wait_ge(sm["ctx_in"], 32)
            pool.tensor_copy(ctx1[:, :, :, 0:XD], ctx_sb[:, :, :].rearrange("p b (h d) -> p b h d", h=XH)).then_inc(sm["par_a"], 1)

            pool.wait_ge(sm["exp_in"], 48)

            def prepare(z, e, slot):
                w = wgu[:, bass.ds(e, 1), :, :].rearrange("p a g f -> p (a g f)")
                hi = whi[:, slot].rearrange("p g f -> p (g f)")
                lo = wlo[:, slot].rearrange("p g f -> p (g f)")
                if not isinstance(z, int) or z >= 2:
                    pool.wait_ge(sm["gu_full"], z * 2 - 2)
                pool.tensor_copy(hi, w).then_inc(sm["whi_done"], 1)
                pool.wait_ge(sm["whi_done"], z + 1)
                pass_waits(pool)
                pool.tensor_tensor(lo, w, hi, ALU.subtract).then_inc(sm["w_ready"], 1)

            prepare(0, 0, 0)
            prepare(1, 1, 1)
            with pool.Fori(1, E // 2) as i:
                for j in range(2):
                    prepare(i * 2 + j, i * 2 + j, j)
            with pool.Fori(0, E // 2) as i:
                for j in range(2):
                    prepare(i * 2 + (E + j), i * 2 + j, j)

        @block.scalar
        def _(act):
            link = linker(act, "chain_a")
            A = act.activation
            act.preload_act_table_set("natural_log_exp_and_others")
            def parameters():
                act.wait_ge(sm["cf_in"], 16)
                act.wait_ge(sm["par_in"], 32)
                link(A(par_w[:, 0, :], par[:, :], ACT.Abs))
                link(A(par_w[:, 1, :], par_w[:, 0, :], ACT.Exp, scale=-1.0))
                A(par_w[:, 2, :], par_w[:, 1, :], ACT.Ln, bias=col(K_1)).then_inc(sm["par_ln"], 1)

            def rstd_start(n, var, eps, done, before, store):
                act.wait_ge(sm[before], n)
                link(A(store[0], var, ACT.Ln, bias=eps))
                A(store[1], store[0], ACT.Exp, scale=-0.5).then_inc(sm[done], 1)

            def norm_rstd(n):
                wait(act, "xn_done", CB * (n - 1))
                rstd_start(CB * (n + 1), mv[:, n % 2, :, 1], eps_col[:, :], "r0_done", "mv_done",
                           (rs[:, n % 2, 0, :], rs[:, n % 2, 1, :]))

            def evacuate_xT(n, src, dst):
                act.wait_ge(sm["tr_full"], n + 1)
                A(dst, src, ACT.Copy).then_inc(sm["xT_done"], 1)

            act.wait_ge(sm["init_done"], 1)
            norm_rstd(NO[0, 0])
            parameters()
            evacuate_xT(NO[0, 0], PM[:, :], tok(xT, 0))
            norm_rstd(NO[0, 1])
            for c in range(NCH):
                wait(act, "split_b", 2 * c)
                wait(act, "nrm_full", 2 * c)
                for s in range(2):
                    act.wait_ge(sm["qk_full"], 2 * c + s + 1)
                    sign = 1.0 if s == 0 else -2.0
                    A(split[c][:, s, 0:3, :] if s == 0 else split[c][:, s, 1:6:2, :],
                      P1[:, s, :].unsqueeze(1).broadcast_to([128, 3, CT]), ACT.Copy, scale=sign)
                    A(qkf[:, s, :], P1[:, s, :], ACT.Copy, scale=sign).then_inc(sm["qkf_done"], 1)
                    A(qk_sq[:, s, :], P1[:, s, :], ACT.Square).then_inc(sm["sq_done"], 1)
                if c == 0:
                    evacuate_xT(NO[0, 1], PM[:, :], tok(xT, 1))
                act.wait_ge(sm["coef_done"], 1)
                wait(act, "split_done", c)
                for s in range(2):
                    act.wait_ge(sm["nrm_full"], 2 * c + s + 1)
                    bias = {} if s == 0 else {"bias": col(K_C)}
                    A(u0[:, s, :], P2[:, s, :], ACT.Identity, scale=coef[:, :], **bias)
                    A(wn[:, s, :], P2[:, s, :], ACT.Identity, scale=coef[:, :], **bias).then_inc(sm["wn_done"], 1)
                act.wait_ge(sm["v_full"], c + 1)
                act.wait_ge(sm["init_done"], 2)
                for k in range(2):
                    va = vab[:, c * CB:(c + 1) * CB, k, 0:72].rearrange("p b (h n) -> p b h n", n=DH + 1)
                    A(va[:, :, :, 0:DH], P3[:, 0, :].rearrange("p (b k h n) -> p b k h n", b=CB, k=2, h=8)[:, :, k, :, :],
                      ACT.Copy)
                    for i in range(2):
                        vb = vab[:, c * CB:(c + 1) * CB, k, 72 + 36 * i:108 + 36 * i].rearrange(
                            "p b (j q n) -> p b j q n", j=2, q=2)
                        lo = P3[0:HALF, 0, :].rearrange("p (b m q j n) -> p b m q j n", b=CB, m=4, q=2, j=2)
                        hi = P3[HALF:128, 1, 0:256].rearrange("p (b m j n) -> p b m j n", b=CB, m=4, j=2)
                        A(vb[0:HALF, :, :, 0, 0:DH], lo[:, :, 2 * k + i, 0, :, :], ACT.Copy)
                        last = A(vb[HALF:128, :, :, 1, 0:DH], hi[:, :, 2 * k + i, :, :], ACT.Copy)
                last.then_inc(sm["v_done"], 1)

            def step(s):
                u, t = s + 1, s - 3
                p = u.k % 2
                ps1, ps2 = (P[:, :, 0:384] for P in (P1, P2))
                def row(t, w=None):
                    r = t[:, :] if w is None else t[:, w, :]
                    return r.rearrange("p (i n) -> p i n", i=2)
                if u.there():
                    wait(act, "d2_full", u.n(1))
                    for w in ("l1_done", "ge_done", "prod_done", "gt_done"):
                        wait(act, w, u.n(-1))
                    A(row(e2, p), ps1, ACT.Relu).then_inc(sm["e2_done"], 1)
                if u.there():
                    wait(act, "e2_done", u.n(1))
                    wait(act, "da_done", u.n(-1))
                    A(l1[:, p, :], e2[:, p, :], ACT.Ln, scale=LN_SHIFT, bias=col(K_SEPS)).then_inc(sm["l1_done"], 1)
                if t.there():
                    wait(act, "t_full", t.n(1))
                    wait(act, "pv_done", t.n(-1))
                    A(row(pT, t.k % 2), P3[:, :, 0:384], ACT.Exp, scale=nbeta[:, :]).then_inc(sm["pT_done"], 1)
                x = s - 5
                if x.ends_batch():
                    act.wait_ge(sm["oT_full"], x.batch(1))
                    A(oT[:, :], PM[:, 0:128], ACT.Copy).then_inc(sm["oT_done"], 1)
                if u.there():
                    wait(act, "n1_full", u.n(1))
                    wait(act, "wt_done", u.n())
                    A(row(sqn), ps2, ACT.Square, scale=col(K_R8), bias=col(K_R8)).then_inc(sm["sqn_done"], 1)
                if s.there():
                    wait(act, "prod_done", s.n(1))
                    wait(act, "ds_done", s.n())
                    A(lp[:, :], prod[:, s.k % 2, :], ACT.Ln, scale=16.0).then_inc(sm["lp_done"], 1)
                if u.there():
                    wait(act, "sqn_done", u.n(1))
                    wait(act, "prod_done", u.n(-1))
                    A(wt[:, p, :], sqn[:, :], ACT.Square, bias=col(K_HALF)).then_inc(sm["wt_done"], 1)
                t = s - 2
                if t.there():
                    wait(act, "nmT_full", t.n(1))
                    wait(act, "t_full", t.n())
                    A(shift[0:24, :], PM[0:24, 0:64].bitcast(bf16), ACT.Copy).then_inc(sm["shift_done"], 1)
                if s.there():
                    wait(act, "lp_done", s.n(1))
                    wait(act, "t_full", s.n(-3))
                    A(dist[:, s.k % 4, :], lp[:, :], ACT.Exp, scale=0.5).then_inc(sm["ds_done"], 1)

            def front(c, k):
                n = NO[1, c]
                if k == 0:
                    norm_rstd(n)
                if k == 2:
                    act.wait_ge(sm["tr_full"], n + 1)
                    A(tok(xT, c), front_banks(c)[0], ACT.Copy).then_inc(sm["xT_done"], 1)
                if k == (2 if c == 0 else 5):
                    act.wait_ge(sm["xblk0"], c + 1)
                    for h in range(XH):
                        r = slice(h * XD, (h + 1) * XD)
                        last = A(xblk[c][r, :, h, :], front_banks(c)[0][r, :].rearrange("p (b s) -> p b s", b=CB), ACT.Copy)
                    last.then_inc(sm["blk_done"], 1)
                if k == 3:
                    act.wait_ge(sm["g_full"], c + 1)
                    fr = slice(32, 36)
                    wait(act, "a_done", c)
                    A(frow[fr, 0, :], front_banks(c)[1][fr, :], ACT.Abs, bias=gb[fr, :]).then_inc(sm["abs_done"], 1)
                    act.wait_ge(sm["abs_done"], c + 1)
                    link(A(frow[fr, 0, :], frow[fr, 0, :], ACT.Exp, scale=-1.0))
                    A(frow[fr, 0, :], frow[fr, 0, :], ACT.Ln, bias=col(K_1, fr)).then_inc(sm["l1p_done"], 1)
                if k == 4:
                    act.wait_ge(sm["rT_full"], c + 1)
                    A(aT[:, c, :, :], front_banks(c)[0][:, 0:144].rearrange("p (b n) -> p b n", b=CB), ACT.Copy).then_inc(sm["aT_done"], 1)
                    act.wait_ge(sm["aT_done"], c + 1)
                    A(enm[:, c, :, :], aT[:, c, :, 32:36], ACT.Exp, scale=-1.0).then_inc(sm["enm_done"], 1)

            def rows(m):
                act.wait_ge(sm["ex_full"], m + 1)
                wait(act, "cT_done", m - 1)
                for h in range(XH):
                    last = A(dT[:, m % 2, h, :], exp_bank(m)[:, h * S:(h + 1) * S], ACT.Exp,
                             bias=aT[:, m // CB, m % CB, h:h + 1])
                last.then_inc(sm["dT_done"], 1)

            def back(c, k):
                n = NO[2, c]
                if k == 0:
                    act.wait_ge(sm["hc_done"], c + 1)
                    A(hq[:, :, :], hc[:, :, :], ACT.Square).then_inc(sm["hq_done"], 1)
                if k == 1:
                    rstd_start(c + 1, hst[:, 2, :], col(K_HEPS), "hr_done", "hvar_done", (hst[:, 3, :], hst[:, 4, :]))
                if k == 2:
                    norm_rstd(n)
                if k == 6:
                    evacuate_xT(n, back_banks(c)[0], tok(x3T, c))
                    act.wait_ge(sm["xT_done"], n + 1)
                    A(tok(xhi, c), tok(x3T, c), ACT.Copy).then_inc(sm["xhi_done"], 1)
                if k == 7:
                    act.wait_ge(sm["re_done"], c + 1)
                    A(rt[:, 2, :, :], rt[:, 1, :, :], ACT.Exp).then_inc(sm["rexp_done"], 1)
                if k == 8:
                    act.wait_ge(sm["wT_full"], c + 1)
                    wait(act, "bias_full", c)
                    A(wtsT[:, :], back_banks(c)[0][0:E, :], ACT.Copy).then_inc(sm["wT_done"], 1)

            def silu(z, e):
                for f in range(FC):
                    n = z * 2 + (f + 1)
                    act.wait_ge(sm["gu_full"], n)
                    wait(act, "h_done", n - 2)
                    P = (P1, P2)[f]
                    pass_waits(act)
                    A(sil[:, f, :], P[:, 0, :], ACT.Silu,
                      bias=gub[:, 0, bass.ds(e * FC + f, 1)]).then_inc(sm["sil_done"], 1)

            def after(s):
                stages = dict(front=front, rows=rows, back=back)
                for stage, *which in ACT_TAIL.get(s, ()):
                    stages[stage](*which)

            steps(act, step, -1, NU + 4, 5, 12, after)
            rows(1)
            front(1, 0)
            rows(2)
            rows(3)
            front(1, 2)
            front(1, 3)
            front(1, 5)
            back(0, 0)
            back(0, 1)
            front(1, 4)
            rows(4)
            rows(5)
            back(0, 2)
            rows(6)
            rows(7)
            back(0, 6)
            back(0, 7)
            for z in range(E + 2):
                silu(z, z % E)
                if z == 0:
                    back(0, 8)
                for k in ACT_AFTER.get(z, ()):
                    back(1, k)
            with act.Fori(2, E) as e:
                silu(e + E, e)

        @block.vector
        def _(dve):
            link = linker(dve, "chain_d")
            V = dve
            V.memset(sq_[0][:, :, :, :], 0.0)
            V.memset(sq_[1][:, :, :, :], 0.0).then_inc(sm["zeroed"], 1)

            def parameters():
                dve.wait_ge(sm["par_in"], 32)
                dve.wait_ge(sm["cf_in"], 16)
                link(V.tensor_scalar(par_w[:, 3, :], par[:, :], 0.0, None, ALU.max))
                dve.wait_ge(sm["par_ln"], 1)
                link(V.tensor_tensor(par_w[:, 3, :], par_w[:, 3, :], par_w[:, 2, :], ALU.add))
                V.tensor_scalar(nbeta[:, :], par_w[:, 3, 1:2], 0.5, -0.25, ALU.add, ALU.mult)
                V.scalar_tensor_tensor(coef[:, :], par_w[:, 3, 0:1], col(K_C), col(K_ONE), ALU.mult,
                                       ALU.add).then_inc(sm["coef_done"], 1)

            def refine(var, eps, r0, t, r):
                link(V.tensor_tensor(t, r0, r0, ALU.mult))
                link(V.scalar_tensor_tensor(t, var, eps, t, ALU.add, ALU.mult))
                link(V.tensor_scalar(t, t, -0.5, 1.5, ALU.mult, ALU.add))
                link(V.tensor_tensor(r, r0, t, ALU.mult))

            def inverse_root(var, eps, t, half, r):
                i32 = mybir.dt.int32
                link(V.tensor_scalar(t, var, eps, None, ALU.add))
                V.tensor_scalar(half, var, eps, -0.5, ALU.add, ALU.mult)
                link(V.tensor_scalar(r.bitcast(i32), t.bitcast(i32), 1, None, ALU.logical_shift_right))
                link(V.tensor_scalar(r.bitcast(i32), r.bitcast(i32), -1, 0x5F3759DF, ALU.mult, ALU.add))
                for _ in range(3):
                    link(V.tensor_tensor(t, r, r, ALU.mult))
                    link(V.tensor_tensor(t, t, half, ALU.mult))
                    link(V.scalar_tensor_tensor(r, t, 1.5, r, ALU.add, ALU.mult))

            def norm_stats(n, src, c):
                p = n % 2
                for b in range(CB):
                    last = V.bn_stats(bst[:, p, b, :], src[:, c * CB + b, :])
                link(last)
                for b in range(CB):
                    V.bn_aggr(mv[:, p, b, :], bst[:, p, b, :]).then_inc(sm["mv_done"], 1)

            def norm_rows(n, src, c):
                p = n % 2
                if n != NO[2, 1]:
                    dve.wait_ge(sm["r0_done"], n + 1)
                    refine(mv[:, p, :, 1], LN_EPS, rs[:, p, 1, :], rs[:, p, 2, :], rs[:, p, 4, :])
                wait(dve, "tr_full", n)
                for b in range(CB):
                    V.tensor_scalar(xn[:, b, :], src[:, c * CB + b, :], mv[:, p, b, 0:1], rs[:, p, 4, b:b + 1],
                                    ALU.subtract, ALU.mult).then_inc(sm["xn_done"], 1)

            for c in range(NCH):
                dve.wait_ge(x_in[c], 16)
                norm_stats(NO[0, c], x_sb, c)
                norm_rows(NO[0, c], x_sb, c)
                if c == 0:
                    parameters()
            for c in range(NCH):
                for s in range(2):
                    sp_ = split[c][:, s]
                    first = sp_[:, s, :]
                    mid = sp_[:, 3:5, :] if s == 0 else sp_[:, 2:5:2, :]
                    dve.wait_ge(sm["qkf_done"], 2 * c + s + 1)
                    wait(dve, "low_done", 2 * c)
                    V.tensor_tensor(r1[:, s, :], qkf[:, s, :], first, ALU.subtract).then_inc(sm["split_b"], 1)
                    dve.wait_ge(sm["split_b"], 2 * c + s + 1)
                    V.tensor_copy(mid, r1[:, s, :].unsqueeze(1).broadcast_to([128, 2, CT])).then_inc(sm["split_c"], 1)
                for s in range(2):
                    dve.wait_ge(sm["wn_done"], 2 * c + s + 1)
                    link(V.scalar_tensor_tensor(w1[:, s, :], u0[:, s, :], col(K_G1), wn[:, s, :], ALU.mult, ALU.add))
                    link(V.tensor_copy(u1[:, s, :], w1[:, s, :]))
                    dst = split[c][:, 0, 6, :] if s == 0 else ksl[:, :]
                    last = V.scalar_tensor_tensor(dst, u1[:, s, :], col(K_G2), w1[:, s, :], ALU.mult, ALU.add)
                    if s == 0:
                        last.then_inc(sm["qsplit_done"], 1)
                    else:
                        link(last)
                V.tensor_scalar(split[c][:, 1, 7, :], ksl[:, :], col(K_M3), None, ALU.mult)
                V.tensor_scalar(nsl[:, c, :], ksl[:, :], col(K_M36), None, ALU.mult).then_inc(sm["split_done"], 1)

            def step(s):
                def row(t, w):
                    return t[:, w, :].rearrange("p (i n) -> p i n", i=2)
                n1 = P2[:, :, 0:384]
                low, far, near = s - 2, s - 1, s + 1
                t = s - 4
                if t.ends_batch():
                    wait(dve, "pv_done", t.n(1))
                    bl = t.k % 2
                    if bl:
                        wait(dve, "o_done", t.batch())
                    o = PO[:, bl * 144:(bl + 1) * 144].rearrange("p (h n) -> p h n", n=DH + 1)
                    V.tensor_copy(o_sb[:, :, :], o).then_inc(sm["o_copied"], 1)
                if s.there():
                    p = s.k % 2
                    wait(dve, "l1_done", s.n(1))
                    wait(dve, "sqn_done", s.n(1))
                    wait(dve, "dist_done", s.n(-1))
                    V.scalar_tensor_tensor(row(da, p), row(l1, p), 2.0, n1, ALU.mult, ALU.add).then_inc(sm["da_done"], 1)
                    wait(dve, "ge_done", s.n(1))
                    wait(dve, "wt_done", s.n(1))
                    pass_waits(dve)
                    V.copy_predicated(row(wt, p), row(m_ge, p), n1).then_inc(sm["sel_done"], 1)
                if t.ends_batch():
                    dve.wait_ge(sm["o_copied"], t.batch(1))
                    V.reciprocal(o_rec[:, :], o_sb[:, :, DH]).then_inc(sm["o_rec_done"], 1)
                if low.there():
                    wait(dve, "causal_done", low.n(1))
                    d = row(dist, low.k % 4)
                    m = nm[:, :].rearrange("p (i q) -> p i q", i=2)
                    V.tensor_reduce(m[:, :, 0:2], d[:, :, 0:256].rearrange("p i (j n) -> p i j n", j=2), AX.X, ALU.min,
                                    negate=True)
                    V.tensor_reduce(m[:, :, 2:4], d[:, :, 256:384].rearrange("p i (j n) -> p i j n", j=2), AX.X, ALU.min,
                                    negate=True).then_inc(sm["nm0_done"], 1)
                if s.there():
                    wait(dve, "sel_done", s.n(1))
                    wait(dve, "lp_done", s.n(-1))
                    V.scalar_tensor_tensor(prod[:, p, :], e2[:, p, :], ATT_EPS, wt[:, p, :], ALU.add,
                                           ALU.mult).then_inc(sm["prod_done"], 1)
                if t.ends_batch():
                    dve.wait_ge(sm["o_rec_done"], t.batch(1))
                    V.tensor_tensor(o_n[:, bl, :, :], o_sb[:, :, 0:DH],
                                    o_rec[:, :].unsqueeze(2).broadcast_to([128, H, DH]), ALU.mult).then_inc(sm["o_done"], 1)
                if low.there():
                    wait(dve, "nm0_done", low.n(1))
                    wait(dve, "nmT_full", low.n())
                    V.tensor_copy(nmp[:, 0, :], nm[:, :]).then_inc(sm["nm1_done"], 1)
                t = s - 5
                if t.ends_batch():
                    dve.wait_ge(sm["wo_full"], t.batch(1))
                    b = bass.ds(t.batch(1) - 1, 1)
                    V.tensor_tensor(x1[:, b, :].rearrange("p a d -> p (a d)"), PM[:, 0:128],
                                    x_sb[:, b, :].rearrange("p a d -> p (a d)"), ALU.add).then_inc(sm["x1_done"], 1)
                if near.there():
                    wait(dve, "e2_done", near.n(1))
                    wait(dve, "sel_done", near.n(-1))
                    V.tensor_scalar(m_ge[:, near.k % 2, :], e2[:, near.k % 2, :], ATT_EPS, 0.01, ALU.add,
                                    ALU.is_ge).then_inc(sm["ge_done"], 1)
                if low.there():
                    wait(dve, "nm1_done", low.n(1))
                    V.tensor_tensor(nmr[:, 0, :], nm[:, :], nmp[:, 0, :], ALU.subtract).then_inc(sm["nm2_done"], 1)
                if low.there():
                    wait(dve, "nm2_done", low.n(1))
                    V.tensor_copy(nmp[:, 1, :], nmr[:, 0, :]).then_inc(sm["nm3_done"], 1)
                    wait(dve, "nm3_done", low.n(1))
                    V.tensor_tensor(nmp[:, 2, :], nmr[:, 0, :], nmp[:, 1, :], ALU.subtract).then_inc(sm["nm_done"], 1)
                if far.there():
                    wait(dve, "ds_done", far.n(1))
                    wait(dve, "gt_done", far.n(1))
                    wait(dve, "da_done", far.n(1))
                    pass_waits(dve)
                    V.copy_predicated(dist[:, far.k % 4, :], m_gt[:, far.k % 2, :], da[:, far.k % 2, :]).then_inc(sm["dist_done"], 1)

            def front(c, k):
                n = NO[1, c]
                if k == 0:
                    if c == 0:
                        dve.wait_ge(sm["misc_in"], 160)
                        link(V.tensor_copy(wg[:, 0, :], wg_raw[:, 0, :]))
                        V.tensor_tensor(wg[:, 1, :], wg_raw[:, 1, :], wg_raw[:, 2, :], ALU.add).then_inc(sm["wg_done"], 1)
                    dve.wait_ge(sm["x1_done"], CB * (c + 1))
                    norm_stats(n, x1, c)
                if k == 1:
                    norm_rows(n, x1, c)
                if k == 3:
                    fr = slice(32, 36)
                    dve.wait_ge(sm["abs_done"], c + 1)
                    link(V.tensor_scalar(frow[fr, 1, :], front_banks(c)[1][fr, :], gb[fr, :], 0.0, ALU.add, ALU.min))
                    dve.wait_ge(sm["l1p_done"], c + 1)
                    link(V.tensor_tensor(lf[:, :], frow[fr, 1, :], frow[fr, 0, :], ALU.subtract))
                    for b in range(CB):
                        cols = slice(b * S, (b + 1) * S)
                        last = V.tensor_tensor_scan(cs[:, cols], col(K_1, slice(0, 4)).to_broadcast([4, S]), lf[:, cols], 0.0, ALU.mult, ALU.add)
                    link(last)
                if k == (3 if c == 0 else 5):
                    wait(dve, "rT_full", c)
                    dve.wait_ge(sm["xblk0"], 1)
                    link(V.scalar_tensor_tensor(arow[0:4, :], front_banks(c)[1][0:4, :], gb[0:4, :], cs[:, :], ALU.add, ALU.subtract))
                    for b in range(CB):
                        cols = slice(b * S, (b + 1) * S)
                        last = V.tensor_tensor_scan(runmax[c][:, cols], arow[0:4, cols], arow[0:4, cols], -3e38, ALU.max, ALU.max)
                    link(last)
                    V.tensor_tensor(arow[32:36, :], cs[:, :], runmax[c][:, :], ALU.add).then_inc(sm["a_done"], 1)

            def rows(m):
                dve.wait_ge(sm["qk2_full"], m + 1)
                dve.wait_ge(sm["dT_done"], m + 1)
                wait(dve, "hh_full", m - 1)
                V.scalar_tensor_tensor(cT[:, m % 2].rearrange("p h s -> p (h s)"), P2[:, m % 2, :], XD ** -0.5,
                                       dT[:, m % 2].rearrange("p h s -> p (h s)"), ALU.mult,
                                       ALU.mult).then_inc(sm["cT_done"], 1)

            def outs(m):
                dve.wait_ge(sm["hh_full"], m + 1)
                V.tensor_copy(hs[:, m % CB, :, :],
                              cross_bank(m)[:, 0:132].rearrange("p (h n) -> p h n", h=XH)).then_inc(sm["hs_done"], 1)

            def back(c, k):
                n = NO[2, c]
                full = [128, CB * XH, XD]
                if k == 0:
                    dve.wait_ge(sm["hs_done"], CB * (c + 1))
                    dve.wait_ge(sm["enm_done"], c + 1)
                    hall = hs[:, :, :, :].rearrange("p b h n -> p (b h) n")
                    enm_ = enm[:, c, :, :].rearrange("p b h -> p (b h)")
                    link(V.scalar_tensor_tensor(hden[:, 0, :], hall[:, :, XD], -1.0, enm_, ALU.mult, ALU.max))
                    link(V.tensor_tensor(hden[:, 0, :], hden[:, 0, :], hall[:, :, XD], ALU.max))
                    link(V.tensor_scalar(hden[:, 1, :], hden[:, 0, :], 1e-6, None, ALU.add))
                    link(V.reciprocal(hden[:, 2, :], hden[:, 1, :]))
                    link(V.tensor_tensor(hn[:, :, :], hall[:, :, 0:XD], hden[:, 2, :].unsqueeze(2).broadcast_to(full), ALU.mult))
                    link(V.tensor_reduce(hst[:, 0, :], hn[:, :, :], AX.X, ALU.add))
                    link(V.tensor_scalar(hst[:, 1, :], hst[:, 0, :], 1.0 / XD, None, ALU.mult))
                    V.tensor_tensor(hc[:, :, :], hn[:, :, :], hst[:, 1, :].unsqueeze(2).broadcast_to(full), ALU.subtract).then_inc(sm["hc_done"], 1)
                if k == 1:
                    dve.wait_ge(sm["hq_done"], c + 1)
                    link(V.tensor_reduce(hst[:, 5, :], hq[:, :, :], AX.X, ALU.add))
                    V.tensor_scalar(hst[:, 2, :], hst[:, 5, :], 1.0 / XD, None, ALU.mult).then_inc(sm["hvar_done"], 1)
                if k == 2:
                    if c == 0:
                        dve.wait_ge(sm["hr_done"], c + 1)
                        refine(hst[:, 2, :], HEAD_EPS, hst[:, 4, :], hst[:, 6, :], hst[:, 7, :])
                    else:
                        dve.wait_ge(sm["hvar_done"], c + 1)
                        inverse_root(hst[:, 2, :], HEAD_EPS, hst[:, 6, :], hst[:, 3, :], hst[:, 7, :])
                    link(V.tensor_tensor(hn[:, :, :], hc[:, :, :], hst[:, 7, :].unsqueeze(2).broadcast_to(full), ALU.mult))
                    hb = hn[:, :, :].rearrange("p (b h) n -> p b (h n)", b=CB)
                    link(V.tensor_tensor(hb, hb, scale_row[:, :].unsqueeze(1).broadcast_to([128, CB, D]), ALU.mult))
                    link(V.tensor_tensor(chunk(x2, c), chunk(x1, c), hb, ALU.add))
                if k == 3:
                    norm_stats(n, x2, c)
                if k == 4:
                    dve.wait_ge(sm["mv_done"], CB * (n + 1))
                    inverse_root(mv[:, n % 2, :, 1], LN_EPS, rs[:, n % 2, 2, :], rs[:, n % 2, 0, :], rs[:, n % 2, 4, :])
                if k == 5:
                    norm_rows(n, x2, c)
                if k == 6:
                    dve.wait_ge(sm["xhi_done"], c + 1)
                    V.tensor_tensor(tok(xlo, c), tok(x3T, c), tok(xhi, c), ALU.subtract).then_inc(sm["xhl_done"], 1)
                if k == 7:
                    dve.wait_ge(sm["lg_full"], c + 1)
                    V.tensor_copy(lg[:, :, :], back_banks(c)[1][:, 0:CB * E].rearrange("p (b e) -> p b e", b=CB)).then_inc(sm["lg_done"], 1)
                    dve.wait_ge(sm["lg_done"], c + 1)
                    for b in range(CB):
                        last = V.max(top[:, b, :], lg[:, b, :])
                    link(last)
                    for b in range(CB):
                        V.max_index(topi[:, b, :], top[:, b, :], lg[:, b, :])
                    all_ = [128, CB, E]
                    link(V.tensor_tensor(rt[:, 1, :, :], lg[:, :, :], top[:, :, 0:1].broadcast_to(all_), ALU.subtract))
                    V.tensor_copy(rt[:, 0, :, 0:2], topi[:, :, 0:2]).then_inc(sm["re_done"], 1)
                    dve.wait_ge(sm["re_done"], c + 1)
                    iota = cf[:, C_IOTA:C_IOTA + CB * E].rearrange("p (b e) -> p b e", b=CB)
                    V.tensor_tensor(rt[:, 3, :, :], iota, rt[:, 0, :, 0:1].broadcast_to(all_), ALU.is_equal)
                    link(V.tensor_tensor(rt[:, 4, :, :], iota, rt[:, 0, :, 1:2].broadcast_to(all_), ALU.is_equal))
                    link(V.tensor_tensor(rt[:, 3, :, :], rt[:, 3, :, :], rt[:, 4, :, :], ALU.add))
                    dve.wait_ge(sm["rexp_done"], c + 1)
                    link(V.tensor_tensor(rt[:, 4, :, :], rt[:, 2, :, :], rt[:, 3, :, :], ALU.mult))
                    V.tensor_reduce(rsum[:, 0, :], rt[:, 2, :, :], AX.X, ALU.add)
                    link(V.tensor_reduce(rsum[:, 1, :], rt[:, 4, :, :], AX.X, ALU.add))
                    link(V.scalar_tensor_tensor(rsum[:, 2, :], rsum[:, 0, :], 1e-9, rsum[:, 1, :], ALU.mult, ALU.add))
                    link(V.reciprocal(rsum[:, 3, :], rsum[:, 2, :]))
                    V.tensor_tensor(chunk(wts, c), rt[:, 4, :, :], rsum[:, 3, :].unsqueeze(2).broadcast_to(all_), ALU.mult).then_inc(sm["wts_done"], 1)
                if k == 9:
                    dve.wait_ge(sm["bias_full"], c + 1)
                    V.tensor_tensor(chunk(acc, c), chunk(x2, c), back_banks(c)[1].rearrange("p (b d) -> p b d", b=CB),
                                    ALU.add).then_inc(sm["acc_done"], 1)

            def hidden(z, e, slot):
                for f in range(FC):
                    dve.wait_ge(sm["sil_done"], z * 2 + (f + 1))
                    if not isinstance(z, int) or z >= 2:
                        dve.wait_ge(sm["y_full"], z - 1)
                    V.scalar_tensor_tensor(hT[:, 2 * slot + f, :], (P1, P2)[f][:, 1, :],
                                           gub[:, 1, bass.ds(e * FC + f, 1)], sil[:, f, :], ALU.add,
                                           ALU.mult).then_inc(sm["h_done"], 1)

            def weigh(z, e, c, slot):
                dve.wait_ge(sm["y_full"], z + 1)
                if not isinstance(z, int) or z >= 1:
                    dve.wait_ge(sm["y_done"], z)
                if isinstance(z, int) and z == c * E:
                    dve.wait_ge(sm["acc_done"], c + 1)
                P = (PO, PM)[slot]
                for b in range(CB):
                    t = c * CB + b
                    last = V.scalar_tensor_tensor(acc[:, t, :], P[:, b * D:(b + 1) * D], wts[:, t, bass.ds(e, 1)],
                                                  acc[:, t, :], ALU.mult, ALU.add)
                last.then_inc(sm["y_done"], 1)

            def after(s):
                stages = dict(front=front, rows=rows, outs=outs, back=back)
                for stage, *which in DVE_TAIL.get(s, ()):
                    stages[stage](*which)

            steps(dve, step, -1, NU + 4, 5, 12, after)
            rows(1)
            front(1, 0)
            front(1, 1)
            outs(0)
            rows(2)
            outs(1)
            outs(2)
            rows(3)
            outs(3)
            back(0, 0)
            front(1, 3)
            back(0, 1)
            front(1, 5)
            rows(4)
            back(0, 2)
            rows(5)
            back(0, 3)
            outs(4)
            back(0, 5)
            rows(6)
            outs(5)
            rows(7)
            outs(6)
            back(0, 6)
            outs(7)
            back(0, 7)
            for z in range(E + 2):
                hidden(z, z % E, z % 2)
                for k in DVE_MID.get(z, ()):
                    back(1, k)
                if z == 0:
                    back(0, 9)
                else:
                    weigh(z - 1, (z - 1) % E, (z - 1) // E, (z - 1) % 2)
                for k in DVE_AFTER.get(z, ()):
                    back(1, k)
            with dve.Fori(0, (E - 2) // 2) as i:
                for j in range(2):
                    hidden(i * 2 + (E + 2 + j), i * 2 + (2 + j), j)
                    weigh(i * 2 + (E + 1 + j), i * 2 + (1 + j), 1, (1 + j) % 2)
            weigh(2 * E - 1, E - 1, 1, 1)

        @block.tensor
        def _(pe):
            def mm(out_, lhsT, rhs, start=True, stop=True, **more):
                return nc.tensor.matmul(out_, lhsT, rhs, start=start, stop=stop, **more)

            def transpose_rows(n, P):
                pe.wait_ge(sm["xn_done"], CB * (n + 1))
                for b in range(CB):
                    last = mm(P[:, b * S:(b + 1) * S], xn[:, b, :], ident, is_transpose=True)
                last.then_inc(sm["tr_full"], 1)

            pe.wait_ge(sm["cf_in"], 16)
            pe.wait_ge(sm["wqkv_in"], 48)
            others = wv_sb[:, :].rearrange("p (m q n) -> p m q n", m=4, q=2)[:, :, 1, :]
            for c in range(NCH):
                if c == 0:
                    transpose_rows(NO[0, 0], PM)
                pe.wait_ge(sm["xT_done"], NO[0, c] + 1)
                for s, w in enumerate((wq_sb, wk_sb)):
                    wait(pe, "sq_done", 2 * c)
                    mm(P1[:, s, :], w[:, :], tok(xT, c)).then_inc(sm["qk_full"], 1)
                if c == 0:
                    transpose_rows(NO[0, 1], PM)
                wait(pe, "v_done", c)
                for b in range(CB):
                    mm(P3[:, 0, b * S:(b + 1) * S], tok(xT, c, b), wv_sb[:, :])
                for b in range(CB):
                    last = mm(P3[HALF:128, 1, b * 64:(b + 1) * 64], tok(xT, c, b)[:, 0:HALF], others)
                last.then_inc(sm["v_full"], 1)
                wait(pe, "wn_done", 2 * c)
                for s in range(2):
                    pe.wait_ge(sm["sq_done"], 2 * c + s + 1)
                    mm(P2[:, s, :], headblk, qk_sq[:, s, :]).then_inc(sm["nrm_full"], 1)

            def scores(u, P, right, done):
                k, bl = u.k % 4 // 2, u.k % 2
                keys = bl * S
                for g in range(4):
                    i, j = g // 2, g % 2
                    q = [sq_[k][:, (g * PB + bl) * 2 + m].rearrange("p h t -> p (h t)") for m in range(2)]
                    mm(P[:, i, j * S:(j + 1) * S], q[1], right[k][:, g, keys:keys + S])
                    last = mm(P[:, i, 2 * S + j * HALF:2 * S + (j + 1) * HALF], q[0], right[k][:, g, keys:keys + HALF])
                last.then_inc(sm[done], 1)

            def pair_count(u, each):
                m = (u.k // 4 + 1) * each
                return m if u.i is None else u.i * each + m

            def step(s):
                u = s + 1
                if u.there():
                    wait(pe, "sel_done", u.n())
                    wait(pe, "wn_done", 4)
                    k = u.k % 4 // 2
                    pe.wait_ge(stack_in[k], pair_count(u, 96))
                    pass_waits(pe)
                    scores(u, P2, sn_, "n1_full")
                u = s + 2
                if u.there():
                    wait(pe, "e2_done", u.n())
                    k = u.k % 4 // 2
                    pe.wait_ge(stack_in[k], pair_count(u, 96))
                    pass_waits(pe)
                    scores(u, P1, sk_, "d2_full")
                t = s - 5
                if t.ends_batch():
                    pe.wait_ge(sm["oT_done"], t.batch(1))
                    mm(PM[:, 0:128], oT[:, :], wo_sb[:, :]).then_inc(sm["wo_full"], 1)
                t = s - 3
                if t.there():
                    wait(pe, "pT_done", t.n(1))
                    k, bl = t.k % 4 // 2, t.k % 2
                    pe.wait_ge(sm[f"v{k}_in"], pair_count(t, 16))
                    v = t.k % 4
                    if v == 0:
                        o = t.batch()
                    elif v == 3:
                        o = t.batch()
                    else:
                        o = None
                    if o is not None:
                        wait(pe, "o_copied", o)
                    out_ = PO[:, bl * 144:(bl + 1) * 144]
                    for i in range(2):
                        for j in range(2):
                            for h in range(2):
                                head = 2 * (4 * k + 2 * i + j) + h
                                hl = 2 * (2 * i + j) + h
                                w = pT[:, t.k % 2, i * 384 + j * S + h * HALF:i * 384 + j * S + (h + 1) * HALF]
                                mm(out_[HALF:128, head * 9:head * 9 + 9], w, v_st[k][:, bl, hl * 9:hl * 9 + 9])
                        for h in range(2):
                            w = pT[:, t.k % 2, i * 384 + 2 * S + h * HALF:i * 384 + 2 * S + (h + 1) * HALF]
                            first = 2 * (4 * k + 2 * i) + h
                            dst = out_[0:HALF, first * 9:first * 9 + 36].rearrange("p (q n) -> p q n", n=18)[:, :, 0:9] \
                                if first * 9 + 36 <= 144 else None
                            if dst is None:
                                dst = out_[0:HALF, (first - 1) * 9:(first - 1) * 9 + 36].rearrange(
                                    "p (q n) -> p q n", n=18)[:, :, 9:18]
                            at = 72 + 36 * i + 18 * h
                            last = mm(dst, w, v_st[k][:, bl, at:at + 18].rearrange("p (q n) -> p q n", q=2))
                    last.then_inc(sm["pv_done"], 1)
                t = s - 2
                if t.there():
                    wait(pe, "nm_done", t.n(1))
                    wait(pe, "shift_done", t.n())
                    x_ = s - 5
                    if x_.ends_batch():
                        wait(pe, "x1_done", x_.batch(1))
                    mm(PM[0:24, 0:64].bitcast(bf16), nmp[:, :, :].rearrange("p a b -> p (a b)"), ident_b,
                       is_transpose=True).then_inc(sm["nmT_full"], 1)
                t = s - 2
                if t.there():
                    wait(pe, "shift_done", t.n(1))
                    wait(pe, "pT_done", t.n())
                    for i in range(2):
                        for q in range(3):
                            cols = slice(q * S, (q + 1) * S)
                            mm(P3[:, i, cols], dist[:, t.k % 4, i * 384 + q * S:i * 384 + (q + 1) * S], ident,
                               stop=False, is_transpose=True)
                            at = B_SEL + 4 * i + q
                            pick = cb[:, at:at + 1].to_broadcast([128, S]) if q < 2 \
                                else cb[:, B_SEL2 + i * S:B_SEL2 + (i + 1) * S]
                            last = mm(P3[:, i, cols], pick, shift[:, :], start=False)
                    last.then_inc(sm["t_full"], 1)
                t = s - 4
                if t.ends_batch():
                    pe.wait_ge(sm["o_done"], t.batch(1))
                    u2 = s - 2
                    if u2.there():
                        wait(pe, "shift_done", u2.n(1))
                    if t.k % 4 == 3:
                        pe.wait_ge(sm["x1_done"], t.batch())
                    mm(PM[:, 0:128], o_n[:, t.k % 2, :, :].rearrange("p h n -> p (h n)"), ident, is_transpose=True).then_inc(sm["oT_full"], 1)

            pe.wait_ge(sm["init_done"], 2)
            pe.wait_ge(sm["cb_in"], 16)
            pe.wait_ge(sm["misc_in"], 160)
            def front(c, k):
                if k == 1:
                    pe.wait_ge(sm["e2_done"] if c == 0 else sm["pT_done"], NU)
                    transpose_rows(NO[1, c], front_banks(c)[0])
                if k == 2:
                    pe.wait_ge(sm["ctx_in"], 32)
                    pe.wait_ge(sm["wg_done"], 1)
                    pe.wait_ge(sm["xT_done"], NO[1, c] + 1)
                    G = front_banks(c)[1]
                    mm(G[0:36, :], wg[:, 0, :], tok(xT, c), stop=False)
                    mm(G[0:36, :], wg[:, 1, :], tok(ctxT, c), start=False).then_inc(sm["g_full"], 1)
                if k == 4:
                    pe.wait_ge(sm["blk_done"], c + 1)
                    pe.wait_ge(sm["a_done"], c + 1)
                    for b in range(CB):
                        last = mm(front_banks(c)[0][:, b * 36:(b + 1) * 36], arow[:, b * S:(b + 1) * S], ident[0:36, 0:36], is_transpose=True)
                    last.then_inc(sm["rT_full"], 1)

            def rows(m):
                c, b = m // CB, m % CB
                if b == 0:
                    pe.wait_ge(sm["aT_done"], c + 1)
                    pe.wait_ge(sm["sel_done"], NU)
                if m % CB >= 2:
                    pe.wait_ge(sm["dT_done"], m - 1)
                for h in range(XH):
                    mm(exp_bank(m)[:, h * S:(h + 1) * S], ident_b, cb[:, B_MASK:B_MASK + S], stop=False)
                    pick = cf[:, C_NSEL + h:C_NSEL + h + 1].to_broadcast([128, S])
                    last = mm(exp_bank(m)[:, h * S:(h + 1) * S], pick, runmax_all[c][:, b * S:(b + 1) * S],
                              start=False)
                last.then_inc(sm["ex_full"], 1)
                wait(pe, "cT_done", m - 1)
                mm(P2[:, m % 2, :], tok(ctxT, c, b), xblk[c][:, b].rearrange("p h s -> p (h s)")).then_inc(sm["qk2_full"], 1)

            def outs(m):
                if m == 0:
                    pe.wait_ge(sm["par_a"], 1)
                    pe.wait_ge(sm["o_copied"], B)
                    pe.wait_ge(sm["x1_done"], B)
                if m == CB:
                    pe.wait_ge(sm["dT_done"], CB)
                pe.wait_ge(sm["cT_done"], m + 1)
                if m % CB >= 2:
                    pe.wait_ge(sm["hs_done"], m - 1)
                for h in range(XH):
                    last = mm(cross_bank(m)[:, h * 33:(h + 1) * 33], cT[:, m % 2, h, :], ctx1[:, m, h, :])
                last.then_inc(sm["hh_full"], 1)

            def back(c, k):
                T, U = back_banks(c)
                if k == 5:
                    pe.wait_ge(sm["hs_done"] if c == 0 else sm["dT_done"], CB if c == 0 else B)
                    transpose_rows(NO[2, c], T)
                if k == 6:
                    pe.wait_ge(sm["xT_done"], NO[2, c] + 1)
                    for b in range(CB):
                        last = mm(U[:, b * E:(b + 1) * E], tok(x3T, c, b), rw[:, :])
                    last.then_inc(sm["lg_full"], 1)
                if k == 8:
                    pe.wait_ge(sm["wts_done"], c + 1)
                    for b in range(CB):
                        last = mm(T[0:E, b * S:(b + 1) * S], wts[:, c * CB + b, :], ident, is_transpose=True)
                    last.then_inc(sm["wT_full"], 1)
                if k == 9:
                    pe.wait_ge(sm["lg_done"], c + 1)
                    pe.wait_ge(sm["wT_done"], c + 1)
                    for b in range(CB):
                        last = mm(U[:, b * D:(b + 1) * D], wtsT[:, b * S:(b + 1) * S], db[:, :])
                    last.then_inc(sm["bias_full"], 1)

            def gate_up(z, c, slot):
                pe.wait_ge(sm["w_ready"], z + 1)
                if isinstance(z, int) and z == 0:
                    pe.wait_ge(sm["exp_in"], 48)
                    pe.wait_ge(sm["hs_done"], B)
                if isinstance(z, int) and z == c * E:
                    pe.wait_ge(sm["xhl_done"], c + 1)
                for f in range(FC):
                    wait(pe, "h_done", z * 2 + (f - 1))
                    P = (P1, P2)[f]
                    for g in range(2):
                        cols = slice(f * 128, (f + 1) * 128)
                        mm(P[:, g, :], whi[:, slot, g, cols], tok(xhi, c), stop=False)
                        mm(P[:, g, :], whi[:, slot, g, cols], tok(xlo, c), start=False, stop=False)
                        last = mm(P[:, g, :], wlo[:, slot, g, cols], tok(xhi, c), start=False)
                    last.then_inc(sm["gu_full"], 1)

            def down(z, e, slot):
                pe.wait_ge(sm["h_done"], z * 2 + 2)
                if isinstance(z, int) and z == 0:
                    pe.wait_ge(sm["acc_done"], 1)
                if not isinstance(z, int) or z >= 2:
                    pe.wait_ge(sm["y_done"], z - 1)
                P = (PO, PM)[slot]
                for b in range(CB):
                    for f in range(FC):
                        last = mm(P[:, b * D:(b + 1) * D], hT[:, 2 * slot + f, b * S:(b + 1) * S],
                                  wd[:, bass.ds(e * FC + f, 1), :].rearrange("p a d -> p (a d)"),
                                  start=(f == 0), stop=(f == FC - 1))
                last.then_inc(sm["y_full"], 1)

            def after(s):
                stages = dict(front=front, rows=rows, outs=outs, back=back)
                for stage, *which in PE_TAIL.get(s, ()):
                    stages[stage](*which)

            steps(pe, step, -2, NU + 4, 5, 12, after)
            rows(1)
            rows(2)
            outs(0)
            rows(3)
            outs(1)
            front(1, 1)
            outs(2)
            front(1, 2)
            outs(3)
            front(1, 4)
            rows(4)
            rows(5)
            rows(6)
            outs(4)
            outs(5)
            rows(7)
            back(0, 5)
            outs(6)
            back(0, 6)
            outs(7)
            for z in range(E + 2):
                gate_up(z, z // E, z % 2)
                if z == 0:
                    back(0, 8)
                    back(0, 9)
                else:
                    down(z - 1, (z - 1) % E, (z - 1) % 2)
                for k in PE_AFTER.get(z, ()):
                    back(1, k)
            with pe.Fori(0, (E - 2) // 2) as i:
                for j in range(2):
                    gate_up(i * 2 + (E + 2 + j), 1, j)
                    down(i * 2 + (E + 1 + j), i * 2 + (1 + j), (1 + j) % 2)
            down(2 * E - 1, E - 1, 1)


def kernel(**inputs):
    import concourse.bacc as bacc
    from concourse.bass_utils import run_bass_kernel_spmd as run

    a = {n: np.asarray(v) for n, v in inputs.items()}
    att = lambda n: np.ascontiguousarray(a["L0_attn_" + n].T)
    const_f, const_b = constants()
    by_unit = lambda t: np.ascontiguousarray(t.reshape(E, FC, 128).transpose(2, 0, 1).reshape(128, E * FC))
    arrays = {
        "x": a["x"], "ctx": a["ctx_1024"],
        "ctx_t": np.ascontiguousarray(a["ctx_1024"].transpose(2, 0, 1).reshape(D, NT)),
        "wq_t": np.ascontiguousarray(att("Wq")[:, head_rows()]), "wk_t": np.ascontiguousarray(att("Wk")[:, head_rows()]),
        "wv_t": att("Wv"), "wo_t": att("Wo"),
        "log_c": a["L0_attn_log_c"].reshape(1, 1), "log_beta": a["L0_attn_log_beta"].reshape(1, 1),
        "ig_k": a["L0_xattn_igate_kernel"], "ig_b": a["L0_xattn_igate_bias"].reshape(XH, 1),
        "fg_k": a["L0_xattn_fgate_kernel"], "fg_b": a["L0_xattn_fgate_bias"].reshape(XH, 1),
        "norm_scale": a["L0_xattn_outnorm_scale"].reshape(1, D),
        "router_t": np.ascontiguousarray(a["L0_ffn_router_w"].T),
        "gate_w": a["L0_ffn_gate_w"], "gate_b": by_unit(a["L0_ffn_gate_b"]),
        "up_w": a["L0_ffn_up_w"], "up_b": by_unit(a["L0_ffn_up_b"]),
        "down_w": a["L0_ffn_down_w"], "down_b": a["L0_ffn_down_b"],
        "const_f": const_f, "const_b": const_b, "stack_init": stack_rows(),
    }
    nc = bacc.Bacc("TRN2", target_bir_lowering=False, num_devices=1)
    args = [nc.dram_tensor(n, v.shape, mybir.dt.from_np(v.dtype), kind="ExternalInput").ap() for n, v in arrays.items()]
    out = nc.dram_tensor("out", (B, S, D), mybir.dt.float32, kind="ExternalOutput").ap()
    decoder_layer(nc, *args, out)
    r = run(nc, [arrays], core_ids=[0])
    return r.results[0]["out"]
```
